# Optimizing a Trainium2 kernel written in Bass

```python
import numpy as np
import jax
import jax.numpy as jnp

def _softmax(x, axis=-1):
    return jax.nn.softmax(x, axis=axis)

def _gelu(x):
    return jax.nn.gelu(x, approximate=True)

def _silu(x):
    return jax.nn.silu(x)

def _sigmoid(x):
    return jax.nn.sigmoid(x)

def _layernorm(x, axis=-1, eps=1e-05):
    m = jnp.mean(x, axis=axis, keepdims=True)
    v = jnp.var(x, axis=axis, keepdims=True)
    return (x - m) / jnp.sqrt(v + eps)

def _scatter_add(tgt, idx, src, axis=0):
    return tgt.at[idx].add(src)

def _segment_sum(src, seg, n):
    return jax.ops.segment_sum(src, seg, n)
kernel_name = 'mk_seq_postln_d2_jaxref_r8_db6b6c'

def setup_inputs(seed: int=0):
    np.random.seed(seed)
    _w = jnp.asarray

    def _L0_attn_setup():
        import jax, jax.numpy as jnp
        import numpy as np
        B, T, H = (8, 256, 256)
        LN_EPS = 1e-05

        def _timemix(x, ln_scale, ln_bias, mix_k, mix_v, mix_r, time_first, time_decay, Wk, Wv, Wr, Wo):
            mean = jnp.mean(x, axis=-1, keepdims=True)
            var = jnp.mean((x - mean) ** 2, axis=-1, keepdims=True)
            xn = (x - mean) * jax.lax.rsqrt(var + LN_EPS) * ln_scale + ln_bias
            prev = jnp.concatenate([jnp.zeros_like(xn[:, :1]), xn[:, :-1]], axis=1)
            kx = xn * mix_k + prev * (1.0 - mix_k)
            vx = xn * mix_v + prev * (1.0 - mix_v)
            rx = xn * mix_r + prev * (1.0 - mix_r)
            r = jax.nn.sigmoid(jnp.einsum('bth,hd->btd', rx, Wr))
            k = jnp.einsum('bth,hd->btd', kx, Wk)
            v = jnp.einsum('bth,hd->btd', vx, Wv)
            w = -jnp.exp(time_decay)
            kT = jnp.moveaxis(k, 1, 0)
            vT = jnp.moveaxis(v, 1, 0)

            def step(carry, kv):
                a, b, p = carry
                kt, vt = kv
                uk = kt + time_first
                q = jnp.maximum(uk, p)
                e1 = jnp.exp(p - q)
                e2 = jnp.exp(uk - q)
                num = e1 * a + e2 * vt
                den = e1 * b + e2
                den_safe = jnp.where(den == 0.0, 1.0, den)
                wkv = jnp.where(den == 0.0, 0.0, num / den_safe)
                cw = w + p
                q2 = jnp.maximum(cw, kt)
                ce1 = jnp.exp(cw - q2)
                ce2 = jnp.exp(kt - q2)
                return ((ce1 * a + ce2 * vt, ce1 * b + ce2, q2), wkv)
            bz = x.shape[0]
            init = (jnp.zeros((bz, H), jnp.float32), jnp.zeros((bz, H), jnp.float32), jnp.full((bz, H), 1.0 - 1e+30, jnp.float32))
            _, wkvT = jax.lax.scan(step, init, (kT, vT))
            wkv = jnp.moveaxis(wkvT, 0, 1)
            out = x + jnp.einsum('bth,hd->btd', r * wkv, Wo)
            return out
        key = jax.random.key(seed)
        ks = jax.random.split(key, 12)
        x = jax.random.normal(ks[0], (B, T, H), dtype=jnp.float32)
        ln_scale = jnp.ones((H,), jnp.float32) + 0.1 * jax.random.normal(ks[1], (H,), jnp.float32)
        ln_bias = 0.1 * jax.random.normal(ks[2], (H,), jnp.float32)
        mix_k = jax.random.uniform(ks[3], (H,), jnp.float32)
        mix_v = jax.random.uniform(ks[4], (H,), jnp.float32)
        mix_r = jax.random.uniform(ks[5], (H,), jnp.float32)
        time_first = 0.3 * jax.random.normal(ks[6], (H,), jnp.float32)
        time_decay = 0.5 * jax.random.normal(ks[7], (H,), jnp.float32)
        std = 0.02
        Wk = std * jax.random.normal(ks[8], (H, H), jnp.float32)
        Wv = std * jax.random.normal(ks[9], (H, H), jnp.float32)
        Wr = std * jax.random.normal(ks[10], (H, H), jnp.float32)
        Wo = std * jax.random.normal(ks[11], (H, H), jnp.float32)
        return {'x': x, 'ln_scale': ln_scale, 'ln_bias': ln_bias, 'mix_k': mix_k, 'mix_v': mix_v, 'mix_r': mix_r, 'time_first': time_first, 'time_decay': time_decay, 'Wk': Wk, 'Wv': Wv, 'Wr': Wr, 'Wo': Wo}
    _L0_attn_in = _L0_attn_setup()

    def _L0_ffn_setup():
        import jax, jax.numpy as jnp
        import numpy as np
        B, S, H = (2, 256, 256)
        E, K = (16, 4)
        I_MOE, I_SH = (176, 704)
        key = jax.random.key(seed)
        ks = jax.random.split(key, 9)

        def w(k, shape, fan_in):
            return jax.random.normal(k, shape, jnp.float32) * fan_in ** (-0.5)
        return {'hidden_states': jax.random.normal(ks[0], (B, S, H), jnp.float32), 'router_w': w(ks[1], (E, H), H), 'w_gate': w(ks[2], (E, H, I_MOE), H), 'w_up': w(ks[3], (E, H, I_MOE), H), 'w_down': w(ks[4], (E, I_MOE, H), I_MOE), 'sh_gate': w(ks[5], (H, I_SH), H), 'sh_up': w(ks[6], (H, I_SH), H), 'sh_down': w(ks[7], (I_SH, H), I_SH), 'sh_gate_w': w(ks[8], (H, 1), H)}
    _L0_ffn_in = _L0_ffn_setup()

    def _L1_attn_setup():
        import math
        import jax, jax.numpy as jnp
        import numpy as np
        H, G = (16, 4)

        def alibi_bias(S, n_heads, dtype):
            n = 2 ** int(math.floor(math.log2(n_heads)))
            m0 = 2.0 ** (-8.0 / n)
            slopes = m0 ** np.arange(1, n + 1)
            if n < n_heads:
                m1 = 2.0 ** (-4.0 / n)
                slopes = np.concatenate([slopes, m1 ** np.arange(1, 1 + 2 * (n_heads - n), 2)])
            i = jnp.arange(S)[:, None]
            j = jnp.arange(S)[None, :]
            dist = jnp.sqrt(jnp.maximum(i - j, 0).astype(dtype))
            bias = -jnp.asarray(slopes, dtype)[:, None, None] * dist[None]
            return jnp.where((j <= i)[None], bias, jnp.asarray(-jnp.inf, dtype))
        key = jax.random.key(seed)
        ks = jax.random.split(key, 5)
        B, S, Hd = (2, 256, 256)
        D = Hd // H
        return {'x': jax.random.normal(ks[0], (B, S, Hd), jnp.float32), 'Wq': jax.random.normal(ks[1], (Hd, Hd), jnp.float32) * 0.02, 'Wk': jax.random.normal(ks[2], (G * D, Hd), jnp.float32) * 0.02, 'Wv': jax.random.normal(ks[3], (G * D, Hd), jnp.float32) * 0.02, 'Wo': jax.random.normal(ks[4], (Hd, Hd), jnp.float32) * 0.02}
    _L1_attn_in = _L1_attn_setup()

    def _L1_ffn_setup():
        import jax, jax.numpy as jnp
        import numpy as np
        B, S, D, H = (4, 256, 256, 1024)

        def fwht(x):
            orig_shape = x.shape
            n = orig_shape[-1]
            x = x.reshape(-1, n)
            h = 1
            while h < n:
                xb = x.reshape(-1, n // (2 * h), 2, h)
                a = xb[:, :, 0, :]
                b = xb[:, :, 1, :]
                x = jnp.stack([a + b, a - b], axis=2).reshape(-1, n)
                h *= 2
            scale = jnp.asarray(1.0 / np.sqrt(n), dtype=x.dtype)
            return (x * scale).reshape(orig_shape)
        key = jax.random.key(seed)
        kx, k1, k2, k3 = jax.random.split(key, 4)
        x = jax.random.normal(kx, (B, S, D), dtype=jnp.float32)
        W1 = jax.random.normal(k1, (H, D), dtype=jnp.float32) * (1.0 / np.sqrt(D))
        W2 = jax.random.normal(k2, (D, H), dtype=jnp.float32) * (1.0 / np.sqrt(H))
        W3 = jax.random.normal(k3, (H, D), dtype=jnp.float32) * (1.0 / np.sqrt(D))
        return {'x': x, 'W1': W1, 'W2': W2, 'W3': W3}
    _L1_ffn_in = _L1_ffn_setup()
    _d = {'L0_attn_x': _L0_attn_in['x'], 'L0_attn_ln_scale': _L0_attn_in['ln_scale'], 'L0_attn_ln_bias': _L0_attn_in['ln_bias'], 'L0_attn_mix_k': _L0_attn_in['mix_k'], 'L0_attn_mix_v': _L0_attn_in['mix_v'], 'L0_attn_mix_r': _L0_attn_in['mix_r'], 'L0_attn_time_first': _L0_attn_in['time_first'], 'L0_attn_time_decay': _L0_attn_in['time_decay'], 'L0_attn_Wk': _L0_attn_in['Wk'], 'L0_attn_Wv': _L0_attn_in['Wv'], 'L0_attn_Wr': _L0_attn_in['Wr'], 'L0_attn_Wo': _L0_attn_in['Wo'], 'L0_ffn_router_w': _L0_ffn_in['router_w'], 'L0_ffn_w_gate': _L0_ffn_in['w_gate'], 'L0_ffn_w_up': _L0_ffn_in['w_up'], 'L0_ffn_w_down': _L0_ffn_in['w_down'], 'L0_ffn_sh_gate': _L0_ffn_in['sh_gate'], 'L0_ffn_sh_up': _L0_ffn_in['sh_up'], 'L0_ffn_sh_down': _L0_ffn_in['sh_down'], 'L0_ffn_sh_gate_w': _L0_ffn_in['sh_gate_w'], 'L1_attn_Wq': _L1_attn_in['Wq'], 'L1_attn_Wk': _L1_attn_in['Wk'], 'L1_attn_Wv': _L1_attn_in['Wv'], 'L1_attn_Wo': _L1_attn_in['Wo'], 'L1_ffn_W1': _L1_ffn_in['W1'], 'L1_ffn_W2': _L1_ffn_in['W2'], 'L1_ffn_W3': _L1_ffn_in['W3']}
    _x0 = _d['L0_attn_x']
    _d['L0_attn_x'] = jax.random.normal(jax.random.fold_in(jax.random.key(seed), 1), (16, 256, 256), dtype=_x0.dtype)
    del _x0
    return _d

def reference(L0_attn_x, L0_attn_ln_scale, L0_attn_ln_bias, L0_attn_mix_k, L0_attn_mix_v, L0_attn_mix_r, L0_attn_time_first, L0_attn_time_decay, L0_attn_Wk, L0_attn_Wv, L0_attn_Wr, L0_attn_Wo, L0_ffn_router_w, L0_ffn_w_gate, L0_ffn_w_up, L0_ffn_w_down, L0_ffn_sh_gate, L0_ffn_sh_up, L0_ffn_sh_down, L0_ffn_sh_gate_w, L1_attn_Wq, L1_attn_Wk, L1_attn_Wv, L1_attn_Wo, L1_ffn_W1, L1_ffn_W2, L1_ffn_W3):

    def _L0_attn_ref(x, ln_scale, ln_bias, mix_k, mix_v, mix_r, time_first, time_decay, Wk, Wv, Wr, Wo):
        import jax, jax.numpy as jnp
        import numpy as np
        B, T, H = (8, 256, 256)
        LN_EPS = 1e-05

        def _timemix(x, ln_scale, ln_bias, mix_k, mix_v, mix_r, time_first, time_decay, Wk, Wv, Wr, Wo):
            mean = jnp.mean(x, axis=-1, keepdims=True)
            var = jnp.mean((x - mean) ** 2, axis=-1, keepdims=True)
            xn = (x - mean) * jax.lax.rsqrt(var + LN_EPS) * ln_scale + ln_bias
            prev = jnp.concatenate([jnp.zeros_like(xn[:, :1]), xn[:, :-1]], axis=1)
            kx = xn * mix_k + prev * (1.0 - mix_k)
            vx = xn * mix_v + prev * (1.0 - mix_v)
            rx = xn * mix_r + prev * (1.0 - mix_r)
            r = jax.nn.sigmoid(jnp.einsum('bth,hd->btd', rx, Wr))
            k = jnp.einsum('bth,hd->btd', kx, Wk)
            v = jnp.einsum('bth,hd->btd', vx, Wv)
            w = -jnp.exp(time_decay)
            kT = jnp.moveaxis(k, 1, 0)
            vT = jnp.moveaxis(v, 1, 0)

            def step(carry, kv):
                a, b, p = carry
                kt, vt = kv
                uk = kt + time_first
                q = jnp.maximum(uk, p)
                e1 = jnp.exp(p - q)
                e2 = jnp.exp(uk - q)
                num = e1 * a + e2 * vt
                den = e1 * b + e2
                den_safe = jnp.where(den == 0.0, 1.0, den)
                wkv = jnp.where(den == 0.0, 0.0, num / den_safe)
                cw = w + p
                q2 = jnp.maximum(cw, kt)
                ce1 = jnp.exp(cw - q2)
                ce2 = jnp.exp(kt - q2)
                return ((ce1 * a + ce2 * vt, ce1 * b + ce2, q2), wkv)
            bz = x.shape[0]
            init = (jnp.zeros((bz, H), jnp.float32), jnp.zeros((bz, H), jnp.float32), jnp.full((bz, H), 1.0 - 1e+30, jnp.float32))
            _, wkvT = jax.lax.scan(step, init, (kT, vT))
            wkv = jnp.moveaxis(wkvT, 0, 1)
            out = x + jnp.einsum('bth,hd->btd', r * wkv, Wo)
            return out
        return _timemix(x, ln_scale, ln_bias, mix_k, mix_v, mix_r, time_first, time_decay, Wk, Wv, Wr, Wo)

    def _L0_ffn_ref(hidden_states, router_w, w_gate, w_up, w_down, sh_gate, sh_up, sh_down, sh_gate_w):
        import jax, jax.numpy as jnp
        import numpy as np
        B, S, H = (2, 256, 256)
        E, K = (16, 4)
        I_MOE, I_SH = (176, 704)
        orig = hidden_states.shape
        h = hidden_states.reshape(-1, orig[-1])
        N = h.shape[0]
        logits = h @ router_w.T
        probs = jax.nn.softmax(logits.astype(jnp.float32), axis=-1)
        top_vals, top_idx = jax.lax.top_k(probs, K)
        top_vals = top_vals / jnp.maximum(top_vals.sum(-1, keepdims=True), 1e-09)
        top_vals = top_vals.astype(h.dtype)
        comb = jnp.zeros((N, E), h.dtype).at[jnp.arange(N)[:, None], top_idx].add(top_vals)
        g = jnp.einsum('nh,ehi->eni', h, w_gate)
        u = jnp.einsum('nh,ehi->eni', h, w_up)
        y = jnp.einsum('eni,eih->enh', jax.nn.silu(g) * u, w_down)
        routed = jnp.einsum('enh,ne->nh', y, comb)
        shared = jax.nn.silu(h @ sh_gate) * (h @ sh_up) @ sh_down
        sg = jax.nn.sigmoid(h @ sh_gate_w)
        return (routed + sg * shared).reshape(orig)

    def _L1_attn_ref(x, Wq, Wk, Wv, Wo):
        import math
        import jax, jax.numpy as jnp
        import numpy as np
        H, G = (16, 4)

        def alibi_bias(S, n_heads, dtype):
            n = 2 ** int(math.floor(math.log2(n_heads)))
            m0 = 2.0 ** (-8.0 / n)
            slopes = m0 ** np.arange(1, n + 1)
            if n < n_heads:
                m1 = 2.0 ** (-4.0 / n)
                slopes = np.concatenate([slopes, m1 ** np.arange(1, 1 + 2 * (n_heads - n), 2)])
            i = jnp.arange(S)[:, None]
            j = jnp.arange(S)[None, :]
            dist = jnp.sqrt(jnp.maximum(i - j, 0).astype(dtype))
            bias = -jnp.asarray(slopes, dtype)[:, None, None] * dist[None]
            return jnp.where((j <= i)[None], bias, jnp.asarray(-jnp.inf, dtype))
        B, S, Hd = x.shape
        D = Hd // H
        rep = H // G
        q = (x @ Wq.T).reshape(B, S, G, rep, D)
        k = (x @ Wk.T).reshape(B, S, G, D)
        v = (x @ Wv.T).reshape(B, S, G, D)
        scale = 1.0 / math.sqrt(D)
        bias = alibi_bias(S, H, x.dtype).reshape(G, rep, S, S)
        scores = jnp.einsum('bqgrd,bkgd->bgrqk', q, k) * scale + bias
        attn = jax.nn.softmax(scores, axis=-1)
        o = jnp.einsum('bgrqk,bkgd->bqgrd', attn, v).reshape(B, S, Hd)
        return o @ Wo.T

    def _L1_ffn_ref(x, W1, W2, W3):
        import jax, jax.numpy as jnp
        import numpy as np
        B, S, D, H = (4, 256, 256, 1024)

        def fwht(x):
            orig_shape = x.shape
            n = orig_shape[-1]
            x = x.reshape(-1, n)
            h = 1
            while h < n:
                xb = x.reshape(-1, n // (2 * h), 2, h)
                a = xb[:, :, 0, :]
                b = xb[:, :, 1, :]
                x = jnp.stack([a + b, a - b], axis=2).reshape(-1, n)
                h *= 2
            scale = jnp.asarray(1.0 / np.sqrt(n), dtype=x.dtype)
            return (x * scale).reshape(orig_shape)
        up_gate = jnp.einsum('bsd,hd->bsh', x, W1)
        up_lin = jnp.einsum('bsd,hd->bsh', x, W3)
        hidden = jax.nn.silu(up_gate) * up_lin
        hidden = fwht(hidden)
        out = jnp.einsum('bsh,dh->bsd', hidden, W2)
        return out
    x = L0_attn_x
    x = _layernorm(x + _L0_attn_ref(x, L0_attn_ln_scale, L0_attn_ln_bias, L0_attn_mix_k, L0_attn_mix_v, L0_attn_mix_r, L0_attn_time_first, L0_attn_time_decay, L0_attn_Wk, L0_attn_Wv, L0_attn_Wr, L0_attn_Wo), axis=-1)
    x = _layernorm(x + _L0_ffn_ref(x, L0_ffn_router_w, L0_ffn_w_gate, L0_ffn_w_up, L0_ffn_w_down, L0_ffn_sh_gate, L0_ffn_sh_up, L0_ffn_sh_down, L0_ffn_sh_gate_w), axis=-1)
    x = _layernorm(x + _L1_attn_ref(x, L1_attn_Wq, L1_attn_Wk, L1_attn_Wv, L1_attn_Wo), axis=-1)
    x = _layernorm(x + _L1_ffn_ref(x, L1_ffn_W1, L1_ffn_W2, L1_ffn_W3), axis=-1)
    return x

_drawn_inputs = setup_inputs


def setup_inputs(seed=0):
    import zlib

    import numpy as np

    out = dict(_drawn_inputs(seed))
    spreads = {}
    factors = {'L0_attn_ln_scale': 8.0,
     'L0_attn_ln_bias': 6.189,
     'L0_attn_mix_k': 8.0,
     'L0_attn_mix_v': 5.106,
     'L0_attn_mix_r': 8.0,
     'L0_attn_time_first': 7.373,
     'L0_attn_time_decay': 5.051,
     'L0_attn_Wk': 7.395,
     'L0_attn_Wr': 7.063,
     'L1_attn_Wq': 8.0,
     'L1_attn_Wk': 8.0}
    for name, (base, spread) in spreads.items():
        noise = np.random.default_rng([zlib.crc32(name.encode()), seed]).standard_normal(out[name].shape)
        drawn = base * np.exp(spread * noise) if base else spread * noise
        out[name] = jnp.asarray(drawn.astype(out[name].dtype))
    for name, factor in factors.items():
        out[name] = (out[name] * factor).astype(out[name].dtype)
    return out
```

```python
from contextlib import ExitStack

import concourse.bass as bass
from concourse import mybir
import numpy as np

ALU = mybir.AluOpType
ACT = mybir.ActivationFunctionType
F32 = mybir.dt.float32
F16 = mybir.dt.float16
BF16 = mybir.dt.bfloat16
AX_X = mybir.AxisListType.X

P = 128
SEQS, T, H = 16, 256, 256
TOK = SEQS * T
TILES = TOK // P
KT = H // P
LN_EPS = 1e-5
NEG = -1.0e30

GROUP = 4
GTOK = GROUP * P
GROUPS = TILES // GROUP
GSEQ = GTOK // T

E, TOPK = 16, 4
I_MOE, I_SH = 176, 704
SH = I_SH // I_MOE
SLICES = E + SH
MOE_BLOCKS = -(-SLICES * I_MOE // 256) * 2
I_FF = 1024
FF_BLOCKS = I_FF // P

HEADS, KV, D = 16, 4, 16
REP = HEADS // KV
SLOT = 32
SCALE = D ** -0.5

C_TM = 4 * KT * H
C_RT = KT * (E + 1)
C_L0 = C_TM + C_RT
C_GU = KT * SLICES * 2 * I_MOE
C_DN = MOE_BLOCKS * H
C_MOE = C_GU + C_DN
C_Q, C_K, C_V, C_O = KT * REP * P, KT * P, KT * KV * D, KT * H
C_FF = KT * 2 * I_FF
C_L1 = C_Q + C_K + C_V + C_O + C_FF


class Steps:

    def __init__(self, sem, names):
        self.sem, self.names = sem, names

    def start(self, eng):
        eng.sem_inc(self.sem, len(self.names))

    def after(self, i, name):
        return (i + 1) * len(self.names) + self.names.index(name) + 1


def hold(eng, sem, value, passed):
    eng.wait_ge(sem, value)
    eng.sem_inc(passed, 1)


def split_matmul(nc, out, stationary, moving, first=True, last=True):
    nc.tensor.matmul(out, stationary[0], moving[0], start=first, stop=False, skip_group_check=True)
    nc.tensor.matmul(out, stationary[1], moving[0], start=False, stop=False, skip_group_check=True)
    return nc.tensor.matmul(out, stationary[0], moving[1], start=False, stop=last, skip_group_check=True)


def load_stage(nc, k):
    with ExitStack() as ctx:
        raw = ctx.enter_context(nc.sbuf_tensor("l0_raw", [P, C_L0], F32))
        vecs = k.vecs
        loaded = ctx.enter_context(nc.semaphore("l0_loaded"))
        x_loaded = ctx.enter_context(nc.semaphore("x_loaded"))
        hi_done = ctx.enter_context(nc.semaphore("l0_hi_done"))
        decay = ctx.enter_context(nc.semaphore("decay_done"))
        vec = ctx.enter_context(nc.semaphore("l0_vec_done"))
        zero = ctx.enter_context(nc.semaphore("l0_zero_done"))
        block = ctx.enter_context(nc.Block())

        @block.sync
        def _(sp):
            sp.dma_start(raw[:, :], k.d_l0).then_inc(loaded, 16)
            sp.dma_start(vecs[:, :], k.d_vecs).then_inc(loaded, 16)
            sp.dma_start(k.ident[:, :], k.d_ident).then_inc(loaded, 16)
            for c in range(4):
                n = TILES // 4
                sp.dma_start(k.x[:, c * n * H:(c + 1) * n * H].rearrange("p (t h) -> p t h", h=H),
                             k.d_x[c * n:(c + 1) * n].rearrange("t p h -> p t h")).then_inc(x_loaded, 16)
            sp.wait_ge(x_loaded, 64)

        @block.scalar
        def _(act):
            act.wait_ge(loaded, 48)
            nc.scalar.activation(k.l0_hi[:, :], raw[:, :], ACT.Identity).then_inc(hi_done, 1)
            nc.scalar.activation(k.decay[:, :], vecs[:, 12:14], ACT.Exp).then_inc(decay, 1)

        @block.gpsimd
        def _(pool):
            nc.gpsimd.memset(k.x[:, TILES * H:], 0.0)
            nc.gpsimd.memset(k.eps[:, :], LN_EPS)
            nc.gpsimd.memset(k.wrow[:, :, :], 0.0).then_inc(zero, 1)

        @block.vector
        def _(dve):
            dve.wait_ge(hi_done, 1)
            nc.vector.tensor_tensor(k.l0_lo[:, :], raw[:, :], k.l0_hi[:, :], ALU.subtract).then_inc(vec, 1)
            dve.wait_ge(decay, 1)
            nc.vector.tensor_scalar_mul(k.decay[:, :], k.decay[:, :], -1.0).then_inc(vec, 1)
            dve.wait_ge(vec, 2)
            dve.wait_ge(zero, 1)
            for m in range(KT):
                nc.vector.tensor_scalar_add(k.wrow[:, m, :], k.wrow[:, m, :], k.decay[:, m:m + 1])\
                    .then_inc(vec, 1)


def time_mix_stage(nc, k):
    VEC = ["stats", "mv", "rstd", "xhat", "diff", "mix_k", "mix_v", "mix_r", "p", "q", "t1", "t2", "t3",
           "t4", "c2v", "b", "a", "e1b", "den", "rec", "e1a", "e2v", "num", "gated", "y",
           "res", "stats2", "mv2", "rstd2", "out"]
    SCA = ["std", "xn", "hi_k", "hi_v", "hi_r", "k", "uk", "gate", "e1", "e2", "c1", "c2", "hi_y", "std2"]
    PEN = ["xT", "k", "v", "r", "wo"]
    POL = ["lo_k", "lo_v", "lo_r", "w_hi", "w_lo", "lo_y"]
    WCOLS = C_MOE // GROUPS
    with ExitStack() as ctx:
        def sb(name, shape, dt=F32):
            return ctx.enter_context(nc.sbuf_tensor("tm_" + name, shape, dt))

        wraw = sb("wraw", [P, WCOLS])
        st = sb("st", [P, GROUP, 6])
        mv = sb("mv", [P, GROUP, 2])
        std = sb("std", [P, GROUP])
        rstd = sb("rstd", [P, GROUP])
        xh = sb("xh", [P, GROUP, H])
        xn = sb("xn", [P, KT, GSEQ, T + 1])
        diff = sb("diff", [P, KT, GSEQ, T])
        mix = [sb(f"mix{j}", [P, KT, GTOK]) for j in range(3)]
        hi = [sb(f"hi{j}", [P, KT, GTOK], F16) for j in range(3)]
        lo = [sb(f"lo{j}", [P, KT, GTOK], F16) for j in range(3)]
        kS, uk, gate = diff, mix[0], mix[1]
        pmax = sb("pmax", [P, KT, GSEQ, T + 1])
        q = mix[2]
        e1, e2, c1, c2 = (sb(n, [P, KT, GSEQ, T]) for n in ("e1", "e2", "c1", "c2"))
        c2v = kS
        asum = sb("asum", [P, KT, GSEQ, T + 1])
        bsum = sb("bsum", [P, KT, GSEQ, T + 1])
        vec = Steps(ctx.enter_context(nc.semaphore("tm_vector_steps")), VEC)
        sca = Steps(ctx.enter_context(nc.semaphore("tm_scalar_steps")), SCA)
        pen = Steps(ctx.enter_context(nc.semaphore("tm_tensor_steps")), PEN)
        pol = Steps(ctx.enter_context(nc.semaphore("tm_pool_steps")), POL)
        w_loaded = ctx.enter_context(nc.semaphore("tm_w_loaded"))
        edges = ctx.enter_context(nc.semaphore("tm_edges"))
        passed = ctx.enter_context(nc.semaphore("tm_aggregate_waits"))
        ps = k.ps

        def flat(t):
            return t[:, :, :, :].rearrange("p m s t -> p (m s) t")

        def by_tok(t):
            return t[:, :, :].rearrange("p m (s t) -> p (m s) t", t=T)

        before, now = flat(xn)[:, :, 0:T], flat(xn)[:, :, 1:T + 1]
        p_old, p_new = flat(pmax)[:, :, 0:T], flat(pmax)[:, :, 1:T + 1]
        a_old, b_old = flat(asum)[:, :, 0:T], flat(bsum)[:, :, 0:T]
        k_ps = ps[:, 2:4, :].rearrange("p m (s t) -> p (m s) t", t=T)
        v_ps = ps[:, 4:6, :].rearrange("p m (s t) -> p (m s) t", t=T)
        r_ps = ps[:, 6:8, :].rearrange("p m (s t) -> p (m s) t", t=T)
        uk3, gate3, q3 = by_tok(uk), by_tok(gate), by_tok(q)
        mix_of = [k.vecs[:, 4:6], k.vecs[:, 6:8], k.vecs[:, 8:10]]
        first = k.vecs[:, 10:12]
        block = ctx.enter_context(nc.Block())

        def xs(i, t):
            return k.x[:, bass.ds(i * (GROUP * H) + t * H, H)]

        @block.sync
        def _(sp):
            with sp.Fori(0, GROUPS) as i:
                sp.wait_ge(pol.sem, pol.after(i - 1, "w_lo"))
                sp.dma_start(wraw[:, :], k.d_moe[:, bass.ds(i * WCOLS, WCOLS)]).then_inc(w_loaded, 16)

        @block.gpsimd
        def _(pool):
            pol.start(pool)
            nc.gpsimd.memset(flat(xn)[:, :, 0:1], 0.0)
            nc.gpsimd.memset(flat(pmax)[:, :, 0:1], NEG)
            nc.gpsimd.memset(flat(asum)[:, :, 0:1], 0.0)
            nc.gpsimd.memset(flat(bsum)[:, :, 0:1], 0.0).then_inc(edges, 1)
            with pool.Fori(0, GROUPS) as i:
                for j, name in enumerate("kvr"):
                    pool.wait_ge(sca.sem, sca.after(i, "hi_" + name))
                    nc.gpsimd.tensor_tensor(lo[j][:, :, :], mix[j][:, :, :], hi[j][:, :, :], ALU.subtract)\
                        .then_inc(pol.sem, 1)
                pool.wait_ge(w_loaded, (i + 1) * 16)
                whi = k.moe_hi[:, bass.ds(i * WCOLS, WCOLS)]
                nc.gpsimd.tensor_copy(whi, wraw[:, :]).then_inc(pol.sem, 1)
                pool.wait_ge(pol.sem, pol.after(i, "w_hi"))
                nc.gpsimd.tensor_tensor(k.moe_lo[:, bass.ds(i * WCOLS, WCOLS)], wraw[:, :], whi,
                                        ALU.subtract).then_inc(pol.sem, 1)
                pool.wait_ge(sca.sem, sca.after(i, "hi_y"))
                nc.gpsimd.tensor_tensor(lo[0][:, :, :], uk[:, :, :], hi[0][:, :, :], ALU.subtract)\
                    .then_inc(pol.sem, 1)

        @block.scalar
        def _(act):
            sca.start(act)
            with act.Fori(0, GROUPS) as i:
                act.wait_ge(vec.sem, vec.after(i, "mv"))
                nc.scalar.activation(std[:, :], mv[:, :, 1], ACT.Sqrt, bias=k.eps[:, 0:1]).then_inc(sca.sem, 1)
                act.wait_ge(pen.sem, pen.after(i, "xT"))
                for m in range(KT):
                    last = nc.scalar.activation(xn[:, m, :, 1:T + 1],
                                                ps[:, m, :].rearrange("p (s t) -> p s t", t=T), ACT.Identity,
                                                scale=k.vecs[:, m:m + 1], bias=k.vecs[:, 2 + m:3 + m])
                last.then_inc(sca.sem, 1)
                for j, name in enumerate("kvr"):
                    act.wait_ge(vec.sem, vec.after(i, "mix_" + name))
                    nc.scalar.activation(hi[j][:, :, :], mix[j][:, :, :], ACT.Copy).then_inc(sca.sem, 1)
                act.wait_ge(pen.sem, pen.after(i, "k"))
                act.wait_ge(vec.sem, vec.after(i, "mix_r"))
                nc.scalar.activation(flat(kS), k_ps, ACT.Copy).then_inc(sca.sem, 1)
                act.wait_ge(pol.sem, pol.after(i, "lo_k"))
                for m in range(KT):
                    last = nc.scalar.activation(uk[:, m, :], ps[:, 2 + m, :], ACT.Identity,
                                                bias=first[:, m:m + 1])
                last.then_inc(sca.sem, 1)
                act.wait_ge(pen.sem, pen.after(i, "r"))
                act.wait_ge(pol.sem, pol.after(i, "lo_v"))
                nc.scalar.activation(gate3, r_ps, ACT.Tanh, scale=0.5).then_inc(sca.sem, 1)
                for name, buf in (("t1", e1), ("t2", e2), ("t3", c1), ("t4", c2)):
                    act.wait_ge(vec.sem, vec.after(i, name))
                    nc.scalar.activation(flat(buf), flat(buf), ACT.Exp).then_inc(sca.sem, 1)
                act.wait_ge(vec.sem, vec.after(i, "y"))
                nc.scalar.activation(hi[0][:, :, :], uk[:, :, :], ACT.Copy).then_inc(sca.sem, 1)
                act.wait_ge(vec.sem, vec.after(i, "mv2"))
                nc.scalar.activation(std[:, :], mv[:, :, 1], ACT.Sqrt, bias=k.eps[:, 0:1]).then_inc(sca.sem, 1)

        @block.vector
        def _(dve):
            vec.start(dve)
            dve.wait_ge(edges, 1)

            def done(i, name):
                dve.wait_ge(vec.sem, vec.after(i, name))

            with dve.Fori(0, GROUPS) as i:
                for t in range(GROUP):
                    last = nc.vector.bn_stats(st[:, t, :], xs(i, t))
                last.then_inc(vec.sem, 1)
                hold(dve, vec.sem, vec.after(i, "stats"), passed)
                for t in range(GROUP):
                    last = nc.vector.bn_aggr(mv[:, t, :], st[:, t, :])
                last.then_inc(vec.sem, 1)
                dve.wait_ge(sca.sem, sca.after(i, "std"))
                nc.vector.reciprocal(rstd[:, :], std[:, :]).then_inc(vec.sem, 1)
                done(i, "rstd")
                for t in range(GROUP):
                    last = nc.vector.tensor_scalar(xh[:, t, :], xs(i, t), mv[:, t, 0:1], rstd[:, t:t + 1],
                                                   ALU.subtract, ALU.mult)
                last.then_inc(vec.sem, 1)
                dve.wait_ge(sca.sem, sca.after(i, "xn"))
                nc.vector.tensor_tensor(flat(diff), now, before, ALU.subtract).then_inc(vec.sem, 1)
                done(i, "diff")
                for j in range(3):
                    for m in range(KT):
                        last = nc.vector.scalar_tensor_tensor(
                            out=mix[j][:, m, :].rearrange("p (s t) -> p s t", t=T), in0=diff[:, m, :, :],
                            scalar=mix_of[j][:, m:m + 1], in1=xn[:, m, :, 0:T], op0=ALU.mult, op1=ALU.add)
                    last.then_inc(vec.sem, 1)
                dve.wait_ge(sca.sem, sca.after(i, "k"))
                for m in range(KT):
                    for s in range(GSEQ):
                        last = nc.vector.tensor_tensor_scan(pmax[:, m, s, 1:T + 1], k.wrow[:, m, :],
                                                            kS[:, m, s, :], NEG, ALU.add, ALU.max)
                last.then_inc(vec.sem, 1)
                done(i, "p")
                dve.wait_ge(sca.sem, sca.after(i, "uk"))
                dve.wait_ge(pol.sem, pol.after(i, "lo_r"))
                nc.vector.tensor_tensor(q3, uk3, p_old, ALU.max).then_inc(vec.sem, 1)
                done(i, "q")
                nc.vector.tensor_tensor(flat(e1), p_old, q3, ALU.subtract).then_inc(vec.sem, 1)
                nc.vector.tensor_tensor(flat(e2), uk3, q3, ALU.subtract).then_inc(vec.sem, 1)
                for m in range(KT):
                    last = nc.vector.scalar_tensor_tensor(
                        out=c1[:, m, :, :], in0=pmax[:, m, :, 0:T], scalar=k.decay[:, m:m + 1],
                        in1=pmax[:, m, :, 1:T + 1], op0=ALU.add, op1=ALU.subtract)
                last.then_inc(vec.sem, 1)
                nc.vector.tensor_tensor(flat(c2), flat(kS), p_new, ALU.subtract).then_inc(vec.sem, 1)
                dve.wait_ge(sca.sem, sca.after(i, "c2"))
                dve.wait_ge(pen.sem, pen.after(i, "v"))
                nc.vector.tensor_tensor(flat(c2v), flat(c2), v_ps, ALU.mult).then_inc(vec.sem, 1)
                for m in range(KT):
                    for s in range(GSEQ):
                        last = nc.vector.tensor_tensor_scan(bsum[:, m, s, 1:T + 1], c1[:, m, s, :],
                                                            c2[:, m, s, :], 0.0, ALU.mult, ALU.add)
                last.then_inc(vec.sem, 1)
                done(i, "c2v")
                for m in range(KT):
                    for s in range(GSEQ):
                        last = nc.vector.tensor_tensor_scan(asum[:, m, s, 1:T + 1], c1[:, m, s, :],
                                                            c2v[:, m, s, :], 0.0, ALU.mult, ALU.add)
                last.then_inc(vec.sem, 1)
                done(i, "a")
                nc.vector.tensor_tensor(flat(c1), flat(e1), b_old, ALU.mult).then_inc(vec.sem, 1)
                done(i, "e1b")
                nc.vector.tensor_tensor(flat(c2), flat(c1), flat(e2), ALU.add).then_inc(vec.sem, 1)
                done(i, "den")
                nc.vector.reciprocal(flat(c1), flat(c2)).then_inc(vec.sem, 1)
                nc.vector.tensor_tensor(flat(c2v), flat(e1), a_old, ALU.mult).then_inc(vec.sem, 1)
                done(i, "rec")
                nc.vector.tensor_tensor(flat(c2), flat(e2), v_ps, ALU.mult).then_inc(vec.sem, 1)
                done(i, "e2v")
                nc.vector.tensor_tensor(flat(e1), flat(c2v), flat(c2), ALU.add).then_inc(vec.sem, 1)
                done(i, "num")
                dve.wait_ge(sca.sem, sca.after(i, "gate"))
                nc.vector.scalar_tensor_tensor(out=flat(e2).rearrange("p a t -> p (a t)"),
                                               in0=gate3.rearrange("p a t -> p (a t)"), scalar=1.0,
                                               in1=flat(e1).rearrange("p a t -> p (a t)"),
                                               op0=ALU.add, op1=ALU.mult).then_inc(vec.sem, 1)
                done(i, "gated")
                nc.vector.scalar_tensor_tensor(out=uk[:, :, :].rearrange("p m t -> p (m t)"),
                                               in0=flat(e2).rearrange("p a t -> p (a t)"), scalar=0.5,
                                               in1=flat(c1).rearrange("p a t -> p (a t)"),
                                               op0=ALU.mult, op1=ALU.mult).then_inc(vec.sem, 1)
                dve.wait_ge(pen.sem, pen.after(i, "wo"))
                for h2 in range(GROUP // 2):
                    last = nc.vector.scalar_tensor_tensor(
                        out=xh[:, 2 * h2:2 * h2 + 2, :].rearrange("p t h -> p (t h)"),
                        in0=k.x[:, bass.ds(i * (GROUP * H) + h2 * 2 * H, 2 * H)], scalar=2.0,
                        in1=ps[:, h2, :], op0=ALU.mult, op1=ALU.add)
                last.then_inc(vec.sem, 1)
                done(i, "res")
                for t in range(GROUP):
                    last = nc.vector.bn_stats(st[:, t, :], xh[:, t, :])
                last.then_inc(vec.sem, 1)
                hold(dve, vec.sem, vec.after(i, "stats2"), passed)
                for t in range(GROUP):
                    last = nc.vector.bn_aggr(mv[:, t, :], st[:, t, :])
                last.then_inc(vec.sem, 1)
                dve.wait_ge(sca.sem, sca.after(i, "std2"))
                nc.vector.reciprocal(rstd[:, :], std[:, :]).then_inc(vec.sem, 1)
                done(i, "rstd2")
                for t in range(GROUP):
                    last = nc.vector.tensor_scalar(xs(i, t), xh[:, t, :], mv[:, t, 0:1], rstd[:, t:t + 1],
                                                   ALU.subtract, ALU.mult)
                last.then_inc(vec.sem, 1)

        @block.tensor
        def _(pe):
            pen.start(pe)
            wt = [[w[:, 0:C_TM].rearrange("p (j m h) -> p j m h", j=4, m=KT) for w in (k.l0_hi, k.l0_lo)]][0]
            with pe.Fori(0, GROUPS) as i:
                pe.wait_ge(vec.sem, vec.after(i, "xhat"))
                for m in range(KT):
                    for t in range(GROUP):
                        last = nc.tensor.transpose(ps[:, m, t * P:(t + 1) * P], xh[:, t, m * P:(m + 1) * P],
                                                   k.ident[:, :])
                last.then_inc(pen.sem, 1)
                for j, name in enumerate("kvr"):
                    pe.wait_ge(pol.sem, pol.after(i, "lo_" + name))
                    for o in range(KT):
                        for m in range(KT):
                            last = split_matmul(nc, ps[:, 2 + 2 * j + o, :],
                                                [w[:, j, m, o * P:(o + 1) * P] for w in wt],
                                                [hi[j][:, m, :], lo[j][:, m, :]], m == 0, m == KT - 1)
                    last.then_inc(pen.sem, 1)
                pe.wait_ge(pol.sem, pol.after(i, "lo_y"))
                for t in range(GROUP):
                    for m in range(KT):
                        last = split_matmul(nc, ps[:, t // 2, (t % 2) * H:(t % 2 + 1) * H],
                                            [y[:, m, t * P:(t + 1) * P] for y in (hi[0], lo[0])],
                                            [w[:, 3, m, :] for w in wt], m == 0, m == KT - 1)
                last.then_inc(pen.sem, 1)


def router_stage(nc, k):
    with ExitStack() as ctx:
        def sb(name, shape, dt=F32):
            return ctx.enter_context(nc.sbuf_tensor("rt_" + name, shape, dt))

        def sem(name):
            return ctx.enter_context(nc.semaphore("rt_" + name))

        xc = sb("xc", [P, GROUP, H])
        xhi = sb("xhi", [P, KT, GTOK], F16)
        xlo = sb("xlo", [P, KT, GTOK], F16)
        logit = sb("logit", [P, TILES, E + 1])
        prob = sb("prob", [P, TILES, E])
        top = sb("top", [P, TILES])
        tot = sb("tot", [P, TILES])
        rec = sb("rec", [P, TILES])
        gate = sb("gate", [P, TILES])
        rank = sb("rank", [P, TILES, E])
        TG = 4
        above = sb("above", [P, TG, E, E])
        tied = sb("tied", [P, TG, E, E])
        copied, transposed, hi_done, lo_done, scored, kept = (
            sem(n) for n in ("copied", "transposed", "hi_done", "lo_done", "scored", "kept"))
        chain, exps = sem("vector_chain"), sem("exps")
        ps = k.ps
        W = E + 1
        wt = [w[:, C_TM:C_L0].rearrange("p (m e) -> p m e", m=KT) for w in (k.l0_hi, k.l0_lo)]
        block = ctx.enter_context(nc.Block())

        @block.gpsimd
        def _(pool):
            pool.sem_inc(copied, 1)
            with pool.Fori(0, GROUPS) as i:
                pool.wait_ge(transposed, i + 1)
                nc.gpsimd.tensor_copy(xc[:, :, :].rearrange("p t h -> p (t h)"),
                                      k.x[:, bass.ds(i * GROUP * H, GROUP * H)]).then_inc(copied, 1)

        @block.tensor
        def _(pe):
            pe.sem_inc(transposed, 1)
            pe.sem_inc(scored, 1)
            with pe.Fori(0, GROUPS) as i:
                pe.wait_ge(copied, i + 2)
                pe.wait_ge(lo_done, i + 1)
                for m in range(KT):
                    for t in range(GROUP):
                        last = nc.tensor.transpose(ps[:, m, t * P:(t + 1) * P], xc[:, t, m * P:(m + 1) * P],
                                                   k.ident[:, :])
                last.then_inc(transposed, 1)
                pe.wait_ge(lo_done, i + 2)
                pe.wait_ge(kept, i + 1)
                for t in range(GROUP):
                    for m in range(KT):
                        last = split_matmul(nc, ps[:, 2, t * W:(t + 1) * W],
                                            [a[:, m, t * P:(t + 1) * P] for a in (xhi, xlo)],
                                            [w[:, m, :] for w in wt], m == 0, m == KT - 1)
                last.then_inc(scored, 1)

        @block.scalar
        def _(act):
            with act.Fori(0, GROUPS) as i:
                act.wait_ge(transposed, i + 2)
                act.wait_ge(scored, i + 1)
                nc.scalar.activation(xhi[:, :, :], ps[:, 0:2, :], ACT.Copy).then_inc(hi_done, 1)
            act.wait_ge(chain, 2)
            nc.scalar.activation(prob[:, :, :], prob[:, :, :], ACT.Exp).then_inc(exps, 1)
            act.wait_ge(chain, 3)
            nc.scalar.activation(gate[:, :], gate[:, :], ACT.Exp).then_inc(exps, 1)

        @block.vector
        def _(dve):
            dve.sem_inc(lo_done, 1)
            dve.sem_inc(kept, 1)
            with dve.Fori(0, GROUPS) as i:
                dve.wait_ge(hi_done, i + 1)
                nc.vector.tensor_tensor(xlo[:, :, :], ps[:, 0:2, :], xhi[:, :, :], ALU.subtract)\
                    .then_inc(lo_done, 1)
                dve.wait_ge(scored, i + 2)
                nc.vector.tensor_copy(logit[:, :, :].rearrange("p t e -> p (t e)")[:, bass.ds(i * GROUP * W, GROUP * W)],
                                      ps[:, 2, 0:GROUP * W]).then_inc(kept, 1)
            dve.wait_ge(kept, GROUPS + 1)
            links = [0]

            def link(ins):
                ins.then_inc(chain, 1)
                links[0] += 1
                dve.wait_ge(chain, links[0])

            def per_expert(t):
                return t.unsqueeze(2).broadcast_to([P, TILES, E])

            link(nc.vector.tensor_reduce(top[:, :], logit[:, :, 0:E], AX_X, ALU.max))
            link(nc.vector.tensor_tensor(prob[:, :, :], logit[:, :, 0:E], per_expert(top[:, :]), ALU.subtract))
            link(nc.vector.tensor_scalar(gate[:, :], logit[:, :, E], -1.0, 87.0, ALU.mult, ALU.min))
            dve.wait_ge(exps, 1)
            link(nc.vector.tensor_reduce(tot[:, :], prob[:, :, :], AX_X, ALU.add))
            link(nc.vector.reciprocal(rec[:, :], tot[:, :]))
            link(nc.vector.tensor_tensor(prob[:, :, :], prob[:, :, :], per_expert(rec[:, :]), ALU.mult))
            for g in range(TILES // TG):
                pg = prob[:, g * TG:(g + 1) * TG, :]
                other = pg.unsqueeze(2).broadcast_to([P, TG, E, E])
                own = pg.unsqueeze(3).broadcast_to([P, TG, E, E])
                earlier = k.earlier[:, :, :].unsqueeze(1).broadcast_to([P, TG, E, E])
                link(nc.vector.tensor_tensor(tied[:, :, :, :], other, own, ALU.is_equal))
                link(nc.vector.tensor_tensor(tied[:, :, :, :], tied[:, :, :, :], earlier, ALU.mult))
                link(nc.vector.tensor_tensor(above[:, :, :, :], other, own, ALU.is_gt))
                link(nc.vector.tensor_tensor(above[:, :, :, :], above[:, :, :, :], tied[:, :, :, :], ALU.add))
                link(nc.vector.tensor_reduce(rank[:, g * TG:(g + 1) * TG, :], above[:, :, :, :], AX_X, ALU.add))
            flat = [t[:, :, :].rearrange("p t e -> p (t e)") for t in (rank, prob)]
            link(nc.vector.scalar_tensor_tensor(out=flat[0], in0=flat[0], scalar=float(TOPK), in1=flat[1],
                                                op0=ALU.is_lt, op1=ALU.mult))
            link(nc.vector.tensor_reduce(tot[:, :], rank[:, :, :], AX_X, ALU.add))
            link(nc.vector.tensor_scalar_max(tot[:, :], tot[:, :], 1e-9))
            link(nc.vector.reciprocal(rec[:, :], tot[:, :]))
            link(nc.vector.tensor_tensor(k.comb[:, 0:TILES, 0:E], rank[:, :, :], per_expert(rec[:, :]), ALU.mult))
            dve.wait_ge(exps, 2)
            link(nc.vector.tensor_scalar_add(gate[:, :], gate[:, :], 1.0))
            link(nc.vector.reciprocal(rec[:, :], gate[:, :]))
            link(nc.vector.tensor_copy(k.comb[:, :, E:SLICES],
                                       rec[:, :].unsqueeze(2).broadcast_to([P, TILES, SH])))


def feed_forward_stage(nc, k, tag, chunks, width, blocks, up, down, comb, unroll, prep=None, store=False):
    U, C, NP = unroll, chunks, blocks // 2
    NB = 3
    ITERS = TILES // U
    bank_of = [j % NB for j in range(U * C)]

    def since(j):
        return next(d for d in range(1, U * C + 1) if bank_of[(j - d) % (U * C)] == bank_of[j])

    def covers(p):
        return min(-(-256 * (p + 1) // width), C) - 1

    def last_pair(c):
        return min(((c + 1) * width - 1) // 256, NP - 1)

    transpose_at, down_at = {}, {}
    for u in range(U):
        for p in range(NP):
            j = u * C + covers(p) + 2
            while len(transpose_at.get(j, [])) >= 1 and NP > 4:
                j += 1
            transpose_at.setdefault(j, []).append((u, p))
            down_at.setdefault(j + 2, []).append((u, p))
    ends = {max(j for j, l in down_at.items() if (u, NP - 1) in l) + 1: u for u in range(U)}
    STEPS = max(max(down_at), max(ends)) + 1

    with ExitStack() as ctx:
        def sb(name, shape, dt=F32):
            return ctx.enter_context(nc.sbuf_tensor(tag + name, shape, dt))

        def sem(name):
            return ctx.enter_context(nc.semaphore(tag + name))

        xc = sb("xc", [P, 2, H])
        xhi = sb("xhi", [P, 2, KT * P], F16)
        xlo = sb("xlo", [P, 2, KT * P], F16)
        sil = sb("sil", [P, NB, width])
        hid = sb("hid", [P, blocks * P])
        hhi = sb("hhi", [P, 2, 256], F16)
        hlo = sb("hlo", [P, 2, 256], F16)
        res = sb("res", [P, 2, H])
        st = sb("st", [P, 2, 6])
        mv = sb("mv", [P, 2, 2])
        std = sb("std", [P, 2])
        rstd = sb("rstd", [P, 2])
        copied = sem("copied")
        x_turned = sem("x_turned")
        x_hi = sem("x_hi")
        x_lo = sem("x_lo")
        up_done = sem("up_done")
        sil_done = sem("sil_done")
        hid_done = sem("hid_done")
        turned = sem("turned")
        h_hi = sem("h_hi")
        h_lo = sem("h_lo")
        down_done = sem("down_done")
        summed = sem("summed")
        std_done = sem("std_done")
        chain = sem("norm_chain")
        passed = sem("aggregate_waits")
        zeroed = sem("zeroed")
        stored = sem("stored")
        ps = k.ps
        parity = U // 2 if U > 1 else 1
        assert U % 2 == 0
        block = ctx.enter_context(nc.Block())

        if prep or store:
            @block.sync
            def _(sp):
                with sp.Fori(0, ITERS) as i:
                    if prep:
                        prep.load(sp, i)
                    if store:
                        for u in range(U):
                            sp.wait_ge(chain, (i * U + u + 1) * 4)
                            sp.dma_start(k.d_out[bass.ds(i * U + u, 1)].rearrange("t p h -> p (t h)"),
                                         k.x[:, bass.ds(i * (U * H) + u * H, H)]).then_inc(stored, 16)
                if store:
                    sp.wait_ge(stored, 16 * TILES)

        @block.gpsimd
        def _(pool):
            if blocks * P > C * width:
                nc.gpsimd.memset(hid[:, C * width:], 0.0).then_inc(zeroed, 1)
            if prep:
                prep.start(pool)
            pool.wait_ge(x_turned, 1)
            nc.gpsimd.tensor_copy(xc[:, 0, :], k.x[:, 0:H]).then_inc(copied, 1)
            with pool.Fori(0, ITERS) as i:
                for u in range(U):
                    pool.wait_ge(x_turned, i * U + u + 1)
                    nc.gpsimd.tensor_copy(xc[:, (u + 1) % 2, :],
                                          k.x[:, bass.ds(i * (U * H) + (u + 1) * H, H)]).then_inc(copied, 1)
                if prep:
                    prep.split(pool, i)

        def x_turn(pe, u):
            for m in range(KT):
                last = nc.tensor.transpose(ps[:, 7, m * P:(m + 1) * P], xc[:, u % 2, m * P:(m + 1) * P],
                                           k.ident[:, :])
            last.then_inc(x_turned, 1)

        @block.tensor
        def _(pe):
            pe.sem_inc(x_turned, 1)
            pe.sem_inc(turned, NP)
            pe.sem_inc(down_done, 2)
            if blocks * P > C * width:
                pe.wait_ge(zeroed, 1)
            pe.wait_ge(copied, 1)
            x_turn(pe, 0)
            with pe.Fori(0, ITERS) as i:
                for j in range(STEPS):
                    u, c = j // C, j % C
                    if j < U * C:
                        if c == 0:
                            pe.wait_ge(x_lo, i * U + u + 1)
                        pe.wait_ge(hid_done, i * (U * C) + j + 1 - since(j) + NB)
                        for m in range(KT):
                            last = split_matmul(nc, ps[:, bank_of[j], 0:2 * width],
                                                [a[:, u % 2, m * P:(m + 1) * P] for a in (xhi, xlo)],
                                                [w[:, m, c, :] for w in up], m == 0, m == KT - 1)
                        last.then_inc(up_done, 1)
                        if c == C // 2:
                            pe.wait_ge(copied, i * U + u + 2)
                            x_turn(pe, u + 1)
                    for uu, p in down_at.get(j, []):
                        pe.wait_ge(h_lo, i * (U * NP) + uu * NP + p + 3)
                        if p == 0:
                            pe.wait_ge(summed, i * U + uu + 1)
                        for b in range(2):
                            last = split_matmul(nc, ps[:, 5 + uu % 2, 0:H],
                                                [a[:, p % 2, b * P:(b + 1) * P] for a in (hhi, hlo)],
                                                [w[:, 2 * p + b, :] for w in down],
                                                p == 0 and b == 0, p == NP - 1 and b == 1)
                        last.then_inc(down_done, 1)
                    for uu, p in transpose_at.get(j, []):
                        pe.wait_ge(hid_done, i * (U * C) + uu * C + covers(p) + 1 + NB)
                        pe.wait_ge(h_lo, i * (U * NP) + uu * NP + p + 1)
                        for b in range(2):
                            last = nc.tensor.transpose(ps[:, 3 + p % 2, b * P:(b + 1) * P],
                                                       hid[:, (2 * p + b) * P:(2 * p + b + 1) * P],
                                                       k.ident[:, :])
                        last.then_inc(turned, 1)

        @block.scalar
        def _(act):
            act.wait_ge(x_turned, 2)
            nc.scalar.activation(xhi[:, 0, :], ps[:, 7, 0:H], ACT.Copy).then_inc(x_hi, 1)
            with act.Fori(0, ITERS) as i:
                for j in range(STEPS):
                    u, c = j // C, j % C
                    if j < U * C:
                        act.wait_ge(up_done, i * (U * C) + j + 1)
                        nc.scalar.activation(sil[:, bank_of[j], :], ps[:, bank_of[j], 0:width], ACT.Silu)\
                            .then_inc(sil_done, 1)
                        if c == C // 2:
                            act.wait_ge(x_turned, i * U + u + 3)
                            nc.scalar.activation(xhi[:, (u + 1) % 2, :], ps[:, 7, 0:H], ACT.Copy)\
                                .then_inc(x_hi, 1)
                    for uu, p in transpose_at.get(j, []):
                        act.wait_ge(turned, i * (U * NP) + uu * NP + p + 1 + NP)
                        act.wait_ge(down_done, i * (U * NP) + uu * NP + p + 1)
                        nc.scalar.activation(hhi[:, p % 2, :], ps[:, 3 + p % 2, 0:256], ACT.Copy)\
                            .then_inc(h_hi, 1)
                    if j in ends:
                        uu = ends[j]
                        act.wait_ge(chain, i * (4 * U) + 4 * uu + 2)
                        nc.scalar.activation(std[:, uu % 2:uu % 2 + 1], mv[:, uu % 2, 1:2], ACT.Sqrt,
                                             bias=k.eps[:, 0:1]).then_inc(std_done, 1)

        @block.vector
        def _(dve):
            dve.sem_inc(hid_done, NB)
            dve.sem_inc(h_lo, 2)
            dve.sem_inc(summed, 2)
            dve.wait_ge(x_hi, 1)
            nc.vector.tensor_tensor(xlo[:, 0, :], ps[:, 7, 0:H], xhi[:, 0, :], ALU.subtract).then_inc(x_lo, 1)
            with dve.Fori(0, ITERS) as i:
                for j in range(STEPS):
                    u, c = j // C, j % C
                    if j < U * C:
                        dve.wait_ge(sil_done, i * (U * C) + j + 1)
                        dve.wait_ge(turned, i * (U * NP) + u * NP + last_pair(c) + 1)
                        out = hid[:, c * width:(c + 1) * width]
                        upper = ps[:, bank_of[j], width:2 * width]
                        if comb is None:
                            nc.vector.tensor_tensor(out, sil[:, bank_of[j], :], upper, ALU.mult)\
                                .then_inc(hid_done, 1)
                        else:
                            nc.vector.scalar_tensor_tensor(
                                out=out, in0=sil[:, bank_of[j], :],
                                scalar=comb[:, bass.ds(i * (U * SLICES) + u * SLICES + c, 1)], in1=upper,
                                op0=ALU.mult, op1=ALU.mult).then_inc(hid_done, 1)
                        if c == C // 2:
                            dve.wait_ge(x_hi, i * U + u + 2)
                            nc.vector.tensor_tensor(xlo[:, (u + 1) % 2, :], ps[:, 7, 0:H],
                                                    xhi[:, (u + 1) % 2, :], ALU.subtract).then_inc(x_lo, 1)
                    for uu, p in transpose_at.get(j, []):
                        dve.wait_ge(h_hi, i * (U * NP) + uu * NP + p + 1)
                        nc.vector.tensor_tensor(hlo[:, p % 2, :], ps[:, 3 + p % 2, 0:256], hhi[:, p % 2, :],
                                                ALU.subtract).then_inc(h_lo, 1)
                    if j in ends:
                        uu = ends[j]
                        s = uu % 2
                        mine = k.x[:, bass.ds(i * (U * H) + uu * H, H)]
                        dve.wait_ge(down_done, i * (U * NP) + (uu + 1) * NP + 2)
                        nc.vector.tensor_tensor(res[:, s, :], ps[:, 5 + s, 0:H], mine, ALU.add)\
                            .then_inc(summed, 1)
                        dve.wait_ge(summed, i * U + uu + 3)
                        nc.vector.bn_stats(st[:, s, :], res[:, s, :]).then_inc(chain, 1)
                        hold(dve, chain, i * (4 * U) + 4 * uu + 1, passed)
                        nc.vector.bn_aggr(mv[:, s, :], st[:, s, :]).then_inc(chain, 1)
                        dve.wait_ge(std_done, i * U + uu + 1)
                        nc.vector.reciprocal(rstd[:, s:s + 1], std[:, s:s + 1]).then_inc(chain, 1)
                        dve.wait_ge(chain, i * (4 * U) + 4 * uu + 3)
                        nc.vector.tensor_scalar(mine, res[:, s, :], mv[:, s, 0:1], rstd[:, s:s + 1],
                                                ALU.subtract, ALU.mult).then_inc(chain, 1)


class Layer1Split:

    def __init__(self, nc, ctx, k, parts):
        self.nc, self.k, self.n = nc, k, C_L1 // parts
        assert C_L1 % parts == 0
        self.raw = ctx.enter_context(nc.sbuf_tensor("l1_raw", [P, self.n], F32))
        self.loaded = ctx.enter_context(nc.semaphore("l1_loaded"))
        self.hi_done = ctx.enter_context(nc.semaphore("l1_hi_done"))
        self.lo_done = ctx.enter_context(nc.semaphore("l1_lo_done"))

    def start(self, pool):
        pool.sem_inc(self.lo_done, 1)

    def load(self, sp, i):
        sp.wait_ge(self.lo_done, i + 1)
        sp.dma_start(self.raw[:, :], self.k.d_l1[:, bass.ds(i * self.n, self.n)]).then_inc(self.loaded, 16)

    def split(self, pool, i):
        nc, k = self.nc, self.k
        hi = k.l1_hi[:, bass.ds(i * self.n, self.n)]
        pool.wait_ge(self.loaded, (i + 1) * 16)
        nc.gpsimd.tensor_copy(hi, self.raw[:, :]).then_inc(self.hi_done, 1)
        pool.wait_ge(self.hi_done, i + 1)
        nc.gpsimd.tensor_tensor(k.l1_lo[:, bass.ds(i * self.n, self.n)], self.raw[:, :], hi, ALU.subtract)\
            .then_inc(self.lo_done, 1)


def hadamard_stage(nc, k):
    with ExitStack() as ctx:
        def sb(name, shape, dt=F32):
            return ctx.enter_context(nc.sbuf_tensor("hd_" + name, shape, dt))

        def sem(name):
            return ctx.enter_context(nc.semaphore("hd_" + name))

        raw = sb("raw", [P, FF_BLOCKS, H])
        had = sb("had", [P, P])
        a = sb("a", [P, FF_BLOCKS, H])
        b = sb("b", [P, FF_BLOCKS, H])
        loaded, multiplied, chain, hi_done = sem("loaded"), sem("multiplied"), sem("chain"), sem("hi_done")
        block = ctx.enter_context(nc.Block())

        @block.sync
        def _(sp):
            sp.dma_start(had[:, :], k.d_had).then_inc(loaded, 16)
            sp.dma_start(raw[:, :, :], k.d_w2).then_inc(loaded, 16)
            sp.dma_start(k.att_const[:, :], k.d_att).then_inc(loaded, 16)
            sp.wait_ge(loaded, 48)

        @block.tensor
        def _(pe):
            pe.wait_ge(loaded, 48)
            for c in range(FF_BLOCKS):
                last = nc.tensor.matmul(k.ps[:, c // 2, (c % 2) * H:(c % 2 + 1) * H], had[:, :], raw[:, c, :],
                                        start=True, stop=True)
            last.then_inc(multiplied, 1)

        @block.vector
        def _(dve):
            dve.wait_ge(multiplied, 1)
            nc.vector.tensor_copy(a[:, :, :].rearrange("p c h -> p (c h)"),
                                  k.ps[:, 0:4, :].rearrange("p b n -> p (b n)")).then_inc(chain, 1)
            src, dst, n = a, b, 1
            for span in (1, 2, 4):
                dve.wait_ge(chain, n)
                v, w = (t[:, :, :].rearrange("p (x two s) h -> p two x (s h)", two=2, s=span) for t in (src, dst))
                nc.vector.tensor_tensor(w[:, 0], v[:, 0], v[:, 1], ALU.add).then_inc(chain, 1)
                nc.vector.tensor_tensor(w[:, 1], v[:, 0], v[:, 1], ALU.subtract).then_inc(chain, 1)
                src, dst, n = dst, src, n + 2
            dve.wait_ge(chain, n)
            nc.vector.tensor_scalar_mul(dst[:, :, :], src[:, :, :], I_FF ** -0.5).then_inc(chain, 1)
            dve.wait_ge(chain, n + 1)
            nc.vector.tensor_copy(k.w2_hi[:, :, :], dst[:, :, :]).then_inc(hi_done, 1)
            dve.wait_ge(hi_done, 1)
            nc.vector.tensor_tensor(k.w2_lo[:, :, :], dst[:, :, :], k.w2_hi[:, :, :], ALU.subtract)\
                .then_inc(chain, 1)


def attention_stage(nc, k):
    UNITS = [(t, g, kt) for t in range(2) for g in range(KV) for kt in range(t + 1)]
    GROUPS_PV = [(t, g) for t in range(2) for g in range(KV)]
    NU, RING_E, RING_P = len(UNITS), 3, 4
    NAT = [(0, 0), (0, 2)] + [(1, g) for g in range(KV)]
    pv_of = {v: GROUPS_PV.index((t, g)) for v, (t, g, _) in enumerate(UNITS)}
    units_of = {n: [v for v in range(NU) if pv_of[v] == n] for n in range(len(GROUPS_PV))}
    V1 = D + 1
    VEC = ["xlo", "q", "klo"] + [f"max{u}" for u in range(len(NAT))] + ["rec", "o", "olo", "res", "stats", "mv",
                                                                       "rstd", "out"]
    SCA = ["xhi", "qhi", "khi", "v", "shift"] + [f"exp{v}" for v in range(NU)] + ["ohi", "std"]
    PEN = ["xT", "q", "kv"] + [f"nat{u}" for u in range(len(NAT))] + ["maxT"]
    for v in range(NU + 2):
        if v < NU:
            PEN.append(f"score{v}")
        PEN += [f"pv{n}" for n, l in units_of.items() if l[-1] == v - 2]
    PEN += ["oT", "wo"]
    POL = ["copy"] + [f"prob{v}" for v in range(NU)]
    with ExitStack() as ctx:
        def sb(name, shape, dt=F32):
            return ctx.enter_context(nc.sbuf_tensor("at_" + name, shape, dt))

        def sem(name):
            return ctx.enter_context(nc.semaphore("at_" + name))

        bias = sb("bias", [P, KV, 2, REP, P])
        cst = sb("cst", [P, 6 * P], BF16)
        eye, mask = cst[:, 0:P], cst[:, P:2 * P]
        pick = cst[:, 2 * P:6 * P].rearrange("p (r n) -> p r n", r=REP)
        negate = k.att_const[:, 0:1]
        xc = sb("xc", [P, 2 * H])
        xhi = sb("xhi", [P, KT, T], F16)
        xlo = sb("xlo", [P, KT, T], F16)
        qh = sb("qh", [P, REP, T], F16)
        q = sb("q", [P, REP, T], F16)
        kh = sb("kh", [P, T], F16)
        kl = sb("kl", [P, T], F16)
        v1 = sb("v1", [P, 2, KV, V1])
        top = sb("top", [P, 2, KV, SLOT])
        shift = sb("shift", [P, 2 * P], BF16)
        ex = sb("ex", [P, RING_E, REP * P])
        pr = sb("pr", [P, RING_P, REP * P])
        rec = sb("rec", [P, 2, HEADS])
        o = sb("o", [P, 2, H])
        ohi = sb("ohi", [P, KT, T], F16)
        olo = sb("olo", [P, KT, T], F16)
        res = sb("res", [P, 2, H])
        st = sb("st", [P, 2, 6])
        mv = sb("mv", [P, 2, 2])
        std = sb("std", [P, 2])
        rstd = sb("rstd", [P, 2])
        vec, sca, pen, pol = (Steps(sem(n), l) for n, l in (("vector_steps", VEC), ("scalar_steps", SCA),
                                                            ("tensor_steps", PEN), ("pool_steps", POL)))
        loaded, ready, passed = sem("bias_loaded"), sem("constants_ready"), sem("aggregate_waits")
        ps = k.ps
        at = [0]
        w = []
        for n, dims in ((C_Q, (REP, P)), (C_K, (1, P)), (C_V, (1, KV * D)), (C_O, (1, H))):
            w.append([s[:, at[0]:at[0] + n].rearrange("p (m r n) -> p m r n", m=KT, r=dims[0])
                      for s in (k.l1_hi, k.l1_lo)])
            at[0] += n
        wq, wk, wv, wo = w
        BANK = [1, 2, 4, 5]
        block = ctx.enter_context(nc.Block())

        def slot(g):
            return slice(SLOT * g, SLOT * (g + 1))

        @block.sync
        def _(sp):
            sp.dma_start(bias[:, :, :, :, :].rearrange("p g y r n -> p (g y r n)"), k.d_bias).then_inc(loaded, 16)

        @block.gpsimd
        def _(pool):
            pol.start(pool)
            nc.gpsimd.memset(top[:, :, :, :], 0.0)
            nc.gpsimd.memset(v1[:, :, :, D:V1], 1.0)
            nc.gpsimd.tensor_copy(cst[:, :], k.att_const[:, 1:]).then_inc(ready, 1)
            pool.wait_ge(loaded, 16)
            with pool.Fori(0, SEQS) as i:
                pool.wait_ge(pen.sem, pen.after(i - 1, "xT"))
                nc.gpsimd.tensor_copy(xc[:, :], k.x[:, bass.ds(i * (2 * H), 2 * H)]).then_inc(pol.sem, 1)
                for v, (t, g, kt) in enumerate(UNITS):
                    pool.wait_ge(sca.sem, sca.after(i, f"exp{v}"))
                    if v >= RING_P:
                        pool.wait_ge(pen.sem, pen.after(i, f"pv{pv_of[v - RING_P]}"))
                    nc.gpsimd.tensor_tensor(pr[:, v % RING_P, :], ex[:, v % RING_E, :],
                                            bias[:, g, t - kt, :, :].rearrange("p r n -> p (r n)"), ALU.mult)\
                        .then_inc(pol.sem, 1)

        @block.tensor
        def _(pe):
            pen.start(pe)
            pe.wait_ge(ready, 1)
            with pe.Fori(0, SEQS) as i:
                pe.wait_ge(pol.sem, pol.after(i, "copy"))
                for m in range(KT):
                    for t in range(2):
                        last = nc.tensor.transpose(ps[:, 0, m * T + t * P:m * T + (t + 1) * P],
                                                   xc[:, t * H + m * P:t * H + (m + 1) * P], k.ident[:, :])
                last.then_inc(pen.sem, 1)
                pe.wait_ge(vec.sem, vec.after(i, "xlo"))
                for r in range(REP):
                    for m in range(KT):
                        last = split_matmul(nc, ps[:, 1 + r // 2, (r % 2) * T:(r % 2 + 1) * T],
                                            [s[:, m, r, :] for s in wq], [s[:, m, :] for s in (xhi, xlo)],
                                            m == 0, m == KT - 1)
                last.then_inc(pen.sem, 1)
                pe.wait_ge(vec.sem, vec.after(i - 1, "res"))
                for m in range(KT):
                    split_matmul(nc, ps[:, 3, 0:T], [s[:, m, 0, :] for s in wk],
                                 [s[:, m, :] for s in (xhi, xlo)], m == 0, m == KT - 1)
                for t in range(2):
                    for m in range(KT):
                        last = split_matmul(nc, ps[:, 3, T + t * KV * D:T + (t + 1) * KV * D],
                                            [s[:, m, t * P:(t + 1) * P] for s in (xhi, xlo)],
                                            [s[:, m, 0, :] for s in wv], m == 0, m == KT - 1)
                last.then_inc(pen.sem, 1)
                pe.wait_ge(vec.sem, vec.after(i, "q"))
                pe.wait_ge(sca.sem, sca.after(i, "khi"))
                for u, (t, g0) in enumerate(NAT):
                    if u >= 2:
                        pe.wait_ge(vec.sem, vec.after(i, f"max{u - 2}"))
                    b0 = (1, 4)[u % 2]
                    for b in range(2):
                        nk = P * (t + 1)
                        out = ps[:, b0 + b, :].rearrange("p (r n) -> p r n", n=nk)
                        reps = 512 // nk
                        nc.tensor.matmul(out[:, :, nk - P:nk], eye, mask.unsqueeze(1).broadcast_to([P, reps, P]),
                                         start=True, stop=False, skip_group_check=True)
                        g = g0 + b if t == 0 else g0
                        for r in range(reps):
                            rr = r if t == 0 else 2 * b + r
                            last = nc.tensor.matmul(out[:, r, :], q[slot(g), rr, t * P:(t + 1) * P],
                                                    kh[slot(g), 0:nk], start=False, stop=r == reps - 1,
                                                    skip_group_check=True, tile_position=(SLOT * g, 0))
                    last.then_inc(pen.sem, 1)
                pe.wait_ge(vec.sem, vec.after(i, f"max{len(NAT) - 1}"))
                for t in range(2):
                    last = nc.tensor.transpose(ps[:, 0, t * P:(t + 1) * P],
                                               top[:, t, :, :].rearrange("p g s -> p (g s)"), k.ident[:, :])
                last.then_inc(pen.sem, 1)
                pe.wait_ge(sca.sem, sca.after(i, "shift"))
                pe.wait_ge(vec.sem, vec.after(i, "klo"))
                for v in range(NU + 2):
                    if v < NU:
                        t, g, kt = UNITS[v]
                        if v >= 4:
                            pe.wait_ge(sca.sem, sca.after(i, f"exp{v - 4}"))
                        out = ps[:, BANK[v % 4], :]
                        for n, keys in enumerate((kh, kl)):
                            nc.tensor.matmul(out.rearrange("p (r n) -> p r n", r=REP),
                                             keys[slot(g), kt * P:(kt + 1) * P], q[slot(g), :, t * P:(t + 1) * P],
                                             start=n == 0, stop=False, skip_group_check=True,
                                             tile_position=(SLOT * g, 0))
                        for r in range(REP):
                            last = nc.tensor.matmul(out[:, r * P:(r + 1) * P], pick[slot(g), r, :],
                                                    shift[slot(g), t * P:(t + 1) * P], start=False,
                                                    stop=r == REP - 1, skip_group_check=True,
                                                    tile_position=(SLOT * g, 0))
                        last.then_inc(pen.sem, 1)
                    for n, l in units_of.items():
                        if l[-1] == v - 2:
                            t, g = GROUPS_PV[n]
                            pe.wait_ge(pol.sem, pol.after(i, f"prob{l[-1]}"))
                            for r in range(REP):
                                h = g * REP + r
                                for kt, vv in enumerate(l):
                                    last = nc.tensor.matmul(ps[:, 6 + t, h * V1:(h + 1) * V1],
                                                            pr[:, vv % RING_P, r * P:(r + 1) * P],
                                                            v1[:, kt, g, :], start=kt == 0, stop=kt == t,
                                                            skip_group_check=True)
                            last.then_inc(pen.sem, 1)
                pe.wait_ge(vec.sem, vec.after(i, "o"))
                for m in range(KT):
                    for t in range(2):
                        last = nc.tensor.transpose(ps[:, 0, m * T + t * P:m * T + (t + 1) * P],
                                                   o[:, t, m * P:(m + 1) * P], k.ident[:, :])
                last.then_inc(pen.sem, 1)
                pe.wait_ge(vec.sem, vec.after(i, "olo"))
                for t in range(2):
                    for m in range(KT):
                        last = split_matmul(nc, ps[:, 3, t * H:(t + 1) * H],
                                            [s[:, m, t * P:(t + 1) * P] for s in (ohi, olo)],
                                            [s[:, m, 0, :] for s in wo], m == 0, m == KT - 1)
                last.then_inc(pen.sem, 1)

        @block.scalar
        def _(act):
            sca.start(act)
            act.wait_ge(ready, 1)
            with act.Fori(0, SEQS) as i:
                act.wait_ge(pen.sem, pen.after(i, "xT"))
                nc.scalar.activation(xhi[:, :, :].rearrange("p m t -> p (m t)"), ps[:, 0, :], ACT.Copy)\
                    .then_inc(sca.sem, 1)
                act.wait_ge(pen.sem, pen.after(i, "q"))
                nc.scalar.activation(qh[:, :, :].rearrange("p r t -> p (r t)"),
                                     ps[:, 1:3, :].rearrange("p b n -> p (b n)"), ACT.Copy).then_inc(sca.sem, 1)
                act.wait_ge(pen.sem, pen.after(i, "kv"))
                nc.scalar.activation(kh[:, :], ps[:, 3, 0:T], ACT.Copy).then_inc(sca.sem, 1)
                nc.scalar.activation(v1[:, :, :, 0:D],
                                     ps[:, 3, T:T + 2 * KV * D].rearrange("p (t g d) -> p t g d", t=2, g=KV),
                                     ACT.Copy).then_inc(sca.sem, 1)
                act.wait_ge(pen.sem, pen.after(i, "maxT"))
                nc.scalar.activation(shift[:, :], ps[:, 0, 0:2 * P], ACT.Copy, scale=-1.0).then_inc(sca.sem, 1)
                for v in range(NU):
                    act.wait_ge(pen.sem, pen.after(i, f"score{v}"))
                    if v >= RING_E:
                        act.wait_ge(pol.sem, pol.after(i, f"prob{v - RING_E}"))
                    nc.scalar.activation(ex[:, v % RING_E, :], ps[:, BANK[v % 4], :], ACT.Exp, scale=SCALE)\
                        .then_inc(sca.sem, 1)
                act.wait_ge(pen.sem, pen.after(i, "oT"))
                nc.scalar.activation(ohi[:, :, :].rearrange("p m t -> p (m t)"), ps[:, 0, :], ACT.Copy)\
                    .then_inc(sca.sem, 1)
                act.wait_ge(vec.sem, vec.after(i, "mv"))
                nc.scalar.activation(std[:, :], mv[:, :, 1], ACT.Sqrt, bias=k.eps[:, 0:1]).then_inc(sca.sem, 1)

        @block.vector
        def _(dve):
            vec.start(dve)
            dve.wait_ge(ready, 1)

            def done(i, name):
                dve.wait_ge(vec.sem, vec.after(i, name))

            with dve.Fori(0, SEQS) as i:
                mine = k.x[:, bass.ds(i * (2 * H), 2 * H)]
                dve.wait_ge(sca.sem, sca.after(i, "xhi"))
                nc.vector.tensor_tensor(xlo[:, :, :].rearrange("p m t -> p (m t)"), ps[:, 0, :],
                                        xhi[:, :, :].rearrange("p m t -> p (m t)"), ALU.subtract)\
                    .then_inc(vec.sem, 1)
                dve.wait_ge(sca.sem, sca.after(i, "qhi"))
                for b in range(2):
                    last = nc.vector.scalar_tensor_tensor(
                        out=q[:, 2 * b:2 * b + 2, :].rearrange("p r t -> p (r t)"),
                        in0=qh[:, 2 * b:2 * b + 2, :].rearrange("p r t -> p (r t)"), scalar=negate,
                        in1=ps[:, 1 + b, :], op0=ALU.mult, op1=ALU.add)
                last.then_inc(vec.sem, 1)
                dve.wait_ge(sca.sem, sca.after(i, "v"))
                nc.vector.tensor_tensor(kl[:, :], ps[:, 3, 0:T], kh[:, :], ALU.subtract).then_inc(vec.sem, 1)
                for u, (t, g0) in enumerate(NAT):
                    b0 = (1, 4)[u % 2]
                    dve.wait_ge(pen.sem, pen.after(i, f"nat{u}"))
                    if t == 0:
                        nc.vector.tensor_reduce(top[:, 0, g0:g0 + 2, 0:REP],
                                                ps[:, b0:b0 + 2, :].rearrange("p g (r n) -> p g r n", r=REP),
                                                AX_X, ALU.max).then_inc(vec.sem, 1)
                    else:
                        nc.vector.tensor_reduce(top[:, 1, g0, 0:REP],
                                                ps[:, b0:b0 + 2, :].rearrange("p b (r n) -> p (b r) n", n=T),
                                                AX_X, ALU.max).then_inc(vec.sem, 1)
                dve.wait_ge(pen.sem, pen.after(i, f"pv{len(GROUPS_PV) - 1}"))
                heads = ps[:, 6:8, 0:HEADS * V1].rearrange("p t (h v) -> p t h v", v=V1)
                nc.vector.reciprocal(rec[:, :, :], heads[:, :, :, D]).then_inc(vec.sem, 1)
                done(i, "rec")
                for t in range(2):
                    last = nc.vector.tensor_tensor(o[:, t, :].rearrange("p (h d) -> p h d", d=D),
                                                   heads[:, t, :, 0:D],
                                                   rec[:, t, :].unsqueeze(2).broadcast_to([P, HEADS, D]), ALU.mult)
                last.then_inc(vec.sem, 1)
                dve.wait_ge(sca.sem, sca.after(i, "ohi"))
                nc.vector.tensor_tensor(olo[:, :, :].rearrange("p m t -> p (m t)"), ps[:, 0, :],
                                        ohi[:, :, :].rearrange("p m t -> p (m t)"), ALU.subtract)\
                    .then_inc(vec.sem, 1)
                dve.wait_ge(pen.sem, pen.after(i, "wo"))
                nc.vector.tensor_tensor(res[:, :, :].rearrange("p t h -> p (t h)"), ps[:, 3, :], mine, ALU.add)\
                    .then_inc(vec.sem, 1)
                done(i, "res")
                for t in range(2):
                    last = nc.vector.bn_stats(st[:, t, :], res[:, t, :])
                last.then_inc(vec.sem, 1)
                hold(dve, vec.sem, vec.after(i, "stats"), passed)
                for t in range(2):
                    last = nc.vector.bn_aggr(mv[:, t, :], st[:, t, :])
                last.then_inc(vec.sem, 1)
                dve.wait_ge(sca.sem, sca.after(i, "std"))
                nc.vector.reciprocal(rstd[:, :], std[:, :]).then_inc(vec.sem, 1)
                done(i, "rstd")
                for t in range(2):
                    last = nc.vector.tensor_scalar(k.x[:, bass.ds(i * (2 * H) + t * H, H)], res[:, t, :],
                                                   mv[:, t, 0:1], rstd[:, t:t + 1], ALU.subtract, ALU.mult)
                last.then_inc(vec.sem, 1)


class Shared:
    pass


def build(nc, x, l0, vecs, moe, l1, w2, ident, had, att, bias, out):
    k = Shared()
    k.d_l0, k.d_vecs, k.d_moe, k.d_l1, k.d_w2, k.d_ident, k.d_had, k.d_att, k.d_bias = \
        l0, vecs, moe, l1, w2, ident, had, att, bias
    k.d_x, k.d_out = x, out
    with ExitStack() as ctx:
        def sb(name, shape, dt=F32):
            return ctx.enter_context(nc.sbuf_tensor(name, shape, dt))

        k.ps = ctx.enter_context(nc.psum_tensor("ps", [P, 8, 512], F32))
        k.x = sb("x", [P, (TILES + 1) * H])
        k.vecs = sb("vecs", [P, 14 + E * E])
        k.earlier = k.vecs[:, 14:14 + E * E].rearrange("p (a b) -> p a b", a=E)
        k.decay = sb("decay", [P, KT])
        k.wrow = sb("wrow", [P, KT, T])
        k.eps = sb("eps", [P, 1])
        k.ident = sb("ident", [P, P])
        k.comb = sb("comb", [P, TILES, SLICES])
        k.l0_hi, k.l0_lo = sb("l0_hi", [P, C_L0], F16), sb("l0_lo", [P, C_L0], F16)
        k.moe_hi, k.moe_lo = sb("moe_hi", [P, C_MOE], F16), sb("moe_lo", [P, C_MOE], F16)
        load_stage(nc, k)
        time_mix_stage(nc, k)
        router_stage(nc, k)
        k.l1_hi, k.l1_lo = sb("l1_hi", [P, C_L1], F16), sb("l1_lo", [P, C_L1], F16)
        k.att_const = sb("att_const", [P, 1 + 6 * P])
        with ExitStack() as inner:
            unroll = 2
            prep = Layer1Split(nc, inner, k, TILES // unroll)
            up = [w[:, 0:C_GU].rearrange("p (m c n) -> p m c n", m=KT, c=SLICES) for w in (k.moe_hi, k.moe_lo)]
            down = [w[:, C_GU:].rearrange("p (b h) -> p b h", h=H) for w in (k.moe_hi, k.moe_lo)]
            feed_forward_stage(nc, k, "moe_", SLICES, I_MOE, MOE_BLOCKS, up, down,
                               k.comb[:, :, :].rearrange("p t e -> p (t e)"), unroll, prep)
        k.w2_hi = k.moe_hi[:, 0:FF_BLOCKS * H].rearrange("p (c h) -> p c h", h=H)
        k.w2_lo = k.moe_lo[:, 0:FF_BLOCKS * H].rearrange("p (c h) -> p c h", h=H)
        hadamard_stage(nc, k)
        attention_stage(nc, k)
        at = C_Q + C_K + C_V + C_O
        up = [w[:, at:at + C_FF].rearrange("p (m c n) -> p m c n", m=KT, c=I_FF // 256)
              for w in (k.l1_hi, k.l1_lo)]
        feed_forward_stage(nc, k, "ff_", I_FF // 256, 256, FF_BLOCKS, up, [k.w2_hi, k.w2_lo], None, 4,
                           store=True)


def rows(a):
    return a.reshape(-1, P, a.shape[-1]).transpose(1, 0, 2)


def cols(*parts):
    return np.ascontiguousarray(np.concatenate([p.reshape(P, -1) for p in parts], axis=1))


def kernel(**inputs):
    import concourse.bacc as bacc
    from concourse.bass_utils import run_bass_kernel_spmd

    a = {n: np.asarray(v) for n, v in inputs.items()}
    A, F, B, G = "L0_attn_", "L0_ffn_", "L1_attn_", "L1_ffn_"
    f32 = np.float32

    gates = np.concatenate([a[F + "w_gate"].transpose(1, 0, 2), a[F + "sh_gate"].reshape(H, SH, I_MOE)], 1)
    ups = np.concatenate([a[F + "w_up"].transpose(1, 0, 2), a[F + "sh_up"].reshape(H, SH, I_MOE)], 1)
    gate_up = np.concatenate([gates, ups], 2).reshape(H, -1)
    down = np.zeros((MOE_BLOCKS * P, H), f32)
    down[:SLICES * I_MOE] = np.concatenate([a[F + "w_down"].reshape(-1, H), a[F + "sh_down"]], 0)

    wq = a[B + "Wq"].T.reshape(H, KV, REP, D).transpose(0, 2, 1, 3)
    wq = np.concatenate([wq, wq], 3).reshape(H, REP * P)
    wk = a[B + "Wk"].T.reshape(H, KV, D)
    wk = np.concatenate([wk, wk], 2).reshape(H, P)
    chunks = I_FF // 256
    ff = np.concatenate([a[G + "W1"].T.reshape(H, chunks, 256), a[G + "W3"].T.reshape(H, chunks, 256)], 2)

    vec_names = ["ln_scale", "ln_bias", "mix_k", "mix_v", "mix_r", "time_first", "time_decay"]
    earlier = np.broadcast_to(np.tril(np.ones((E, E), f32), -1), (P, E, E))

    had = np.ones((1, 1), f32)
    while had.shape[0] < P:
        had = np.block([[had, had], [had, -had]])
    row, col = np.arange(P)[:, None], np.arange(P)[None, :]
    negate = np.where(np.arange(P)[:, None] % SLOT < D, 0.0, -1.0).astype(f32)
    mask = np.where(col > row, NEG, 0.0).astype(f32)
    pick = np.stack([np.broadcast_to((np.arange(P) % SLOT == r)[:, None], (P, P)) for r in range(REP)], 1)
    slopes = 2.0 ** (-8.0 / HEADS * np.arange(1, HEADS + 1))
    dist = np.stack([col - row, col - row + P], 0).astype(np.float64)
    bias = np.exp(-slopes[:, None, None, None] * np.sqrt(np.maximum(dist, 0))) * (dist >= 0)
    bias = bias.reshape(KV, REP, 2, P, P).transpose(3, 0, 2, 1, 4).astype(f32)

    arrays = {
        "x": a[A + "x"].reshape(TILES, P, H),
        "l0": cols(*[rows(a[A + n]) for n in ("Wk", "Wv", "Wr", "Wo")],
                   rows(np.concatenate([a[F + "router_w"].T, a[F + "sh_gate_w"]], 1))),
        "vecs": cols(*[a[A + n].reshape(KT, P).T for n in vec_names], earlier),
        "moe": cols(rows(gate_up), rows(down)),
        "l1": cols(rows(wq), rows(wk), rows(a[B + "Wv"].T), rows(a[B + "Wo"].T), rows(ff.reshape(H, -1))),
        "w2": cols(rows(a[G + "W2"].T)),
        "ident": np.eye(P, dtype=f32),
        "had": had,
        "att": cols(negate, np.eye(P, dtype=f32), mask, pick.astype(f32)),
        "bias": cols(bias),
    }
    nc = bacc.Bacc("TRN2", target_bir_lowering=False, num_devices=1)
    args = {}
    feed = {}
    for name, v in arrays.items():
        v = np.ascontiguousarray(v)
        feed[f"in_{name}"] = v
        args[name] = nc.dram_tensor(f"in_{name}", v.shape, F32, kind="ExternalInput").ap()
    args["out"] = nc.dram_tensor("out_0", (TILES, P, H), F32, kind="ExternalOutput").ap()
    build(nc, **args)
    r = run_bass_kernel_spmd(nc, [feed], core_ids=[0])
    return r.results[0]["out_0"].reshape(SEQS, T, H)
```

```python
from contextlib import ExitStack

import concourse.bass as bass
from concourse import mybir
import numpy as np

ALU = mybir.AluOpType
ACT = mybir.ActivationFunctionType
F32 = mybir.dt.float32
F16 = mybir.dt.float16
BF16 = mybir.dt.bfloat16
I32 = mybir.dt.int32
AX_X = mybir.AxisListType.X

P = 128
SEQS, T, H = 16, 256, 256
TOK = SEQS * T
TILES = TOK // P
KT = H // P
LN_EPS = 1e-5
NEG = -1.0e30

GROUP = 4
GTOK = GROUP * P
GROUPS = TILES // GROUP
GSEQ = GTOK // T

E, TOPK = 16, 4
I_MOE, I_SH = 176, 704
SH = I_SH // I_MOE
SLICES = E + SH
EXPERT_BLOCKS = 2
SHARED_BLOCKS = 6
I_FF = 1024
FF_BLOCKS = I_FF // P

HEADS, KV, D = 16, 4, 16
REP = HEADS // KV
SLOT = 32
SCALE = D ** -0.5

CHAINS = 2
CTILES = TILES // CHAINS
BODY = 20
SLOT_TILES = -(-((CTILES * P * TOPK + (P - 1) * E) // P) // BODY) * BODY
LOADS_AHEAD = 5
ROUTE_TILES = SLOT_TILES + 16
C_ROUTE = P + CTILES + ROUTE_TILES

C_TM = 4 * KT * H
C_RT = KT * (E + 1)
C_L0 = C_TM + C_RT
C_GU = KT * SLICES * 2 * I_MOE
C_DN = (E * EXPERT_BLOCKS + SHARED_BLOCKS) * H
C_MOE = C_GU + C_DN
C_Q, C_K, C_V, C_O = KT * REP * P, KT * P, KT * KV * D, REP * H
C_FF = KT * 2 * I_FF
C_L1 = C_Q + C_K + C_V + C_O + C_FF


class Count:

    def __init__(self, sem):
        self.sem = sem

    def start(self, eng):
        eng.sem_inc(self.sem, 2)

    def after(self, n):
        return n + 3


class Steps:

    def __init__(self, sem, names):
        self.sem, self.names = sem, names

    def start(self, eng):
        eng.sem_inc(self.sem, len(self.names))

    def after(self, i, name):
        return (i + 1) * len(self.names) + self.names.index(name) + 1


def hold(eng, sem, value, passed):
    eng.wait_ge(sem, value)
    eng.sem_inc(passed, 1)


def split_matmul(nc, out, stationary, moving, first=True, last=True):
    nc.tensor.matmul(out, stationary[0], moving[0], start=first, stop=False, skip_group_check=True)
    nc.tensor.matmul(out, stationary[1], moving[0], start=False, stop=False, skip_group_check=True)
    return nc.tensor.matmul(out, stationary[0], moving[1], start=False, stop=last, skip_group_check=True)


def load_stage(nc, k):
    with ExitStack() as ctx:
        raw = ctx.enter_context(nc.sbuf_tensor("l0_raw", [P, C_L0], F32))
        vecs = k.vecs
        loaded = ctx.enter_context(nc.semaphore("l0_loaded"))
        x_loaded = ctx.enter_context(nc.semaphore("x_loaded"))
        hi_done = ctx.enter_context(nc.semaphore("l0_hi_done"))
        decay = ctx.enter_context(nc.semaphore("decay_done"))
        vec = ctx.enter_context(nc.semaphore("l0_vec_done"))
        zero = ctx.enter_context(nc.semaphore("l0_zero_done"))
        block = ctx.enter_context(nc.Block())

        @block.sync
        def _(sp):
            sp.dma_start(raw[:, :], k.d_l0).then_inc(loaded, 16)
            sp.dma_start(vecs[:, :], k.d_vecs).then_inc(loaded, 16)
            sp.dma_start(k.ident[:, :], k.d_ident).then_inc(loaded, 16)
            for c in range(4):
                n = TILES // 4
                sp.dma_start(k.x[:, c * n * H:(c + 1) * n * H].rearrange("p (t h) -> p t h", h=H),
                             k.d_x[c * n:(c + 1) * n].rearrange("t p h -> p t h")).then_inc(x_loaded, 16)
            sp.wait_ge(x_loaded, 64)

        @block.scalar
        def _(act):
            act.wait_ge(loaded, 48)
            nc.scalar.activation(k.l0_hi[:, :], raw[:, :], ACT.Identity).then_inc(hi_done, 1)
            nc.scalar.activation(k.decay[:, :], vecs[:, 12:14], ACT.Exp).then_inc(decay, 1)

        @block.gpsimd
        def _(pool):
            nc.gpsimd.memset(k.x[:, TILES * H:], 0.0)
            nc.gpsimd.memset(k.x_all[:, 0:2 * H], 0.0)
            nc.gpsimd.memset(k.eps[:, :], LN_EPS)
            nc.gpsimd.memset(k.wrow[:, :, :], 0.0).then_inc(zero, 1)

        @block.vector
        def _(dve):
            dve.wait_ge(hi_done, 1)
            nc.vector.tensor_tensor(k.l0_lo[:, :], raw[:, :], k.l0_hi[:, :], ALU.subtract).then_inc(vec, 1)
            dve.wait_ge(decay, 1)
            nc.vector.tensor_scalar_mul(k.decay[:, :], k.decay[:, :], -1.0).then_inc(vec, 1)
            dve.wait_ge(vec, 2)
            dve.wait_ge(zero, 1)
            for m in range(KT):
                nc.vector.tensor_scalar_add(k.wrow[:, m, :], k.wrow[:, m, :], k.decay[:, m:m + 1])\
                    .then_inc(vec, 1)


def time_mix_stage(nc, k):
    VEC = ["stats", "mv", "rstd", "xhat", "diff", "mix_k", "mix_v", "mix_r", "p", "q", "t1", "t2", "t3",
           "t4", "c2v", "b", "a", "e1b", "den", "rec", "e1a", "e2v", "num", "gated", "y",
           "res", "stats2", "mv2", "rstd2", "out"]
    SCA = ["std", "xn", "hi_k", "hi_v", "hi_r", "k", "uk", "gate", "e1", "e2", "c1", "c2", "hi_y", "std2"]
    PEN = ["xT", "k", "v", "r", "wo"]
    PARTS = 4
    WCOLS = C_MOE // GROUPS // PARTS
    FILLS = SLOT_TILES // GROUPS // 2
    POL = ["lo_k", "lo_v", "lo_r"] + [w + str(n) for n in range(PARTS) for w in ("w_hi", "w_lo")] + ["lo_y"]
    with ExitStack() as ctx:
        def sb(name, shape, dt=F32):
            return ctx.enter_context(nc.sbuf_tensor("tm_" + name, shape, dt))

        wraw = sb("wraw", [P, WCOLS])
        st = sb("st", [P, GROUP, 6])
        mv = sb("mv", [P, GROUP, 2])
        std = sb("std", [P, GROUP])
        rstd = sb("rstd", [P, GROUP])
        xh = sb("xh", [P, GROUP, H])
        xn = sb("xn", [P, KT, GSEQ, T + 1])
        diff = sb("diff", [P, KT, GSEQ, T])
        mix = [sb(f"mix{j}", [P, KT, GTOK]) for j in range(3)]
        hi = [sb(f"hi{j}", [P, KT, GTOK], F16) for j in range(3)]
        lo = [sb(f"lo{j}", [P, KT, GTOK], F16) for j in range(3)]
        kS, uk, gate = diff, mix[0], mix[1]
        pmax = sb("pmax", [P, KT, GSEQ, T + 1])
        q = mix[2]
        e1, e2, c1, c2 = (sb(n, [P, KT, GSEQ, T]) for n in ("e1", "e2", "c1", "c2"))
        c2v = kS
        asum = sb("asum", [P, KT, GSEQ, T + 1])
        bsum = sb("bsum", [P, KT, GSEQ, T + 1])
        vec = Steps(ctx.enter_context(nc.semaphore("tm_vector_steps")), VEC)
        sca = Steps(ctx.enter_context(nc.semaphore("tm_scalar_steps")), SCA)
        pen = Steps(ctx.enter_context(nc.semaphore("tm_tensor_steps")), PEN)
        pol = Steps(ctx.enter_context(nc.semaphore("tm_pool_steps")), POL)
        w_loaded = ctx.enter_context(nc.semaphore("tm_w_loaded"))
        filled = ctx.enter_context(nc.semaphore("tm_slots_filled"))
        edges = ctx.enter_context(nc.semaphore("tm_edges"))
        passed = ctx.enter_context(nc.semaphore("tm_aggregate_waits"))
        ps = k.ps

        def flat(t):
            return t[:, :, :, :].rearrange("p m s t -> p (m s) t")

        def by_tok(t):
            return t[:, :, :].rearrange("p m (s t) -> p (m s) t", t=T)

        before, now = flat(xn)[:, :, 0:T], flat(xn)[:, :, 1:T + 1]
        p_old, p_new = flat(pmax)[:, :, 0:T], flat(pmax)[:, :, 1:T + 1]
        a_old, b_old = flat(asum)[:, :, 0:T], flat(bsum)[:, :, 0:T]
        k_ps = ps[:, 2:4, :].rearrange("p m (s t) -> p (m s) t", t=T)
        v_ps = ps[:, 4:6, :].rearrange("p m (s t) -> p (m s) t", t=T)
        r_ps = ps[:, 6:8, :].rearrange("p m (s t) -> p (m s) t", t=T)
        uk3, gate3, q3 = by_tok(uk), by_tok(gate), by_tok(q)
        mix_of = [k.vecs[:, 4:6], k.vecs[:, 6:8], k.vecs[:, 8:10]]
        first = k.vecs[:, 10:12]
        block = ctx.enter_context(nc.Block())

        def xs(i, t):
            return k.x[:, bass.ds(i * (GROUP * H) + t * H, H)]

        @block.sync
        def _(sp):
            zeros = k.x[:, TILES * H:].bitcast(F16)
            for c in range(CHAINS):
                for n in range(LOADS_AHEAD):
                    sp.dma_start(k.d_slots[c][(SLOT_TILES + n) * P:(SLOT_TILES + n + 1) * P], zeros[:, 0:2 * H])\
                        .then_inc(filled, 16)
            with sp.Fori(0, GROUPS) as i:
                for n in range(PARTS):
                    sp.wait_ge(pol.sem, pol.after(i if n else i - 1, f"w_lo{(n - 1) % PARTS}"))
                    sp.dma_start(wraw[:, :], k.d_moe[:, bass.ds(i * (PARTS * WCOLS) + n * WCOLS, WCOLS)])\
                        .then_inc(w_loaded, 16)
                    if n == 0:
                        for c in range(CHAINS):
                            for m in range(FILLS):
                                rows = k.d_slots[c][bass.ds(i * (2 * FILLS * P) + m * 2 * P, 2 * P)]
                                sp.dma_start(rows.rearrange("(p r) h -> p (r h)", r=2), zeros)\
                                    .then_inc(filled, 16)
            sp.wait_ge(filled, 16 * CHAINS * (LOADS_AHEAD + GROUPS * FILLS))

        @block.gpsimd
        def _(pool):
            pol.start(pool)
            nc.gpsimd.memset(flat(xn)[:, :, 0:1], 0.0)
            nc.gpsimd.memset(flat(pmax)[:, :, 0:1], NEG)
            nc.gpsimd.memset(flat(asum)[:, :, 0:1], 0.0)
            nc.gpsimd.memset(flat(bsum)[:, :, 0:1], 0.0).then_inc(edges, 1)
            with pool.Fori(0, GROUPS) as i:
                for j, name in enumerate("kvr"):
                    pool.wait_ge(sca.sem, sca.after(i, "hi_" + name))
                    nc.gpsimd.tensor_tensor(lo[j][:, :, :], mix[j][:, :, :], hi[j][:, :, :], ALU.subtract)\
                        .then_inc(pol.sem, 1)
                for n in range(PARTS):
                    pool.wait_ge(w_loaded, i * (16 * PARTS) + (n + 1) * 16)
                    whi, wlo = (w[:, bass.ds(i * (PARTS * WCOLS) + n * WCOLS, WCOLS)] for w in (k.moe_hi, k.moe_lo))
                    nc.gpsimd.tensor_copy(whi, wraw[:, :]).then_inc(pol.sem, 1)
                    pool.wait_ge(pol.sem, pol.after(i, f"w_hi{n}"))
                    nc.gpsimd.tensor_tensor(wlo, wraw[:, :], whi, ALU.subtract).then_inc(pol.sem, 1)
                pool.wait_ge(sca.sem, sca.after(i, "hi_y"))
                nc.gpsimd.tensor_tensor(lo[0][:, :, :], uk[:, :, :], hi[0][:, :, :], ALU.subtract)\
                    .then_inc(pol.sem, 1)

        @block.scalar
        def _(act):
            sca.start(act)
            with act.Fori(0, GROUPS) as i:
                act.wait_ge(vec.sem, vec.after(i, "mv"))
                nc.scalar.activation(std[:, :], mv[:, :, 1], ACT.Sqrt, bias=k.eps[:, 0:1]).then_inc(sca.sem, 1)
                act.wait_ge(pen.sem, pen.after(i, "xT"))
                for m in range(KT):
                    last = nc.scalar.activation(xn[:, m, :, 1:T + 1],
                                                ps[:, m, :].rearrange("p (s t) -> p s t", t=T), ACT.Identity,
                                                scale=k.vecs[:, m:m + 1], bias=k.vecs[:, 2 + m:3 + m])
                last.then_inc(sca.sem, 1)
                for j, name in enumerate("kvr"):
                    act.wait_ge(vec.sem, vec.after(i, "mix_" + name))
                    nc.scalar.activation(hi[j][:, :, :], mix[j][:, :, :], ACT.Copy).then_inc(sca.sem, 1)
                act.wait_ge(pen.sem, pen.after(i, "k"))
                act.wait_ge(vec.sem, vec.after(i, "mix_r"))
                nc.scalar.activation(flat(kS), k_ps, ACT.Copy).then_inc(sca.sem, 1)
                act.wait_ge(pol.sem, pol.after(i, "lo_k"))
                for m in range(KT):
                    last = nc.scalar.activation(uk[:, m, :], ps[:, 2 + m, :], ACT.Identity,
                                                bias=first[:, m:m + 1])
                last.then_inc(sca.sem, 1)
                act.wait_ge(pen.sem, pen.after(i, "r"))
                act.wait_ge(pol.sem, pol.after(i, "lo_v"))
                nc.scalar.activation(gate3, r_ps, ACT.Tanh, scale=0.5).then_inc(sca.sem, 1)
                for name, buf in (("t1", e1), ("t2", e2), ("t3", c1), ("t4", c2)):
                    act.wait_ge(vec.sem, vec.after(i, name))
                    nc.scalar.activation(flat(buf), flat(buf), ACT.Exp).then_inc(sca.sem, 1)
                act.wait_ge(vec.sem, vec.after(i, "y"))
                nc.scalar.activation(hi[0][:, :, :], uk[:, :, :], ACT.Copy).then_inc(sca.sem, 1)
                act.wait_ge(vec.sem, vec.after(i, "mv2"))
                nc.scalar.activation(std[:, :], mv[:, :, 1], ACT.Sqrt, bias=k.eps[:, 0:1]).then_inc(sca.sem, 1)

        @block.vector
        def _(dve):
            vec.start(dve)
            dve.wait_ge(edges, 1)

            def done(i, name):
                dve.wait_ge(vec.sem, vec.after(i, name))

            with dve.Fori(0, GROUPS) as i:
                for t in range(GROUP):
                    last = nc.vector.bn_stats(st[:, t, :], xs(i, t))
                last.then_inc(vec.sem, 1)
                hold(dve, vec.sem, vec.after(i, "stats"), passed)
                for t in range(GROUP):
                    last = nc.vector.bn_aggr(mv[:, t, :], st[:, t, :])
                last.then_inc(vec.sem, 1)
                dve.wait_ge(sca.sem, sca.after(i, "std"))
                nc.vector.reciprocal(rstd[:, :], std[:, :]).then_inc(vec.sem, 1)
                done(i, "rstd")
                for t in range(GROUP):
                    last = nc.vector.tensor_scalar(xh[:, t, :], xs(i, t), mv[:, t, 0:1], rstd[:, t:t + 1],
                                                   ALU.subtract, ALU.mult)
                last.then_inc(vec.sem, 1)
                dve.wait_ge(sca.sem, sca.after(i, "xn"))
                nc.vector.tensor_tensor(flat(diff), now, before, ALU.subtract).then_inc(vec.sem, 1)
                done(i, "diff")
                for j in range(3):
                    for m in range(KT):
                        last = nc.vector.scalar_tensor_tensor(
                            out=mix[j][:, m, :].rearrange("p (s t) -> p s t", t=T), in0=diff[:, m, :, :],
                            scalar=mix_of[j][:, m:m + 1], in1=xn[:, m, :, 0:T], op0=ALU.mult, op1=ALU.add)
                    last.then_inc(vec.sem, 1)
                dve.wait_ge(sca.sem, sca.after(i, "k"))
                for m in range(KT):
                    for s in range(GSEQ):
                        last = nc.vector.tensor_tensor_scan(pmax[:, m, s, 1:T + 1], k.wrow[:, m, :],
                                                            kS[:, m, s, :], NEG, ALU.add, ALU.max)
                last.then_inc(vec.sem, 1)
                done(i, "p")
                dve.wait_ge(sca.sem, sca.after(i, "uk"))
                dve.wait_ge(pol.sem, pol.after(i, "lo_r"))
                nc.vector.tensor_tensor(q3, uk3, p_old, ALU.max).then_inc(vec.sem, 1)
                done(i, "q")
                nc.vector.tensor_tensor(flat(e1), p_old, q3, ALU.subtract).then_inc(vec.sem, 1)
                nc.vector.tensor_tensor(flat(e2), uk3, q3, ALU.subtract).then_inc(vec.sem, 1)
                for m in range(KT):
                    last = nc.vector.scalar_tensor_tensor(
                        out=c1[:, m, :, :], in0=pmax[:, m, :, 0:T], scalar=k.decay[:, m:m + 1],
                        in1=pmax[:, m, :, 1:T + 1], op0=ALU.add, op1=ALU.subtract)
                last.then_inc(vec.sem, 1)
                nc.vector.tensor_tensor(flat(c2), flat(kS), p_new, ALU.subtract).then_inc(vec.sem, 1)
                dve.wait_ge(sca.sem, sca.after(i, "c2"))
                dve.wait_ge(pen.sem, pen.after(i, "v"))
                nc.vector.tensor_tensor(flat(c2v), flat(c2), v_ps, ALU.mult).then_inc(vec.sem, 1)
                for m in range(KT):
                    for s in range(GSEQ):
                        last = nc.vector.tensor_tensor_scan(bsum[:, m, s, 1:T + 1], c1[:, m, s, :],
                                                            c2[:, m, s, :], 0.0, ALU.mult, ALU.add)
                last.then_inc(vec.sem, 1)
                done(i, "c2v")
                for m in range(KT):
                    for s in range(GSEQ):
                        last = nc.vector.tensor_tensor_scan(asum[:, m, s, 1:T + 1], c1[:, m, s, :],
                                                            c2v[:, m, s, :], 0.0, ALU.mult, ALU.add)
                last.then_inc(vec.sem, 1)
                done(i, "a")
                nc.vector.tensor_tensor(flat(c1), flat(e1), b_old, ALU.mult).then_inc(vec.sem, 1)
                done(i, "e1b")
                nc.vector.tensor_tensor(flat(c2), flat(c1), flat(e2), ALU.add).then_inc(vec.sem, 1)
                done(i, "den")
                nc.vector.reciprocal(flat(c1), flat(c2)).then_inc(vec.sem, 1)
                nc.vector.tensor_tensor(flat(c2v), flat(e1), a_old, ALU.mult).then_inc(vec.sem, 1)
                done(i, "rec")
                nc.vector.tensor_tensor(flat(c2), flat(e2), v_ps, ALU.mult).then_inc(vec.sem, 1)
                done(i, "e2v")
                nc.vector.tensor_tensor(flat(e1), flat(c2v), flat(c2), ALU.add).then_inc(vec.sem, 1)
                done(i, "num")
                dve.wait_ge(sca.sem, sca.after(i, "gate"))
                nc.vector.scalar_tensor_tensor(out=flat(e2).rearrange("p a t -> p (a t)"),
                                               in0=gate3.rearrange("p a t -> p (a t)"), scalar=1.0,
                                               in1=flat(e1).rearrange("p a t -> p (a t)"),
                                               op0=ALU.add, op1=ALU.mult).then_inc(vec.sem, 1)
                done(i, "gated")
                nc.vector.scalar_tensor_tensor(out=uk[:, :, :].rearrange("p m t -> p (m t)"),
                                               in0=flat(e2).rearrange("p a t -> p (a t)"), scalar=0.5,
                                               in1=flat(c1).rearrange("p a t -> p (a t)"),
                                               op0=ALU.mult, op1=ALU.mult).then_inc(vec.sem, 1)
                dve.wait_ge(pen.sem, pen.after(i, "wo"))
                for h2 in range(GROUP // 2):
                    last = nc.vector.scalar_tensor_tensor(
                        out=xh[:, 2 * h2:2 * h2 + 2, :].rearrange("p t h -> p (t h)"),
                        in0=k.x[:, bass.ds(i * (GROUP * H) + h2 * 2 * H, 2 * H)], scalar=2.0,
                        in1=ps[:, h2, :], op0=ALU.mult, op1=ALU.add)
                last.then_inc(vec.sem, 1)
                done(i, "res")
                for t in range(GROUP):
                    last = nc.vector.bn_stats(st[:, t, :], xh[:, t, :])
                last.then_inc(vec.sem, 1)
                hold(dve, vec.sem, vec.after(i, "stats2"), passed)
                for t in range(GROUP):
                    last = nc.vector.bn_aggr(mv[:, t, :], st[:, t, :])
                last.then_inc(vec.sem, 1)
                dve.wait_ge(sca.sem, sca.after(i, "std2"))
                nc.vector.reciprocal(rstd[:, :], std[:, :]).then_inc(vec.sem, 1)
                done(i, "rstd2")
                for t in range(GROUP):
                    last = nc.vector.tensor_scalar(xs(i, t), xh[:, t, :], mv[:, t, 0:1], rstd[:, t:t + 1],
                                                   ALU.subtract, ALU.mult)
                last.then_inc(vec.sem, 1)

        @block.tensor
        def _(pe):
            pen.start(pe)
            wt = [[w[:, 0:C_TM].rearrange("p (j m h) -> p j m h", j=4, m=KT) for w in (k.l0_hi, k.l0_lo)]][0]
            with pe.Fori(0, GROUPS) as i:
                pe.wait_ge(vec.sem, vec.after(i, "xhat"))
                for m in range(KT):
                    for t in range(GROUP):
                        last = nc.tensor.transpose(ps[:, m, t * P:(t + 1) * P], xh[:, t, m * P:(m + 1) * P],
                                                   k.ident[:, :])
                last.then_inc(pen.sem, 1)
                for j, name in enumerate("kvr"):
                    pe.wait_ge(pol.sem, pol.after(i, "lo_" + name))
                    for o in range(KT):
                        for m in range(KT):
                            last = split_matmul(nc, ps[:, 2 + 2 * j + o, :],
                                                [w[:, j, m, o * P:(o + 1) * P] for w in wt],
                                                [hi[j][:, m, :], lo[j][:, m, :]], m == 0, m == KT - 1)
                    last.then_inc(pen.sem, 1)
                pe.wait_ge(pol.sem, pol.after(i, "lo_y"))
                for t in range(GROUP):
                    for m in range(KT):
                        last = split_matmul(nc, ps[:, t // 2, (t % 2) * H:(t % 2 + 1) * H],
                                            [y[:, m, t * P:(t + 1) * P] for y in (hi[0], lo[0])],
                                            [w[:, 3, m, :] for w in wt], m == 0, m == KT - 1)
                last.then_inc(pen.sem, 1)


def router_stage(nc, k):
    with ExitStack() as ctx:
        def sb(name, shape, dt=F32):
            return ctx.enter_context(nc.sbuf_tensor("rt_" + name, shape, dt))

        def sem(name):
            return ctx.enter_context(nc.semaphore("rt_" + name))

        xc = sb("xc", [P, GROUP, H])
        xhi = sb("xhi", [P, KT, GTOK], F16)
        xlo = sb("xlo", [P, KT, GTOK], F16)
        logit = sb("logit", [P, TILES, E + 1])
        prob = sb("prob", [P, TILES, E])
        top = sb("top", [P, TILES])
        tot = sb("tot", [P, TILES])
        rec = sb("rec", [P, TILES])
        gate = sb("gate", [P, TILES])
        eight = sb("eight", [P, TILES, 8])
        above, level, order, chosen = (sb(n, [P, TILES, E]) for n in ("above", "level", "order", "chosen"))
        need = sb("need", [P, TILES])
        picked = sb("picked", [P, TILES, E])
        slot_f = sb("slot_f", [P, TILES, TOPK])
        consts = sb("consts", [P, C_ROUTE])
        upper_f, steps, tile_no = consts[:, 0:P], consts[:, P:P + CTILES], consts[:, P + CTILES:]
        upper = sb("upper", [P, P], BF16)
        ones = sb("ones", [P, P], BF16)
        restart = sb("restart", [P, TILES, E])
        mask = sb("mask", [P, CHAINS, E, CTILES], BF16)
        total, upto, place = (sb(n, [P, CHAINS, E, CTILES]) for n in ("total", "upto", "place"))
        tiles_of, tiles_to, first_of = (sb(n, [P, CHAINS, E]) for n in ("tiles_of", "tiles_to", "first_of"))
        begun = sb("begun", [1, CHAINS, ROUTE_TILES, E])
        expert_f = sb("expert_f", [1, CHAINS, ROUTE_TILES])
        loaded, prepared, counted = sem("loaded"), sem("prepared"), sem("counted")
        copied, transposed, hi_done, lo_done, scored, kept = (
            sem(n) for n in ("copied", "transposed", "hi_done", "lo_done", "scored", "kept"))
        chain, exps, masked = sem("vector_chain"), sem("exps"), sem("masked")
        ps = k.ps
        W = E + 1
        wt = [w[:, C_TM:C_L0].rearrange("p (m e) -> p m e", m=KT) for w in (k.l0_hi, k.l0_lo)]
        block = ctx.enter_context(nc.Block())

        @block.sync
        def _(sp):
            sp.dma_start(consts[:, :], k.d_route).then_inc(loaded, 16)

        @block.gpsimd
        def _(pool):
            nc.gpsimd.memset(ones[:, :], 1.0)
            nc.gpsimd.memset(restart[:, :, 1:], 1.0)
            nc.gpsimd.memset(restart[:, :, 0:1], 0.0)
            pool.wait_ge(loaded, 16)
            nc.gpsimd.tensor_copy(upper[:, :], upper_f).then_inc(prepared, 1)
            pool.sem_inc(copied, 1)
            with pool.Fori(0, GROUPS) as i:
                pool.wait_ge(transposed, i + 1)
                nc.gpsimd.tensor_copy(xc[:, :, :].rearrange("p t h -> p (t h)"),
                                      k.x[:, bass.ds(i * GROUP * H, GROUP * H)]).then_inc(copied, 1)

        @block.tensor
        def _(pe):
            pe.sem_inc(transposed, 1)
            pe.sem_inc(scored, 1)
            with pe.Fori(0, GROUPS) as i:
                pe.wait_ge(copied, i + 2)
                pe.wait_ge(lo_done, i + 1)
                for m in range(KT):
                    for t in range(GROUP):
                        last = nc.tensor.transpose(ps[:, m, t * P:(t + 1) * P], xc[:, t, m * P:(m + 1) * P],
                                                   k.ident[:, :])
                last.then_inc(transposed, 1)
                pe.wait_ge(lo_done, i + 2)
                pe.wait_ge(kept, i + 1)
                for t in range(GROUP):
                    for m in range(KT):
                        last = split_matmul(nc, ps[:, 2, t * W:(t + 1) * W],
                                            [a[:, m, t * P:(t + 1) * P] for a in (xhi, xlo)],
                                            [w[:, m, :] for w in wt], m == 0, m == KT - 1)
                last.then_inc(scored, 1)
            pe.wait_ge(prepared, 1)
            pe.wait_ge(masked, 1)
            taken = mask[:, :, :, :].rearrange("p c e t -> p (c e t)")
            nc.tensor.matmul(ps[:, 3, :], upper[:, :], taken, start=True, stop=True)
            nc.tensor.matmul(ps[:, 4, :], ones[:, :], taken, start=True, stop=True).then_inc(counted, 1)

        @block.scalar
        def _(act):
            with act.Fori(0, GROUPS) as i:
                act.wait_ge(transposed, i + 2)
                act.wait_ge(scored, i + 1)
                nc.scalar.activation(xhi[:, :, :], ps[:, 0:2, :], ACT.Copy).then_inc(hi_done, 1)
            act.wait_ge(chain, 2)
            nc.scalar.activation(prob[:, :, :], prob[:, :, :], ACT.Exp).then_inc(exps, 1)
            act.wait_ge(chain, 3)
            nc.scalar.activation(gate[:, :], gate[:, :], ACT.Exp).then_inc(exps, 1)

        @block.vector
        def _(dve):
            dve.sem_inc(lo_done, 1)
            dve.sem_inc(kept, 1)
            with dve.Fori(0, GROUPS) as i:
                dve.wait_ge(hi_done, i + 1)
                nc.vector.tensor_tensor(xlo[:, :, :], ps[:, 0:2, :], xhi[:, :, :], ALU.subtract)\
                    .then_inc(lo_done, 1)
                dve.wait_ge(scored, i + 2)
                nc.vector.tensor_copy(logit[:, :, :].rearrange("p t e -> p (t e)")[:, bass.ds(i * GROUP * W, GROUP * W)],
                                      ps[:, 2, 0:GROUP * W]).then_inc(kept, 1)
            dve.wait_ge(kept, GROUPS + 1)
            links = [0]

            def link(ins):
                ins.then_inc(chain, 1)
                links[0] += 1
                dve.wait_ge(chain, links[0])

            def per_expert(t):
                return t.unsqueeze(2).broadcast_to([P, TILES, E])

            link(nc.vector.tensor_reduce(top[:, :], logit[:, :, 0:E], AX_X, ALU.max))
            link(nc.vector.tensor_tensor(prob[:, :, :], logit[:, :, 0:E], per_expert(top[:, :]), ALU.subtract))
            link(nc.vector.tensor_scalar(gate[:, :], logit[:, :, E], -1.0, 87.0, ALU.mult, ALU.min))
            dve.wait_ge(exps, 1)
            link(nc.vector.tensor_reduce(tot[:, :], prob[:, :, :], AX_X, ALU.add))
            link(nc.vector.reciprocal(rec[:, :], tot[:, :]))
            link(nc.vector.tensor_tensor(prob[:, :, :], prob[:, :, :], per_expert(rec[:, :]), ALU.mult))
            dve.wait_ge(prepared, 1)
            for t in range(TILES):
                last = nc.vector.max(eight[:, t, :], prob[:, t, :])
            link(last)
            fourth = per_expert(eight[:, :, TOPK - 1])
            link(nc.vector.tensor_tensor(above[:, :, :], prob[:, :, :], fourth, ALU.is_gt))
            link(nc.vector.tensor_tensor(level[:, :, :], prob[:, :, :], fourth, ALU.is_equal))
            link(nc.vector.tensor_reduce(need[:, :], above[:, :, :], AX_X, ALU.add))
            link(nc.vector.tensor_scalar(need[:, :], need[:, :], -1.0, float(TOPK), ALU.mult, ALU.add))

            def flat(t):
                return t[:, :, :].rearrange("p t e -> p (t e)")

            def scan(out, begin, values):
                return nc.vector.tensor_tensor_scan(out, begin, values, 0.0, ALU.mult, ALU.add)

            link(scan(flat(order), flat(restart), flat(level)))
            link(nc.vector.tensor_tensor(order[:, :, :], order[:, :, :], per_expert(need[:, :]), ALU.is_le))
            link(nc.vector.tensor_tensor(flat(level), flat(level), flat(order), ALU.mult))
            link(nc.vector.tensor_tensor(flat(chosen), flat(above), flat(level), ALU.add))
            nc.vector.tensor_copy(mask[:, :, :, :].rearrange("p c e t -> p t c e"),
                                  chosen[:, :, :].rearrange("p (t c) e -> p t c e", c=CHAINS)).then_inc(masked, 1)
            link(scan(flat(order), flat(restart), flat(chosen)))
            link(nc.vector.tensor_tensor(flat(order), flat(order), flat(chosen), ALU.mult))
            link(nc.vector.tensor_tensor(flat(above), flat(prob), flat(chosen), ALU.mult))
            link(nc.vector.tensor_reduce(tot[:, :], above[:, :, :], AX_X, ALU.add))
            link(nc.vector.tensor_scalar_max(tot[:, :], tot[:, :], 1e-9))
            link(nc.vector.reciprocal(rec[:, :], tot[:, :]))
            link(nc.vector.tensor_tensor(above[:, :, :], above[:, :, :], per_expert(rec[:, :]), ALU.mult))
            for j in range(TOPK):
                link(nc.vector.scalar_tensor_tensor(out=flat(picked), in0=flat(order), scalar=float(j + 1),
                                                    in1=flat(above), op0=ALU.is_equal, op1=ALU.mult))
                link(nc.vector.tensor_reduce(k.weight[:, 0:TILES, j], picked[:, :, :], AX_X, ALU.add))
            dve.wait_ge(counted, 1)

            def wide(t):
                return t[:, :, :, :].rearrange("p c e t -> p (c e t)")

            link(nc.vector.tensor_copy(wide(total), ps[:, 4, :]))
            link(scan(wide(upto), flat(restart), wide(total)))
            link(nc.vector.tensor_tensor(wide(place), wide(upto), wide(total), ALU.subtract))
            link(nc.vector.tensor_tensor(wide(place), wide(place), ps[:, 3, :], ALU.add))
            count = upto[:, :, :, CTILES - 1].rearrange("p c e -> p (c e)")
            pairs = [P, CHAINS * E, CTILES]
            link(nc.vector.tensor_tensor(total[:, :, :, :].rearrange("p c e t -> p (c e) t"),
                                         count.unsqueeze(2).broadcast_to(pairs),
                                         steps.unsqueeze(1).broadcast_to(pairs), ALU.is_gt))
            link(nc.vector.tensor_reduce(tiles_of[:, :, :].rearrange("p c e -> p (c e)"),
                                         total[:, :, :, :].rearrange("p c e t -> p (c e) t"), AX_X, ALU.add))
            link(scan(flat(tiles_to), restart[:, 0:CHAINS, :].rearrange("p c e -> p (c e)"), flat(tiles_of)))
            link(nc.vector.tensor_tensor(flat(first_of), flat(tiles_to), flat(tiles_of), ALU.subtract))
            link(nc.vector.scalar_tensor_tensor(out=place[:, :, :, :].rearrange("p c e t -> p (c e) t"),
                                                in0=flat(first_of).unsqueeze(2).broadcast_to(pairs),
                                                scalar=float(P),
                                                in1=place[:, :, :, :].rearrange("p c e t -> p (c e) t"),
                                                op0=ALU.mult, op1=ALU.add))
            link(nc.vector.tensor_copy(chosen[:, :, :].rearrange("p (t c) e -> p t c e", c=CHAINS),
                                       place[:, :, :, :].rearrange("p c e t -> p t c e")))
            for j in range(TOPK):
                link(nc.vector.scalar_tensor_tensor(out=flat(picked), in0=flat(order), scalar=float(j + 1),
                                                    in1=flat(chosen), op0=ALU.is_equal, op1=ALU.mult))
                link(nc.vector.tensor_reduce(slot_f[:, :, j], picked[:, :, :], AX_X, ALU.add))
            link(nc.vector.tensor_copy(k.slot[:, 0:TILES, :], slot_f[:, :, :]))
            dims = [1, CHAINS, ROUTE_TILES, E]
            for c in range(CHAINS):
                link(nc.vector.tensor_tensor(begun[:, c, :, :],
                                             first_of[0:1, c, :].unsqueeze(1).broadcast_to([1] + dims[2:]),
                                             tile_no[0:1, :].unsqueeze(2).broadcast_to([1] + dims[2:]), ALU.is_le))
                link(nc.vector.tensor_reduce(expert_f[:, c, :], begun[:, c, :, :], AX_X, ALU.add))
            link(nc.vector.tensor_scalar(expert_f[:, :, :], expert_f[:, :, :], -1.0, 0.0, ALU.add, ALU.max))
            link(nc.vector.tensor_copy(k.expert[:, :].rearrange("p (c t) -> p c t", c=CHAINS), expert_f[:, :, :]))
            dve.wait_ge(exps, 2)
            link(nc.vector.tensor_scalar_add(gate[:, :], gate[:, :], 1.0))
            link(nc.vector.reciprocal(k.gate[:, :], gate[:, :]))


def feed_forward_stage(nc, k, tag, chunks, width, blocks, up, down, unroll, shared=False):
    U, C, NP = unroll, chunks, blocks // 2
    NB = 3
    ITERS = TILES // U
    bank_of = [j % NB for j in range(U * C)]

    def since(j):
        return next(d for d in range(1, U * C + 1) if bank_of[(j - d) % (U * C)] == bank_of[j])

    def covers(p):
        return min(-(-256 * (p + 1) // width), C) - 1

    def last_pair(c):
        return min(((c + 1) * width - 1) // 256, NP - 1)

    transpose_at, down_at = {}, {}
    for u in range(U):
        for p in range(NP):
            j = u * C + covers(p) + 2
            while len(transpose_at.get(j, [])) >= 1 and NP > 4:
                j += 1
            transpose_at.setdefault(j, []).append((u, p))
            down_at.setdefault(j + 2, []).append((u, p))
    ends = {max(j for j, l in down_at.items() if (u, NP - 1) in l) + 1: u for u in range(U)}
    STEPS = max(max(down_at), max(ends)) + 1

    with ExitStack() as ctx:
        def sb(name, shape, dt=F32):
            return ctx.enter_context(nc.sbuf_tensor(tag + name, shape, dt))

        def sem(name):
            return ctx.enter_context(nc.semaphore(tag + name))

        xc = sb("xc", [P, 2, H])
        xhi = sb("xhi", [P, 2, KT * P], F16)
        xlo = sb("xlo", [P, 2, KT * P], F16)
        sil = sb("sil", [P, NB, width])
        hid = sb("hid", [P, blocks * P])
        hhi = sb("hhi", [P, 2, 256], F16)
        hlo = sb("hlo", [P, 2, 256], F16)
        res = sb("res", [P, 2, H])
        st = sb("st", [P, 2, 6])
        mv = sb("mv", [P, 2, 2])
        std = sb("std", [P, 2])
        rstd = sb("rstd", [P, 2])
        copied = sem("copied")
        x_turned = sem("x_turned")
        x_hi = sem("x_hi")
        x_lo = sem("x_lo")
        up_done = sem("up_done")
        sil_done = sem("sil_done")
        hid_done = sem("hid_done")
        turned = sem("turned")
        h_hi = sem("h_hi")
        h_lo = sem("h_lo")
        down_done = sem("down_done")
        summed = sem("summed")
        std_done = sem("std_done")
        chain = sem("norm_chain")
        passed = sem("aggregate_waits")
        zeroed = sem("zeroed")
        stored = sem("stored")
        ps = k.ps
        slots = k.slot[:, :, :].rearrange("p t j -> p (t j)")
        assert U % 2 == 0
        block = ctx.enter_context(nc.Block())

        if shared:
            split = sb("split", [P, U, 2 * H], F16)
            slot = sb("slot", [P, U, TOPK], I32)
            split_hi, scatter_waits = sem("split_hi"), sem("scatter_waits")
            split_lo = sem("split_lo")
            scattered = [sem(f"scattered{c}") for c in range(CHAINS)]
            spread = sem("spread")
            ROUNDS = U // CHAINS
        else:
            @block.sync
            def _(sp):
                with sp.Fori(0, ITERS) as i:
                    for u in range(U):
                        sp.wait_ge(chain, (i * U + u + 1) * 4)
                        sp.dma_start(k.d_out[bass.ds(i * U + u, 1)].rearrange("t p h -> p (t h)"),
                                     k.x[:, bass.ds(i * (U * H) + u * H, H)]).then_inc(stored, 16)
                sp.wait_ge(stored, 16 * TILES)

        @block.gpsimd
        def _(pool):
            if blocks * P > C * width:
                nc.gpsimd.memset(hid[:, C * width:], 0.0).then_inc(zeroed, 1)
            if shared:
                pool.sem_inc(spread, ROUNDS)
            pool.wait_ge(x_turned, 1)
            nc.gpsimd.tensor_copy(xc[:, 0, :], k.x[:, 0:H]).then_inc(copied, 1)

            def scatter(i, q, j):
                for c in range(CHAINS):
                    u = q * CHAINS + c
                    if j == 0:
                        hold(pool, split_lo, i * U + u + 3, scatter_waits)
                    nc.gpsimd.indirect_dma_start(k.d_slots[c],
                                                 bass.IndirectOffsetOnAxis(slot[:, u, j:j + 1], 0),
                                                 split[:, u, :], None).then_inc(scattered[c], 16)
                for c in range(CHAINS):
                    pool.wait_ge(scattered[c], i * (16 * TOPK * ROUNDS) + 16 * (q * TOPK + j + 1))
                    pool.sem_inc(spread if (c, j) == (CHAINS - 1, TOPK - 1) else scatter_waits, 1)

            with pool.Fori(0, ITERS) as i:
                if shared:
                    for q in range(ROUNDS):
                        for j in range(TOPK):
                            scatter(i, q, j)
                else:
                    for u in range(U):
                        pool.wait_ge(x_turned, i * U + u + 1)
                        nc.gpsimd.tensor_copy(xc[:, (u + 1) % 2, :],
                                              k.x[:, bass.ds(i * (U * H) + (u + 1) * H, H)]).then_inc(copied, 1)
        def x_turn(pe, u):
            for m in range(KT):
                last = nc.tensor.transpose(ps[:, 7, m * P:(m + 1) * P], xc[:, u % 2, m * P:(m + 1) * P],
                                           k.ident[:, :])
            last.then_inc(x_turned, 1)

        @block.tensor
        def _(pe):
            pe.sem_inc(x_turned, 1)
            pe.sem_inc(turned, NP)
            pe.sem_inc(down_done, 2)
            if blocks * P > C * width:
                pe.wait_ge(zeroed, 1)
            pe.wait_ge(copied, 1)
            x_turn(pe, 0)
            with pe.Fori(0, ITERS) as i:
                for j in range(STEPS):
                    u, c = j // C, j % C
                    if j < U * C:
                        if c == 0:
                            pe.wait_ge(x_lo, i * U + u + 1)
                        pe.wait_ge(hid_done, i * (U * C) + j + 1 - since(j) + NB)
                        for m in range(KT):
                            last = split_matmul(nc, ps[:, bank_of[j], 0:2 * width],
                                                [a[:, u % 2, m * P:(m + 1) * P] for a in (xhi, xlo)],
                                                [w[:, m, c, :] for w in up], m == 0, m == KT - 1)
                        last.then_inc(up_done, 1)
                        if c == C // 2:
                            pe.wait_ge(copied, i * U + u + 2)
                            x_turn(pe, u + 1)
                    for uu, p in down_at.get(j, []):
                        pe.wait_ge(h_lo, i * (U * NP) + uu * NP + p + 3)
                        if p == 0:
                            pe.wait_ge(summed, i * U + uu + 1)
                        for b in range(2):
                            last = split_matmul(nc, ps[:, 5 + uu % 2, 0:H],
                                                [a[:, p % 2, b * P:(b + 1) * P] for a in (hhi, hlo)],
                                                [w[:, 2 * p + b, :] for w in down],
                                                p == 0 and b == 0, p == NP - 1 and b == 1)
                        last.then_inc(down_done, 1)
                    for uu, p in transpose_at.get(j, []):
                        pe.wait_ge(hid_done, i * (U * C) + uu * C + covers(p) + 1 + NB)
                        pe.wait_ge(h_lo, i * (U * NP) + uu * NP + p + 1)
                        for b in range(2):
                            last = nc.tensor.transpose(ps[:, 3 + p % 2, b * P:(b + 1) * P],
                                                       hid[:, (2 * p + b) * P:(2 * p + b + 1) * P],
                                                       k.ident[:, :])
                        last.then_inc(turned, 1)

        @block.scalar
        def _(act):
            act.wait_ge(x_turned, 2)
            nc.scalar.activation(xhi[:, 0, :], ps[:, 7, 0:H], ACT.Copy).then_inc(x_hi, 1)
            with act.Fori(0, ITERS) as i:
                for j in range(STEPS):
                    u, c = j // C, j % C
                    if shared and j < U * C and c == 1:
                        act.wait_ge(copied, i * U + u + 1)
                        act.wait_ge(spread, i * ROUNDS + u // CHAINS + 1)
                        nc.scalar.activation(split[:, u, 0:H], xc[:, u % 2, :], ACT.Copy).then_inc(split_hi, 1)
                    if j < U * C:
                        act.wait_ge(up_done, i * (U * C) + j + 1)
                        nc.scalar.activation(sil[:, bank_of[j], :], ps[:, bank_of[j], 0:width], ACT.Silu)\
                            .then_inc(sil_done, 1)
                        if c == C // 2:
                            act.wait_ge(x_turned, i * U + u + 3)
                            nc.scalar.activation(xhi[:, (u + 1) % 2, :], ps[:, 7, 0:H], ACT.Copy)\
                                .then_inc(x_hi, 1)
                    for uu, p in transpose_at.get(j, []):
                        act.wait_ge(turned, i * (U * NP) + uu * NP + p + 1 + NP)
                        act.wait_ge(down_done, i * (U * NP) + uu * NP + p + 1)
                        nc.scalar.activation(hhi[:, p % 2, :], ps[:, 3 + p % 2, 0:256], ACT.Copy)\
                            .then_inc(h_hi, 1)
                    if j in ends and not shared:
                        uu = ends[j]
                        act.wait_ge(chain, i * (4 * U) + 4 * uu + 2)
                        nc.scalar.activation(std[:, uu % 2:uu % 2 + 1], mv[:, uu % 2, 1:2], ACT.Sqrt,
                                             bias=k.eps[:, 0:1]).then_inc(std_done, 1)

        @block.vector
        def _(dve):
            dve.sem_inc(hid_done, NB)
            dve.sem_inc(h_lo, 2)
            dve.sem_inc(summed, 2)
            if shared:
                dve.sem_inc(split_lo, 2)
            dve.wait_ge(x_hi, 1)
            nc.vector.tensor_tensor(xlo[:, 0, :], ps[:, 7, 0:H], xhi[:, 0, :], ALU.subtract).then_inc(x_lo, 1)
            with dve.Fori(0, ITERS) as i:
                for j in range(STEPS):
                    u, c = j // C, j % C
                    if shared and j < U * C and c == 1:
                        dve.wait_ge(split_hi, i * U + u + 1)
                        nc.vector.tensor_tensor(split[:, u, H:2 * H], xc[:, u % 2, :], split[:, u, 0:H], ALU.subtract)
                        nc.vector.tensor_copy(slot[:, u, :],
                                              slots[:, bass.ds(i * (U * TOPK) + u * TOPK, TOPK)])\
                            .then_inc(split_lo, 1)
                        dve.wait_ge(x_turned, i * U + u + 1)
                        dve.wait_ge(split_lo, i * U + u + 2)
                        nc.vector.tensor_copy(xc[:, (u + 1) % 2, :],
                                              k.x[:, bass.ds(i * (U * H) + (u + 1) * H, H)]).then_inc(copied, 1)
                    if j < U * C:
                        dve.wait_ge(sil_done, i * (U * C) + j + 1)
                        dve.wait_ge(turned, i * (U * NP) + u * NP + last_pair(c) + 1)
                        out = hid[:, c * width:(c + 1) * width]
                        upper = ps[:, bank_of[j], width:2 * width]
                        if not shared:
                            nc.vector.tensor_tensor(out, sil[:, bank_of[j], :], upper, ALU.mult)\
                                .then_inc(hid_done, 1)
                        else:
                            nc.vector.scalar_tensor_tensor(
                                out=out, in0=sil[:, bank_of[j], :],
                                scalar=k.gate[:, bass.ds(i * U + u, 1)], in1=upper,
                                op0=ALU.mult, op1=ALU.mult).then_inc(hid_done, 1)
                        if c == C // 2:
                            dve.wait_ge(x_hi, i * U + u + 2)
                            nc.vector.tensor_tensor(xlo[:, (u + 1) % 2, :], ps[:, 7, 0:H],
                                                    xhi[:, (u + 1) % 2, :], ALU.subtract).then_inc(x_lo, 1)
                    for uu, p in transpose_at.get(j, []):
                        dve.wait_ge(h_hi, i * (U * NP) + uu * NP + p + 1)
                        nc.vector.tensor_tensor(hlo[:, p % 2, :], ps[:, 3 + p % 2, 0:256], hhi[:, p % 2, :],
                                                ALU.subtract).then_inc(h_lo, 1)
                    if j in ends:
                        uu = ends[j]
                        s = uu % 2
                        mine = k.x[:, bass.ds(i * (U * H) + uu * H, H)]
                        dve.wait_ge(down_done, i * (U * NP) + (uu + 1) * NP + 2)
                        if shared:
                            nc.vector.tensor_tensor(mine, ps[:, 5 + s, 0:H], mine, ALU.add).then_inc(summed, 1)
                            continue
                        nc.vector.tensor_tensor(res[:, s, :], ps[:, 5 + s, 0:H], mine, ALU.add)\
                            .then_inc(summed, 1)
                        dve.wait_ge(summed, i * U + uu + 3)
                        nc.vector.bn_stats(st[:, s, :], res[:, s, :]).then_inc(chain, 1)
                        hold(dve, chain, i * (4 * U) + 4 * uu + 1, passed)
                        nc.vector.bn_aggr(mv[:, s, :], st[:, s, :]).then_inc(chain, 1)
                        dve.wait_ge(std_done, i * U + uu + 1)
                        nc.vector.reciprocal(rstd[:, s:s + 1], std[:, s:s + 1]).then_inc(chain, 1)
                        dve.wait_ge(chain, i * (4 * U) + 4 * uu + 3)
                        nc.vector.tensor_scalar(mine, res[:, s, :], mv[:, s, 0:1], rstd[:, s:s + 1],
                                                ALU.subtract, ALU.mult).then_inc(chain, 1)


def expert_stage(nc, k, tag, chain=None, combine=None):
    ITERS = SLOT_TILES // BODY
    RING = LOADS_AHEAD
    PART = BODY // 2
    PARTS = SLOT_TILES // PART
    PER = CTILES // PARTS
    MIX = [f"mix{s}{j}" for s in range(PER) for j in range(TOPK)]
    MIX_AT, STATS_AT, SQRT_AT, OUT_AT = {0: (0, 0), 1: (0, 2), 2: (1, 0), 3: (1, 2)}, 4, 6, 8
    assert BODY % RING == 0 and BODY % 2 == 0 and CTILES % PARTS == 0

    with ExitStack() as ctx:
        def sb(name, shape, dt=F32):
            return ctx.enter_context(nc.sbuf_tensor(tag + name, shape, dt))

        def sem(name):
            return ctx.enter_context(nc.semaphore(tag + name))

        ps = k.ps
        if chain is not None:
            xs = sb("xs", [P, RING, 2 * H], F16)
            xt = sb("xt", [P, 2, 2, KT, P], F16)
            ident = sb("ident", [P, P], F16)
            sil = sb("sil", [P, 2, I_MOE])
            hid = sb("hid", [P, 2, EXPERT_BLOCKS * P])
            hhi = sb("hhi", [P, 2, EXPERT_BLOCKS * P], F16)
            hlo = sb("hlo", [P, 2, EXPERT_BLOCKS * P], F16)
            y = sb("y", [P, RING, H])
            loaded = [sem(f"loaded{r}") for r in range(RING)]
            stored = [sem(f"stored{r}") for r in range(RING)]
            prepared = sem("prepared")
            x_turned, x_copied, up_done, sil_done, hid_done, turned, h_hi, h_lo, down_done, y_done = (
                Count(sem(n)) for n in ("x_turned", "x_copied", "up_done", "sil_done", "hid_done", "turned",
                                        "h_hi", "h_lo", "down_done", "y_done"))
            prep = Layer1Split(nc, ctx, k, PARTS) if chain == 0 else None
        if combine is not None:
            got = sb("got", [P, PER, TOPK * H])
            slot = sb("slot", [P, PER, TOPK], I32)
            res = sb("res", [P, PER, H])
            st = sb("st", [P, PER, 6])
            mv = sb("mv", [P, PER, 2])
            std = sb("std", [P, PER])
            rstd = sb("rstd", [P, PER])
            gathered = [sem(f"gathered{s}") for s in range(PER)]
            slots_here, gather_waits = sem("slots_here"), sem("gather_waits")
            mix = Steps(sem("mix_steps"), MIX + ["stats", "mv", "rstd", "out"])
            root = Steps(sem("root_steps"), ["std"])
            passed = sem("aggregate_waits")
        block = ctx.enter_context(nc.Block())

        def wait(eng, count, n):
            eng.wait_ge(count.sem, count.after(n))

        if chain is not None:
            @block.sync
            def _(sp):
                def load(n, r):
                    sp.dma_start(xs[:, r, :], k.d_slots[chain][bass.ds(n * P, P)]).then_inc(loaded[r], 16)

                for r in range(RING):
                    load(r, r)
                with sp.Fori(0, ITERS) as i:
                    for s in range(BODY):
                        n, r = i * BODY + s, s % RING
                        if prep and s % PART == 0:
                            prep.load(sp, i * 2 + s // PART)
                        wait(sp, x_turned, n)
                        load(n + RING, r)
                        wait(sp, y_done, n)
                        sp.dma_start(k.d_y[chain][bass.ds(n * P, P)], y[:, r, :]).then_inc(stored[r], 16)
                for r in range(RING):
                    sp.wait_ge(stored[r], 16 * (SLOT_TILES // RING + 1))
                    sp.wait_ge(loaded[r], 16 * (SLOT_TILES // RING + 1))

            @block.tensor
            def _(pe):
                def load_experts(first, count):
                    row = k.expert[0:1, bass.ds(first + chain * ROUTE_TILES, count)]
                    return nc.values_load_multi_w_load_instructions(row, engines=[mybir.EngineType.PE],
                                                                    min_val=0, max_val=E - 1)[1]

                def turn_x(n, r, turn, par):
                    pe.wait_ge(loaded[r], turn)
                    wait(pe, x_copied, n - 2)
                    for h in range(2):
                        for m in range(KT):
                            last = nc.tensor.matmul(ps[:, par, (h * KT + m) * P:(h * KT + m + 1) * P],
                                                    xs[:, r, h * H + m * P:h * H + (m + 1) * P], ident[:, :],
                                                    start=True, stop=True, skip_group_check=True)
                    last.then_inc(x_turned.sem, 1)

                def gate_up(n, par, expert):
                    wait(pe, x_copied, n)
                    wait(pe, hid_done, n - 2)
                    for m in range(KT):
                        cols = bass.ds(expert * (2 * I_MOE) + m * (SLICES * 2 * I_MOE), 2 * I_MOE)
                        last = split_matmul(nc, ps[:, 2 + par, 0:2 * I_MOE], [xt[:, par, h, m, :] for h in range(2)],
                                            [w[:, cols] for w in (k.moe_hi, k.moe_lo)], m == 0, m == KT - 1)
                    last.then_inc(up_done.sem, 1)

                def turn_hidden(n, par):
                    wait(pe, hid_done, n)
                    wait(pe, h_lo, n - 2)
                    for b in range(EXPERT_BLOCKS):
                        last = nc.tensor.transpose(ps[:, 4 + par, b * P:(b + 1) * P],
                                                   hid[:, par, b * P:(b + 1) * P], k.ident[:, :])
                    last.then_inc(turned.sem, 1)

                def multiply_down(n, par, expert):
                    wait(pe, h_lo, n)
                    wait(pe, y_done, n - 2)
                    for b in range(EXPERT_BLOCKS):
                        cols = bass.ds(expert * (EXPERT_BLOCKS * H) + C_GU + b * H, H)
                        last = split_matmul(nc, ps[:, 6 + par, 0:H],
                                            [a[:, par, b * P:(b + 1) * P] for a in (hhi, hlo)],
                                            [w[:, cols] for w in (k.moe_hi, k.moe_lo)], b == 0,
                                            b == EXPERT_BLOCKS - 1)
                    last.then_inc(down_done.sem, 1)

                for c in (x_turned, up_done, turned, down_done):
                    c.start(pe)
                pe.wait_ge(prepared, 1)
                begin = load_experts(0, 2)
                turn_x(0, 0, 16, 0)
                turn_x(1, 1, 16, 1)
                gate_up(0, 0, begin[0])
                turn_x(2, 2, 16, 0)
                gate_up(1, 1, begin[1])
                turn_hidden(0, 0)
                with pe.Fori(0, ITERS) as i:
                    experts = list(load_experts(i * BODY, 2))
                    for s in range(BODY):
                        n = i * BODY + s
                        experts += load_experts(n + 2, 1)
                        turn_x(n + 3, (s + 3) % RING, i * (16 * BODY // RING) + 16 * ((s + 3) // RING + 1),
                               (s + 3) % 2)
                        gate_up(n + 2, s % 2, experts[s + 2])
                        turn_hidden(n + 1, (s + 1) % 2)
                        multiply_down(n, s % 2, experts[s])

        @block.gpsimd
        def _(pool):
            if chain is not None:
                nc.gpsimd.memset(hid[:, :, I_MOE:], 0.0)
                nc.gpsimd.tensor_copy(ident[:, :], k.ident[:, :]).then_inc(prepared, 1)
                if prep:
                    prep.start(pool)
            with pool.Fori(0, PARTS) as i:
                if combine is not None:
                    for s in range(PER):
                        at = i * (PER * CHAINS * TOPK) + (s * CHAINS + combine) * TOPK
                        pool.wait_ge(mix.sem, mix.after(i - 1, f"mix{s}{TOPK - 1}"))
                        nc.gpsimd.tensor_copy(slot[:, s, :],
                                              k.slot[:, :, :].rearrange("p t j -> p (t j)")[:, bass.ds(at, TOPK)])\
                            .then_inc(slots_here, 1)
                        hold(pool, slots_here, i * PER + s + 1, gather_waits)
                        for j in range(TOPK):
                            nc.gpsimd.indirect_dma_start(got[:, s, j * H:(j + 1) * H], None, k.d_y[combine],
                                                         bass.IndirectOffsetOnAxis(slot[:, s, j:j + 1], 0))\
                                .then_inc(gathered[s], 16)
                if chain is not None and prep:
                    prep.split(pool, i)

        @block.scalar
        def _(act):
            def copy_x(n, par):
                wait(act, x_turned, n)
                wait(act, up_done, n - 2)
                nc.scalar.activation(xt[:, par, :, :, :].rearrange("p a m t -> p (a m t)"), ps[:, par, :],
                                     ACT.Copy).then_inc(x_copied.sem, 1)

            def silu(n, par):
                wait(act, up_done, n)
                wait(act, hid_done, n - 2)
                nc.scalar.activation(sil[:, par, :], ps[:, 2 + par, 0:I_MOE], ACT.Silu).then_inc(sil_done.sem, 1)

            def split_hi(n, par):
                wait(act, turned, n)
                wait(act, down_done, n - 2)
                nc.scalar.activation(hhi[:, par, :], ps[:, 4 + par, 0:EXPERT_BLOCKS * P], ACT.Copy)\
                    .then_inc(h_hi.sem, 1)

            if chain is not None:
                for c in (x_copied, sil_done, h_hi):
                    c.start(act)
                copy_x(0, 0)
                copy_x(1, 1)
                silu(0, 0)
                copy_x(2, 0)
                silu(1, 1)
                split_hi(0, 0)
            if combine is not None:
                root.start(act)
            with act.Fori(0, ITERS) as i:
                for s in range(BODY):
                    n = i * BODY + s
                    if chain is not None:
                        silu(n + 2, s % 2)
                        copy_x(n + 3, (s + 3) % 2)
                        split_hi(n + 1, (s + 1) % 2)
                    if combine is not None and s % PART == SQRT_AT:
                        act.wait_ge(mix.sem, mix.after(i * 2 + s // PART, "mv"))
                        nc.scalar.activation(std[:, :], mv[:, :, 1], ACT.Sqrt, bias=k.eps[:, 0:1])\
                            .then_inc(root.sem, 1)

        @block.vector
        def _(dve):
            def hidden(n, par):
                wait(dve, sil_done, n)
                wait(dve, turned, n - 2)
                nc.vector.tensor_tensor(hid[:, par, 0:I_MOE], sil[:, par, :], ps[:, 2 + par, I_MOE:2 * I_MOE],
                                        ALU.mult).then_inc(hid_done.sem, 1)

            def split_lo(n, par):
                wait(dve, h_hi, n)
                nc.vector.tensor_tensor(hlo[:, par, :], ps[:, 4 + par, 0:EXPERT_BLOCKS * P], hhi[:, par, :],
                                        ALU.subtract).then_inc(h_lo.sem, 1)

            def keep(n, par, r, turn):
                wait(dve, down_done, n)
                dve.wait_ge(stored[r], turn)
                nc.vector.tensor_copy(y[:, r, :], ps[:, 6 + par, 0:H]).then_inc(y_done.sem, 1)

            if chain is not None:
                for c in (hid_done, h_lo, y_done):
                    c.start(dve)
                for r in range(RING):
                    dve.sem_inc(stored[r], 16)
                hidden(0, 0)
                hidden(1, 1)
                split_lo(0, 0)
            if combine is not None:
                mix.start(dve)

            def tile_of(i, s):
                return k.x[:, bass.ds(i * (PER * CHAINS * H) + (s * CHAINS + combine) * H, H)]

            def combine_step(i, s):
                if s in MIX_AT:
                    t, first = MIX_AT[s]
                    for j in range(first, first + 2):
                        if j == 0:
                            dve.wait_ge(gathered[t], i * (16 * TOPK) + 16 * TOPK)
                            dve.wait_ge(mix.sem, mix.after(i - 1, "out"))
                        else:
                            dve.wait_ge(mix.sem, mix.after(i, f"mix{t}{j - 1}"))
                        at = i * (PER * CHAINS * TOPK) + (t * CHAINS + combine) * TOPK + j
                        nc.vector.scalar_tensor_tensor(
                            out=res[:, t, :], in0=got[:, t, j * H:(j + 1) * H],
                            scalar=k.weight[:, :, :].rearrange("p t j -> p (t j)")[:, bass.ds(at, 1)],
                            in1=tile_of(i, t) if j == 0 else res[:, t, :], op0=ALU.mult, op1=ALU.add)\
                            .then_inc(mix.sem, 1)
                if s == STATS_AT:
                    dve.wait_ge(mix.sem, mix.after(i, MIX[-1]))
                    for t in range(PER):
                        last = nc.vector.bn_stats(st[:, t, :], res[:, t, :])
                    last.then_inc(mix.sem, 1)
                    hold(dve, mix.sem, mix.after(i, "stats"), passed)
                    for t in range(PER):
                        last = nc.vector.bn_aggr(mv[:, t, :], st[:, t, :])
                    last.then_inc(mix.sem, 1)
                if s == OUT_AT:
                    dve.wait_ge(root.sem, root.after(i, "std"))
                    nc.vector.reciprocal(rstd[:, :], std[:, :]).then_inc(mix.sem, 1)
                    dve.wait_ge(mix.sem, mix.after(i, "rstd"))
                    for t in range(PER):
                        last = nc.vector.tensor_scalar(tile_of(i, t), res[:, t, :], mv[:, t, 0:1],
                                                       rstd[:, t:t + 1], ALU.subtract, ALU.mult)
                    last.then_inc(mix.sem, 1)

            with dve.Fori(0, ITERS) as i:
                for s in range(BODY):
                    n, r = i * BODY + s, s % RING
                    if chain is not None:
                        hidden(n + 2, s % 2)
                        split_lo(n + 1, (s + 1) % 2)
                        keep(n, s % 2, r, i * (16 * BODY // RING) + 16 * (s // RING + 1))
                    if combine is not None:
                        combine_step(i * 2 + s // PART, s % PART)


class Layer1Split:

    def __init__(self, nc, ctx, k, parts):
        self.nc, self.k, self.n = nc, k, C_L1 // parts
        assert C_L1 % parts == 0
        self.raw = ctx.enter_context(nc.sbuf_tensor("l1_raw", [P, self.n], F32))
        self.loaded = ctx.enter_context(nc.semaphore("l1_loaded"))
        self.hi_done = ctx.enter_context(nc.semaphore("l1_hi_done"))
        self.lo_done = ctx.enter_context(nc.semaphore("l1_lo_done"))

    def start(self, pool):
        pool.sem_inc(self.lo_done, 1)

    def load(self, sp, i):
        sp.wait_ge(self.lo_done, i + 1)
        sp.dma_start(self.raw[:, :], self.k.d_l1[:, bass.ds(i * self.n, self.n)]).then_inc(self.loaded, 16)

    def split(self, pool, i):
        nc, k = self.nc, self.k
        hi = k.l1_hi[:, bass.ds(i * self.n, self.n)]
        pool.wait_ge(self.loaded, (i + 1) * 16)
        nc.gpsimd.tensor_copy(hi, self.raw[:, :]).then_inc(self.hi_done, 1)
        pool.wait_ge(self.hi_done, i + 1)
        nc.gpsimd.tensor_tensor(k.l1_lo[:, bass.ds(i * self.n, self.n)], self.raw[:, :], hi, ALU.subtract)\
            .then_inc(self.lo_done, 1)


def hadamard_stage(nc, k):
    with ExitStack() as ctx:
        def sb(name, shape, dt=F32):
            return ctx.enter_context(nc.sbuf_tensor("hd_" + name, shape, dt))

        def sem(name):
            return ctx.enter_context(nc.semaphore("hd_" + name))

        raw = sb("raw", [P, FF_BLOCKS, H])
        had = sb("had", [P, P])
        a = sb("a", [P, FF_BLOCKS, H])
        b = sb("b", [P, FF_BLOCKS, H])
        loaded, multiplied, chain, hi_done = sem("loaded"), sem("multiplied"), sem("chain"), sem("hi_done")
        block = ctx.enter_context(nc.Block())

        @block.sync
        def _(sp):
            sp.dma_start(had[:, :], k.d_had).then_inc(loaded, 16)
            sp.dma_start(raw[:, :, :], k.d_w2).then_inc(loaded, 16)
            sp.dma_start(k.att_const[:, :], k.d_att).then_inc(loaded, 16)
            sp.wait_ge(loaded, 48)

        @block.tensor
        def _(pe):
            pe.wait_ge(loaded, 48)
            for c in range(FF_BLOCKS):
                last = nc.tensor.matmul(k.ps[:, c // 2, (c % 2) * H:(c % 2 + 1) * H], had[:, :], raw[:, c, :],
                                        start=True, stop=True)
            last.then_inc(multiplied, 1)

        @block.vector
        def _(dve):
            dve.wait_ge(multiplied, 1)
            nc.vector.tensor_copy(a[:, :, :].rearrange("p c h -> p (c h)"),
                                  k.ps[:, 0:4, :].rearrange("p b n -> p (b n)")).then_inc(chain, 1)
            src, dst, n = a, b, 1
            for span in (1, 2, 4):
                dve.wait_ge(chain, n)
                v, w = (t[:, :, :].rearrange("p (x two s) h -> p two x (s h)", two=2, s=span) for t in (src, dst))
                nc.vector.tensor_tensor(w[:, 0], v[:, 0], v[:, 1], ALU.add).then_inc(chain, 1)
                nc.vector.tensor_tensor(w[:, 1], v[:, 0], v[:, 1], ALU.subtract).then_inc(chain, 1)
                src, dst, n = dst, src, n + 2
            dve.wait_ge(chain, n)
            nc.vector.tensor_scalar_mul(dst[:, :, :], src[:, :, :], I_FF ** -0.5).then_inc(chain, 1)
            dve.wait_ge(chain, n + 1)
            nc.vector.tensor_copy(k.w2_hi[:, :, :], dst[:, :, :]).then_inc(hi_done, 1)
            dve.wait_ge(hi_done, 1)
            nc.vector.tensor_tensor(k.w2_lo[:, :, :], dst[:, :, :], k.w2_hi[:, :, :], ALU.subtract)\
                .then_inc(chain, 1)


def attention_stage(nc, k):
    AU = 4
    PV = [(t, kt) for t in range(2) for kt in range(t + 1)]
    UNITS = [(t, g, kt) for t, kt in PV for g in range(KV)]
    NU, RING_E, RING_P = len(UNITS), 3, 2 * KV
    NAT = [(0, g, 0, REP) for g in range(KV)] + [(1, g, r, 2) for g in range(KV) for r in (0, 2)]
    NN = len(NAT)
    LAG = 2
    SLOTS = NU + LAG
    pv_at = {v: [p for p in range(len(PV)) if KV * p + KV - 1 == v - LAG] for v in range(SLOTS)}
    A_AT = {0: ["x"], 2: ["qkv"], 10: ["top"]}
    for u in range(NN):
        A_AT.setdefault(3 + u // 2, []).append(u)
    C_AT = {0: ["o"], 3: ["wo"]}
    NORM_AT, SQRT_AT, OUT_AT = 6, 8, 10
    V1 = 2 * D

    with ExitStack() as ctx:
        def sb(name, shape, dt=F32):
            return ctx.enter_context(nc.sbuf_tensor("at_" + name, shape, dt))

        def sem(name):
            return ctx.enter_context(nc.semaphore("at_" + name))

        free = FF_BLOCKS * H
        bias_flat = k.moe_hi[:, free:free + 4 * HEADS * P].bitcast(F32)
        bias = bias_flat.rearrange("p (g y r n) -> p g y r n", g=KV, y=2, r=REP)
        cst = sb("cst", [P, 2 * P], BF16)
        eye, mask = cst[:, 0:P], cst[:, P:2 * P]
        negate = k.att_const[:, 0:1]
        xc = sb("xc", [P, 2 * H])
        xhi = sb("xhi", [P, KT, T], F16)
        xlo = sb("xlo", [P, KT, T], F16)
        qh = sb("qh", [P, REP, T], F16)
        q_ = sb("q", [P, 2, REP, T], F16)
        v1_ = sb("v1", [P, 2, 2, KV, V1])
        top = sb("top", [P, 2, KV, SLOT])
        shift_ = sb("shift", [P, 2, 2 * P], BF16)
        taken = [free + 4 * HEADS * P, free]

        def there(which, dt, *dims):
            size = int(np.prod(dims)) * (2 if dt == F32 else 1)
            whole = (k.moe_hi, k.moe_lo)[which][:, taken[which]:taken[which] + size]
            taken[which] += size
            names = " ".join("abcd"[:len(dims)])
            return whole.bitcast(dt).rearrange(f"p ({names}) -> p {names}", **dict(zip("abcd", dims)))

        ex = there(1, F32, RING_E, REP * P)
        pr = there(1, F32, RING_P, REP * P)
        kh_, kl_ = (there(0, F16, 2, KV, T) for _ in range(2))
        pick = there(0, BF16, KV, REP, P)
        rec = sb("rec", [P, 2, REP * P])
        o = sb("o", [P, 2, REP * P])
        ohi = sb("ohi", [P, 2, REP, P], F16)
        olo = sb("olo", [P, 2, REP, P], F16)
        res = sb("res", [P, AU, 2 * H])
        st = sb("st", [P, 2 * AU, 6])
        mv = sb("mv", [P, 2 * AU, 2])
        std = sb("std", [P, 2 * AU])
        rstd = sb("rstd", [P, 2 * AU])
        nat_names, unit_names = [f"max{u}" for u in range(NN)], [f"unit{v}" for v in range(NU)]
        a_vec = Steps(sem("a_vector_steps"), ["xlo", "q", "klo"] + nat_names)
        a_sca = Steps(sem("a_scalar_steps"), ["xhi", "qhi", "khi", "v", "shift"])
        a_pen = Steps(sem("a_tensor_steps"), ["xT", "q", "kv"] + nat_names + ["maxT"])
        a_pol = Steps(sem("a_pool_steps"), ["copy"])
        scores = Steps(sem("b_scores"), unit_names)
        exps = Steps(sem("b_exps"), unit_names)
        probs = Steps(sem("b_probs"), unit_names)
        pvs = Steps(sem("b_pv"), [f"pv{n}" for n in range(len(PV))])
        c_vec = Steps(sem("c_vector_steps"), ["sum", "rec", "o", "res", "stats"])
        c_sca = Steps(sem("c_scalar_steps"), ["ohi"])
        c_pol = Steps(sem("c_pool_steps"), ["olo"])
        c_pen = Steps(sem("c_tensor_steps"), ["wo"])
        norm_vec = Steps(sem("norm_vector_steps"), ["mv", "rstd", "out"])
        norm_sca = Steps(sem("norm_scalar_steps"), ["std"])
        loaded, ready, passed = sem("bias_loaded"), sem("constants_ready"), sem("aggregate_waits")
        cleared = sem("constants_cleared")
        ps = k.ps
        at = [0]
        w = []
        for n, dims in ((C_Q, (REP, P)), (C_K, (1, P)), (C_V, (1, KV * D)), (C_O, (REP, H))):
            w.append([s[:, at[0]:at[0] + n].rearrange("p (m r n) -> p m r n", r=dims[0], n=dims[1])
                      for s in (k.l1_hi, k.l1_lo)])
            at[0] += n
        wq, wk, wv, wo = w
        block = ctx.enter_context(nc.Block())

        def slot(g):
            return slice(SLOT * g, SLOT * (g + 1))

        def wait(eng, steps, n, name):
            eng.wait_ge(steps.sem, steps.after(n, name))

        @block.sync
        def _(sp):
            sp.dma_start(bias_flat, k.d_bias).then_inc(loaded, 16)

        @block.gpsimd
        def _(pool):
            for s in (a_pol, probs, c_pol):
                s.start(pool)
            nc.gpsimd.memset(top[:, :, :, :], 0.0)
            nc.gpsimd.memset(v1_[:, :, :, :, D:V1], 1.0)
            for t in (kh_, kl_):
                nc.gpsimd.memset(t, 0.0)
            nc.gpsimd.memset(pick, 0.0).then_inc(cleared, 1)
            for g in range(KV):
                pool.wait_ge(cleared, g + 1)
                nc.gpsimd.tensor_copy(pick[slot(g), g, :, :],
                                      k.att_const[slot(g), 1 + 2 * P:].rearrange("p (r n) -> p r n", r=REP))\
                    .then_inc(cleared, 1)
            pool.wait_ge(cleared, KV + 1)
            nc.gpsimd.tensor_copy(cst[:, :], k.att_const[:, 1:1 + 2 * P]).then_inc(ready, 1)

            def phase_a(n):
                wait(pool, a_pen, n - 1, "xT")
                nc.gpsimd.tensor_copy(xc[:, :], k.x[:, bass.ds(n * (2 * H), 2 * H)]).then_inc(a_pol.sem, 1)

            def phase_c(n):
                wait(pool, c_sca, n, "ohi")
                nc.gpsimd.tensor_tensor(olo[:, :, :, :].rearrange("p t r n -> p (t r n)"),
                                        o[:, :, :].rearrange("p t n -> p (t n)"),
                                        ohi[:, :, :, :].rearrange("p t r n -> p (t r n)"), ALU.subtract)\
                    .then_inc(c_pol.sem, 1)

            phase_a(0)
            pool.wait_ge(loaded, 16)
            with pool.Fori(0, SEQS // AU) as i:
                for s in range(AU):
                    n = i * AU + s
                    for v, (t, g, kt) in enumerate(UNITS):
                        wait(pool, exps, n, f"unit{v}")
                        wait(pool, pvs, n if v >= RING_P else n - 1, f"pv{len(PV) - 1 - v // KV}")
                        nc.gpsimd.tensor_tensor(pr[:, v % RING_P, :], ex[:, v % RING_E, :],
                                                bias[:, g, t - kt, :, :].rearrange("p r n -> p (r n)"), ALU.mult)\
                            .then_inc(probs.sem, 1)
                        if v == 0:
                            phase_a(n + 1)
                        if v == 1:
                            phase_c(n)
            phase_c(SEQS)

        @block.tensor
        def _(pe):
            for s in (a_pen, scores, pvs, c_pen):
                s.start(pe)
            pe.wait_ge(ready, 1)

            def phase_a(step, n, par):
                q, kh = q_[:, par], kh_[:, par]
                if step == "x":
                    wait(pe, a_pol, n, "copy")
                    wait(pe, a_sca, n - 1, "shift")
                    for m in range(KT):
                        for t in range(2):
                            last = nc.tensor.transpose(ps[:, 0, m * T + t * P:m * T + (t + 1) * P],
                                                       xc[:, t * H + m * P:t * H + (m + 1) * P], k.ident[:, :])
                    last.then_inc(a_pen.sem, 1)
                elif step == "qkv":
                    wait(pe, a_vec, n, "xlo")
                    wait(pe, a_vec, n - 1, f"max{NN - 1}")
                    for r in range(REP):
                        for m in range(KT):
                            last = split_matmul(nc, ps[:, 1 + r // 2, (r % 2) * T:(r % 2 + 1) * T],
                                                [s[:, m, r, :] for s in wq], [s[:, m, :] for s in (xhi, xlo)],
                                                m == 0, m == KT - 1)
                    last.then_inc(a_pen.sem, 1)
                    for m in range(KT):
                        split_matmul(nc, ps[:, 0, 0:T], [s[:, m, 0, :] for s in wk],
                                     [s[:, m, :] for s in (xhi, xlo)], m == 0, m == KT - 1)
                    for t in range(2):
                        for m in range(KT):
                            last = split_matmul(nc, ps[:, 0, T + t * KV * D:T + (t + 1) * KV * D],
                                                [s[:, m, t * P:(t + 1) * P] for s in (xhi, xlo)],
                                                [s[:, m, 0, :] for s in wv], m == 0, m == KT - 1)
                    last.then_inc(a_pen.sem, 1)
                elif step == "top":
                    wait(pe, a_vec, n, f"max{NN - 1}")
                    for t in range(2):
                        last = nc.tensor.transpose(ps[:, 0, t * P:(t + 1) * P],
                                                   top[:, t, :, :].rearrange("p g s -> p (g s)"), k.ident[:, :])
                    last.then_inc(a_pen.sem, 1)
                else:
                    u = step
                    t, g, r0, heads = NAT[u]
                    if u == 0:
                        wait(pe, a_vec, n, "q")
                        wait(pe, a_sca, n, "khi")
                    if u >= 2:
                        wait(pe, a_vec, n, f"max{u - 2}")
                    nk = P * (t + 1)
                    out = ps[:, 1 + u % 2, :].rearrange("p (r n) -> p r n", n=nk)
                    nc.tensor.matmul(out[:, :, nk - P:nk], eye, mask.unsqueeze(1).broadcast_to([P, heads, P]),
                                     start=True, stop=False, skip_group_check=True)
                    for r in range(heads):
                        last = nc.tensor.matmul(out[:, r, :], q[:, r0 + r, t * P:(t + 1) * P],
                                                kh[:, g, 0:nk], start=False, stop=r == heads - 1,
                                                skip_group_check=True)
                    last.then_inc(a_pen.sem, 1)

            def phase_c(step, n):
                if step == "wo":
                    wait(pe, c_pol, n, "olo")
                    wait(pe, c_vec, n - 1, "res")
                    for t in range(2):
                        for r in range(REP):
                            last = split_matmul(nc, ps[:, 5, t * H:(t + 1) * H],
                                                [s[:, t, r, :] for s in (ohi, olo)],
                                                [s[:, 0, r, :] for s in wo], r == 0, r == REP - 1)
                    last.then_inc(c_pen.sem, 1)

            for v in range(SLOTS):
                for step in A_AT.get(v, []):
                    phase_a(step, 0, 0)
            with pe.Fori(0, SEQS // AU) as i:
                for s in range(AU):
                    n, par = i * AU + s, s % 2
                    q, keys = q_[:, par], (kh_[:, par], kl_[:, par])
                    for v in range(SLOTS):
                        if v < NU:
                            t, g, kt = UNITS[v]
                            if v == 0:
                                wait(pe, a_sca, n, "shift")
                            wait(pe, exps, n if v >= 2 else n - 1, f"unit{(v - 2) % NU}")
                            out = ps[:, 3 + v % 2, :]
                            for e in range(2):
                                nc.tensor.matmul(out.rearrange("p (r n) -> p r n", r=REP),
                                                 keys[e][:, g, kt * P:(kt + 1) * P],
                                                 q[:, :, t * P:(t + 1) * P],
                                                 start=e == 0, stop=False, skip_group_check=True)
                            for r in range(REP):
                                last = nc.tensor.matmul(out[:, r * P:(r + 1) * P], pick[:, g, r, :],
                                                        shift_[:, par, t * P:(t + 1) * P], start=False,
                                                        stop=r == REP - 1, skip_group_check=True)
                            last.then_inc(scores.sem, 1)
                        for p in pv_at[v]:
                            t, kt = PV[p]
                            wait(pe, probs, n, f"unit{KV * p + KV - 1}")
                            if p == 0:
                                wait(pe, c_vec, n, "o")
                            for g in range(KV):
                                last = nc.tensor.matmul(ps[slot(g), 6 + t, :], v1_[:, par, kt, g, :],
                                                        pr[:, (KV * p + g) % RING_P, :], start=kt == 0,
                                                        stop=kt == t, skip_group_check=True,
                                                        tile_position=(0, SLOT * g))
                            last.then_inc(pvs.sem, 1)
                        for step in A_AT.get(v, []):
                            phase_a(step, n + 1, 1 - par)
                        for step in C_AT.get(v, []):
                            phase_c(step, n)
            phase_c("wo", SEQS)

        @block.scalar
        def _(act):
            for s in (a_sca, exps, c_sca, norm_sca):
                s.start(act)
            act.wait_ge(ready, 1)

            def phase_a(step, n, par):
                if step == "x":
                    wait(act, a_pen, n, "xT")
                    nc.scalar.activation(xhi[:, :, :].rearrange("p m t -> p (m t)"), ps[:, 0, :], ACT.Copy)\
                        .then_inc(a_sca.sem, 1)
                elif step == "qkv":
                    wait(act, a_pen, n, "q")
                    nc.scalar.activation(qh[:, :, :].rearrange("p r t -> p (r t)"),
                                         ps[:, 1:3, :].rearrange("p b n -> p (b n)"), ACT.Copy)\
                        .then_inc(a_sca.sem, 1)
                    wait(act, a_pen, n, "kv")
                    for g in range(KV):
                        last = nc.scalar.activation(kh_[slot(g), par, g, :], ps[slot(g), 0, 0:T], ACT.Copy)
                    last.then_inc(a_sca.sem, 1)
                    nc.scalar.activation(v1_[:, par, :, :, 0:D],
                                         ps[:, 0, T:T + 2 * KV * D].rearrange("p (t g d) -> p t g d", t=2, g=KV),
                                         ACT.Copy).then_inc(a_sca.sem, 1)
                elif step == "top":
                    wait(act, a_pen, n, "maxT")
                    nc.scalar.activation(shift_[:, par, :], ps[:, 0, 0:2 * P], ACT.Copy, scale=-1.0)\
                        .then_inc(a_sca.sem, 1)

            def phase_c(step, n):
                if step == "o":
                    wait(act, c_vec, n, "o")
                    nc.scalar.activation(ohi[:, :, :, :].rearrange("p t r n -> p (t r n)"),
                                         o[:, :, :].rearrange("p t n -> p (t n)"), ACT.Copy)\
                        .then_inc(c_sca.sem, 1)

            def root(i):
                wait(act, norm_vec, i, "mv")
                nc.scalar.activation(std[:, :], mv[:, :, 1], ACT.Sqrt, bias=k.eps[:, 0:1])\
                    .then_inc(norm_sca.sem, 1)

            for v in range(SLOTS):
                for step in A_AT.get(v, []):
                    phase_a(step, 0, 0)
            with act.Fori(0, SEQS // AU) as i:
                for s in range(AU):
                    n, par = i * AU + s, s % 2
                    for v in range(SLOTS):
                        if v < NU:
                            wait(act, scores, n, f"unit{v}")
                            wait(act, probs, n if v >= RING_E else n - 1, f"unit{(v - RING_E) % NU}")
                            nc.scalar.activation(ex[:, v % RING_E, :], ps[:, 3 + v % 2, :], ACT.Exp, scale=SCALE)\
                                .then_inc(exps.sem, 1)
                        for step in A_AT.get(v, []):
                            phase_a(step, n + 1, 1 - par)
                        for step in C_AT.get(v, []):
                            phase_c(step, n)
                        if s == AU - 1 and v == SQRT_AT:
                            root(i)
            phase_c("o", SEQS)
            root(SEQS // AU)

        @block.vector
        def _(dve):
            for s in (a_vec, c_vec, norm_vec):
                s.start(dve)
            dve.wait_ge(ready, 1)
            nc.vector.memset(ps[:, 6:8, :], 1.0).then_inc(ready, 1)
            hold(dve, ready, 2, passed)

            def phase_a(step, n, par):
                if step == "x":
                    wait(dve, a_sca, n, "xhi")
                    nc.vector.tensor_tensor(xlo[:, :, :].rearrange("p m t -> p (m t)"), ps[:, 0, :],
                                            xhi[:, :, :].rearrange("p m t -> p (m t)"), ALU.subtract)\
                        .then_inc(a_vec.sem, 1)
                elif step == "qkv":
                    wait(dve, a_sca, n, "qhi")
                    for b in range(2):
                        last = nc.vector.scalar_tensor_tensor(
                            out=q_[:, par, 2 * b:2 * b + 2, :].rearrange("p r t -> p (r t)"),
                            in0=qh[:, 2 * b:2 * b + 2, :].rearrange("p r t -> p (r t)"), scalar=negate,
                            in1=ps[:, 1 + b, :], op0=ALU.mult, op1=ALU.add)
                    last.then_inc(a_vec.sem, 1)
                    wait(dve, a_sca, n, "v")
                    for g in range(KV):
                        last = nc.vector.tensor_tensor(kl_[slot(g), par, g, :], ps[slot(g), 0, 0:T],
                                                       kh_[slot(g), par, g, :], ALU.subtract)
                    last.then_inc(a_vec.sem, 1)
                elif step != "top":
                    u = step
                    t, g, r0, heads = NAT[u]
                    wait(dve, a_pen, n, f"max{u}")
                    nc.vector.tensor_reduce(top[:, t, g, r0:r0 + heads],
                                            ps[:, 1 + u % 2, :].rearrange("p (r n) -> p r n", r=heads),
                                            AX_X, ALU.max).then_inc(a_vec.sem, 1)

            def phase_c(step, n, s):
                if step == "o":
                    hold(dve, pvs.sem, pvs.after(n - 1, f"pv{len(PV) - 1}"), passed)
                    nc.vector.stream_shuffle(rec[:, :, :], ps[:, 6:8, :], [D] * SLOT).then_inc(c_vec.sem, 1)
                    wait(dve, c_vec, n, "sum")
                    nc.vector.reciprocal(rec[:, :, :], rec[:, :, :]).then_inc(c_vec.sem, 1)
                    wait(dve, c_vec, n, "rec")
                    nc.vector.tensor_tensor(o[:, :, :], ps[:, 6:8, :], rec[:, :, :], ALU.mult)\
                        .then_inc(c_vec.sem, 1)
                elif step == "wo":
                    wait(dve, c_pen, n, "wo")
                    nc.vector.tensor_tensor(res[:, s, :], ps[:, 5, :], k.x_all[:, bass.ds(n * (2 * H), 2 * H)],
                                            ALU.add)\
                        .then_inc(c_vec.sem, 1)
                    wait(dve, c_vec, n, "res")
                    for t in range(2):
                        last = nc.vector.bn_stats(st[:, 2 * s + t, :], res[:, s, t * H:(t + 1) * H])
                    last.then_inc(c_vec.sem, 1)

            for v in range(SLOTS):
                for step in A_AT.get(v, []):
                    phase_a(step, 0, 0)
            def variance(i, last_s, tiles):
                hold(dve, c_vec.sem, c_vec.after(i * AU + last_s, "stats"), passed)
                for t in range(tiles):
                    last = nc.vector.bn_aggr(mv[:, t, :], st[:, t, :])
                last.then_inc(norm_vec.sem, 1)

            def normalise(i, tiles):
                wait(dve, norm_sca, i, "std")
                nc.vector.reciprocal(rstd[:, :], std[:, :]).then_inc(norm_vec.sem, 1)
                wait(dve, norm_vec, i, "rstd")
                for t in range(tiles):
                    last = nc.vector.tensor_scalar(k.x_all[:, bass.ds(i * (2 * AU * H) + t * H, H)],
                                                   res[:, t // 2, (t % 2) * H:(t % 2 + 1) * H],
                                                   mv[:, t, 0:1], rstd[:, t:t + 1], ALU.subtract, ALU.mult)
                last.then_inc(norm_vec.sem, 1)

            with dve.Fori(0, SEQS // AU) as i:
                for s in range(AU):
                    n, par = i * AU + s, s % 2
                    for v in range(SLOTS):
                        for step in C_AT.get(v, []):
                            phase_c(step, n, s)
                        for step in A_AT.get(v, []):
                            phase_a(step, n + 1, 1 - par)
                        if s == AU - 1 and v == NORM_AT:
                            variance(i, AU - 1, 2 * AU)
                        if s == AU - 1 and v == OUT_AT:
                            normalise(i, 2 * AU)
            for step in ("o", "wo"):
                phase_c(step, SEQS, 0)
            variance(SEQS // AU, 0, 2)
            normalise(SEQS // AU, 2)


class Shared:
    pass


def build(nc, x, l0, vecs, route, moe, l1, w2, ident, had, att, bias, slots, results, out):
    k = Shared()
    k.d_l0, k.d_vecs, k.d_moe, k.d_l1, k.d_w2, k.d_ident, k.d_had, k.d_att, k.d_bias = \
        l0, vecs, moe, l1, w2, ident, had, att, bias
    k.d_x, k.d_out, k.d_route = x, out, route
    k.d_slots, k.d_y = slots, results
    with ExitStack() as ctx:
        def sb(name, shape, dt=F32):
            return ctx.enter_context(nc.sbuf_tensor(name, shape, dt))

        k.ps = ctx.enter_context(nc.psum_tensor("ps", [P, 8, 512], F32))
        k.x_all = sb("x", [P, (TILES + 4) * H])
        k.x = k.x_all[:, 2 * H:]
        k.vecs = sb("vecs", [P, 14])
        k.decay = sb("decay", [P, KT])
        k.wrow = sb("wrow", [P, KT, T])
        k.eps = sb("eps", [P, 1])
        k.ident = sb("ident", [P, P])
        k.l0_hi, k.l0_lo = sb("l0_hi", [P, C_L0], F16), sb("l0_lo", [P, C_L0], F16)
        k.moe_hi, k.moe_lo = sb("moe_hi", [P, C_MOE], F16), sb("moe_lo", [P, C_MOE], F16)
        load_stage(nc, k)
        time_mix_stage(nc, k)
        k.gate = sb("gate", [P, TILES])
        k.weight = sb("weight", [P, TILES, TOPK])
        k.slot = sb("slot", [P, TILES, TOPK], I32)
        k.expert = sb("expert", [1, CHAINS * ROUTE_TILES], I32)
        router_stage(nc, k)
        k.l1_hi, k.l1_lo = sb("l1_hi", [P, C_L1], F16), sb("l1_lo", [P, C_L1], F16)
        k.att_const = sb("att_const", [P, 1 + 6 * P])
        gate_up = [w[:, 0:C_GU].rearrange("p (m c n) -> p m c n", m=KT, c=SLICES) for w in (k.moe_hi, k.moe_lo)]
        down = [w[:, C_GU:].rearrange("p (b h) -> p b h", h=H) for w in (k.moe_hi, k.moe_lo)]
        feed_forward_stage(nc, k, "sh_", SH, I_MOE, SHARED_BLOCKS, [w[:, :, E:, :] for w in gate_up],
                           [w[:, E * EXPERT_BLOCKS:, :] for w in down], 2 * CHAINS, shared=True)
        expert_stage(nc, k, "even_", chain=0)
        expert_stage(nc, k, "odd_", chain=1, combine=0)
        expert_stage(nc, k, "last_", combine=1)
        k.w2_hi = k.moe_hi[:, 0:FF_BLOCKS * H].rearrange("p (c h) -> p c h", h=H)
        k.w2_lo = k.moe_lo[:, 0:FF_BLOCKS * H].rearrange("p (c h) -> p c h", h=H)
        hadamard_stage(nc, k)
        attention_stage(nc, k)
        at = C_Q + C_K + C_V + C_O
        up = [w[:, at:at + C_FF].rearrange("p (m c n) -> p m c n", m=KT, c=I_FF // 256)
              for w in (k.l1_hi, k.l1_lo)]
        feed_forward_stage(nc, k, "ff_", I_FF // 256, 256, FF_BLOCKS, up, [k.w2_hi, k.w2_lo], 4)


def rows(a):
    return a.reshape(-1, P, a.shape[-1]).transpose(1, 0, 2)


def cols(*parts):
    return np.ascontiguousarray(np.concatenate([p.reshape(P, -1) for p in parts], axis=1))


def kernel(**inputs):
    import concourse.bacc as bacc
    from concourse.bass_utils import run_bass_kernel_spmd

    a = {n: np.asarray(v) for n, v in inputs.items()}
    A, F, B, G = "L0_attn_", "L0_ffn_", "L1_attn_", "L1_ffn_"
    f32 = np.float32

    gates = np.concatenate([a[F + "w_gate"].transpose(1, 0, 2), a[F + "sh_gate"].reshape(H, SH, I_MOE)], 1)
    ups = np.concatenate([a[F + "w_up"].transpose(1, 0, 2), a[F + "sh_up"].reshape(H, SH, I_MOE)], 1)
    gate_up = np.concatenate([gates, ups], 2).reshape(H, -1)
    down = np.zeros((E, EXPERT_BLOCKS * P, H), f32)
    down[:, :I_MOE] = a[F + "w_down"]
    sh_down = np.zeros((SHARED_BLOCKS * P, H), f32)
    sh_down[:I_SH] = a[F + "sh_down"]
    down = np.concatenate([down.reshape(-1, H), sh_down], 0)

    wq = a[B + "Wq"].T.reshape(H, KV, REP, D).transpose(0, 2, 1, 3)
    wq = np.concatenate([wq, wq], 3).reshape(H, REP * P)
    wk = a[B + "Wk"].T.reshape(H, KV, D)
    wk = np.concatenate([wk, wk], 2).reshape(H, P)
    wo = np.zeros((REP, KV, SLOT, H), f32)
    wo[:, :, :D] = a[B + "Wo"].T.reshape(KV, REP, D, H).transpose(1, 0, 2, 3)
    chunks = I_FF // 256
    ff = np.concatenate([a[G + "W1"].T.reshape(H, chunks, 256), a[G + "W3"].T.reshape(H, chunks, 256)], 2)

    vec_names = ["ln_scale", "ln_bias", "mix_k", "mix_v", "mix_r", "time_first", "time_decay"]
    upper = np.triu(np.ones((P, P), f32), 1)
    numbers = np.concatenate([P * np.arange(CTILES), np.arange(ROUTE_TILES)]).astype(f32)

    had = np.ones((1, 1), f32)
    while had.shape[0] < P:
        had = np.block([[had, had], [had, -had]])
    row, col = np.arange(P)[:, None], np.arange(P)[None, :]
    negate = np.where(np.arange(P)[:, None] % SLOT < D, 0.0, -1.0).astype(f32)
    mask = np.where(col > row, NEG, 0.0).astype(f32)
    pick = np.stack([np.broadcast_to((np.arange(P) % SLOT == r)[:, None], (P, P)) for r in range(REP)], 1)
    slopes = 2.0 ** (-8.0 / HEADS * np.arange(1, HEADS + 1))
    dist = np.stack([col - row, col - row + P], 0).astype(np.float64)
    bias = np.exp(-slopes[:, None, None, None] * np.sqrt(np.maximum(dist, 0))) * (dist >= 0)
    bias = bias.reshape(KV, REP, 2, P, P).transpose(3, 0, 2, 1, 4).astype(f32)

    arrays = {
        "x": a[A + "x"].reshape(TILES, P, H),
        "l0": cols(*[rows(a[A + n]) for n in ("Wk", "Wv", "Wr", "Wo")],
                   rows(np.concatenate([a[F + "router_w"].T, a[F + "sh_gate_w"]], 1))),
        "vecs": cols(*[a[A + n].reshape(KT, P).T for n in vec_names]),
        "route": cols(upper, np.broadcast_to(numbers, (P, len(numbers)))),
        "moe": cols(rows(gate_up), rows(down)),
        "l1": cols(rows(wq), rows(wk), rows(a[B + "Wv"].T), rows(wo.reshape(-1, H)), rows(ff.reshape(H, -1))),
        "w2": cols(rows(a[G + "W2"].T)),
        "ident": np.eye(P, dtype=f32),
        "had": had,
        "att": cols(negate, np.eye(P, dtype=f32), mask, pick.astype(f32)),
        "bias": cols(bias),
    }
    nc = bacc.Bacc("TRN2", target_bir_lowering=False, num_devices=1)
    args = {}
    feed = {}
    for name, v in arrays.items():
        v = np.ascontiguousarray(v)
        feed[f"in_{name}"] = v
        args[name] = nc.dram_tensor(f"in_{name}", v.shape, F32, kind="ExternalInput").ap()
    for name, tiles, width, dt in (("slots", SLOT_TILES + LOADS_AHEAD, 2 * H, F16), ("results", SLOT_TILES, H, F32)):
        args[name] = [nc.dram_tensor(f"{name}_{c}", (tiles * P, width), dt, kind="Internal").ap()
                      for c in range(CHAINS)]
    args["out"] = nc.dram_tensor("out_0", (TILES, P, H), F32, kind="ExternalOutput").ap()
    build(nc, **args)
    r = run_bass_kernel_spmd(nc, [feed], core_ids=[0])
    return r.results[0]["out_0"].reshape(SEQS, T, H)
```

```python
from contextlib import ExitStack

import concourse.bass as bass
from concourse import mybir
import numpy as np

ALU = mybir.AluOpType
ACT = mybir.ActivationFunctionType
F32 = mybir.dt.float32
F16 = mybir.dt.float16
BF16 = mybir.dt.bfloat16
I32 = mybir.dt.int32
AX_X = mybir.AxisListType.X

P = 128
SEQS, T, H = 16, 256, 256
TOK = SEQS * T
TILES = TOK // P
KT = H // P
LN_EPS = 1e-5
NEG = -1.0e30

GROUP = 4
GTOK = GROUP * P
GROUPS = TILES // GROUP
GSEQ = GTOK // T

E, TOPK = 16, 4
I_MOE, I_SH = 176, 704
SH = I_SH // I_MOE
SLICES = E + SH
EXPERT_BLOCKS = 2
SHARED_BLOCKS = 6
I_FF = 1024
FF_BLOCKS = I_FF // P

HEADS, KV, D = 16, 4, 16
REP = HEADS // KV
SLOT = 32
SCALE = D ** -0.5

CHAINS = 2
CTILES = TILES // CHAINS
BODY = 20
SLOT_TILES = -(-((CTILES * P * TOPK + (P - 1) * E) // P) // BODY) * BODY
LOADS_AHEAD = 5
C_ROUTE = P + CTILES + 1

C_MIX = 2 * 3 * KT * H
C_TM = C_MIX + KT * H
C_RT = KT * (E + 1)
C_L0 = C_TM + C_RT
C_RAW = 4 * KT * H + C_RT
C_GU = KT * SLICES * 2 * I_MOE
C_DN = (E * EXPERT_BLOCKS + SHARED_BLOCKS) * H
C_MOE = C_GU + C_DN
C_Q, C_K, C_V, C_O = KT * REP * P, KT * P, KT * KV * D, REP * H
C_FF = KT * 2 * I_FF
C_L1 = C_Q + C_K + C_V + C_O + C_FF


class Count:

    def __init__(self, sem):
        self.sem = sem

    def start(self, eng):
        eng.sem_inc(self.sem, 2)

    def after(self, n):
        return n + 3


class Steps:

    def __init__(self, sem, names):
        self.sem, self.names = sem, names

    def start(self, eng):
        eng.sem_inc(self.sem, len(self.names))

    def after(self, i, name):
        return (i + 1) * len(self.names) + self.names.index(name) + 1


def hold(eng, sem, value, passed):
    eng.wait_ge(sem, value)
    eng.sem_inc(passed, 1)


def split_matmul(nc, out, stationary, moving, first=True, last=True):
    nc.tensor.matmul(out, stationary[0], moving[0], start=first, stop=False, skip_group_check=True)
    nc.tensor.matmul(out, stationary[1], moving[0], start=False, stop=False, skip_group_check=True)
    return nc.tensor.matmul(out, stationary[0], moving[1], start=False, stop=last, skip_group_check=True)


def load_stage(nc, k):
    with ExitStack() as ctx:
        def sb(name, shape, dt=F32):
            return ctx.enter_context(nc.sbuf_tensor("ld_" + name, shape, dt))

        def sem(name):
            return ctx.enter_context(nc.semaphore("ld_" + name))

        raw = sb("raw", [P, C_RAW])
        full = sb("full", [P, C_L0])
        rest = sb("rest", [P, 3, KT])
        vecs = k.vecs
        loaded, x_loaded, hi_done, decay, scaled, vec = (
            sem(n) for n in ("loaded", "x_loaded", "hi_done", "decay", "scaled", "vector"))
        block = ctx.enter_context(nc.Block())
        shares = vecs[:, 4:10].rearrange("p (j m) -> p j m", m=KT)

        @block.sync
        def _(sp):
            sp.dma_start(raw[:, :], k.d_l0).then_inc(loaded, 16)
            sp.dma_start(vecs[:, :], k.d_vecs).then_inc(loaded, 16)
            sp.dma_start(k.ident[:, :], k.d_ident).then_inc(loaded, 16)
            for c in range(4):
                n = TILES // 4
                sp.dma_start(k.x[:, c * n * H:(c + 1) * n * H].rearrange("p (t h) -> p t h", h=H),
                             k.d_x[c * n:(c + 1) * n].rearrange("t p h -> p t h")).then_inc(x_loaded, 16)
            sp.wait_ge(x_loaded, 64)

        @block.scalar
        def _(act):
            act.wait_ge(loaded, 48)
            nc.scalar.activation(full[:, C_MIX:], raw[:, 3 * KT * H:], ACT.Copy).then_inc(scaled, 1)
            act.wait_ge(scaled, 2)
            nc.scalar.activation(k.l0_hi[:, :], full[:, :], ACT.Copy).then_inc(hi_done, 1)
            nc.scalar.activation(k.decay[:, :], vecs[:, 12:14], ACT.Exp).then_inc(decay, 1)

        @block.gpsimd
        def _(pool):
            nc.gpsimd.memset(k.x[:, TILES * H:], 0.0)
            nc.gpsimd.memset(k.x_all[:, 0:2 * H], 0.0)
            nc.gpsimd.memset(k.eps[:, :], LN_EPS)

        @block.vector
        def _(dve):
            dve.wait_ge(loaded, 48)
            nc.vector.tensor_scalar(rest[:, :, :], shares, -1.0, 1.0, ALU.mult, ALU.add).then_inc(vec, 1)
            dve.wait_ge(vec, 1)
            whole = raw[:, 0:3 * KT * H].rearrange("p (j m h) -> p j m h", j=3, m=KT)
            mixed = full[:, 0:C_MIX].rearrange("p (j a m h) -> p j a m h", j=3, a=2, m=KT)
            for j in range(3):
                for a, part in enumerate((shares, rest)):
                    for m in range(KT):
                        last = nc.vector.tensor_scalar_mul(mixed[:, j, a, m, :], whole[:, j, m, :],
                                                           part[:, j, m:m + 1])
            last.then_inc(scaled, 1)
            dve.wait_ge(hi_done, 1)
            nc.vector.tensor_tensor(k.l0_lo[:, :], full[:, :], k.l0_hi[:, :], ALU.subtract).then_inc(vec, 1)
            dve.wait_ge(decay, 1)
            nc.vector.tensor_scalar_mul(k.decay[:, :], k.decay[:, :], -1.0).then_inc(vec, 1)


def time_mix_stage(nc, k):
    PARTS = 8
    WCOLS = C_MOE // GROUPS // PARTS
    FILLS = SLOT_TILES // GROUPS // 2
    with ExitStack() as ctx:
        def sb(name, shape, dt=F32):
            return ctx.enter_context(nc.sbuf_tensor("tm_" + name, shape, dt))

        def sem(name):
            return ctx.enter_context(nc.semaphore("tm_" + name))

        wraw = sb("wraw", [P, 2, WCOLS])
        st, mv, std, rstd, shift = [], [], [], [], []
        for n in ("front_", "end_"):
            st.append(sb(n + "st", [P, GROUP, 6]))
            mv.append(sb(n + "mv", [P, GROUP, 2]))
            std.append(sb(n + "std", [P, GROUP]))
            rstd.append(sb(n + "rstd", [P, GROUP]))
            shift.append(sb(n + "shift", [P, GROUP]))
        xh = sb("xhat", [P, GROUP, H])
        res = sb("res", [P, GROUP, H])
        xn = sb("xn", [P, KT, GSEQ, T + 1])
        xhi, xlo = (sb(n, [P, KT, GSEQ, T + 1], F16) for n in ("xhi", "xlo"))
        yhi, ylo = (sb(n, [P, KT, GTOK], F16) for n in ("yhi", "ylo"))
        kS = sb("k", [P, KT, GSEQ, T])
        gate = sb("gate", [P, KT, GSEQ, T])
        e1, e2, c1, c2 = (sb(n, [P, KT, GSEQ, T]) for n in ("e1", "e2", "c1", "c2"))
        pmax = sb("pmax", [P, KT, GSEQ, T + 1])
        asum = pmax
        bsum = sb("bsum", [P, KT, GSEQ, T + 1])
        f_vec = Steps(sem("front_vector"), ["stats", "mv", "rstd", "shift"])
        b_vec = Steps(sem("back_vector"), ["p", "q", "t1", "t2", "t3", "t4", "c2v", "b", "a", "e1b", "den", "e2v",
                                           "rec", "gated", "y"])
        e_vec = Steps(sem("end_vector"), ["res", "stats", "mv", "rstd", "shift"])
        f_sca = Steps(sem("front_scalar"), ["std", "xhat", "xn", "hi"])
        s_sca = Steps(sem("start_scalar"), ["k", "gate"])
        b_sca = Steps(sem("back_scalar"), ["e1", "e2", "c1", "c2", "hi_y"])
        e_sca = Steps(sem("end_scalar"), ["std", "out"])
        f_pen = Steps(sem("front_tensor"), ["xT", "k", "r", "v"])
        b_pen = Steps(sem("back_tensor"), ["wo"])
        f_pol = Steps(sem("front_pool"), ["lo"])
        b_pol = Steps(sem("back_pool"), ["e1a", "num", "lo_y"])
        w_pol = Steps(sem("weights_pool"), [w + str(n) for n in range(PARTS) for w in ("hi", "lo")])
        w_loaded = [sem(f"w_loaded{r}") for r in range(2)]
        filled, edges, passed = sem("slots_filled"), sem("edges"), k.vector_waits
        ps = k.ps

        def flat(t):
            return t[:, :, :, :].rearrange("p m s t -> p (m s) t")

        def line(t):
            return t[:, :, :, :].rearrange("p m s t -> p (m s t)")

        p_old, p_new = flat(pmax)[:, :, 0:T], flat(pmax)[:, :, 1:T + 1]
        a_old, b_old = flat(asum)[:, :, 0:T], flat(bsum)[:, :, 0:T]
        bank = {n: 2 + 2 * j for j, n in enumerate("kvr")}
        k_ps, v_ps, r_ps = (ps[:, bank[n]:bank[n] + 2, :].rearrange("p m (s t) -> p (m s) t", t=T) for n in "kvr")
        first = k.vecs[:, 10:12]
        block = ctx.enter_context(nc.Block())

        def xs(i, t):
            return k.x[:, bass.ds(i * (GROUP * H) + t * H, H)]

        def wait(eng, steps, i, name):
            eng.wait_ge(steps.sem, steps.after(i, name))

        def groups(eng, body):
            body(0, end=False)
            with eng.Fori(1, GROUPS - 1) as i:
                body(i)
            body(GROUPS - 1, front=False)

        @block.sync
        def _(sp):
            zeros = k.x[:, TILES * H:(TILES + 2) * H].bitcast(F16)
            for c in range(CHAINS):
                for n in range(LOADS_AHEAD):
                    sp.dma_start(k.d_slots[c][(SLOT_TILES + n) * P:(SLOT_TILES + n + 1) * P], zeros[:, 0:2 * H])\
                        .then_inc(filled, 16)
            with sp.Fori(0, GROUPS) as i:
                for n in range(PARTS):
                    wait(sp, w_pol, i if n >= 2 else i - 1, f"lo{(n - 2) % PARTS}")
                    sp.dma_start(wraw[:, n % 2, :], k.d_moe[:, bass.ds(i * (PARTS * WCOLS) + n * WCOLS, WCOLS)])\
                        .then_inc(w_loaded[n % 2], 16)
                    if n == 4:
                        for c in range(CHAINS):
                            for m in range(FILLS):
                                rows = k.d_slots[c][bass.ds(i * (2 * FILLS * P) + m * 2 * P, 2 * P)]
                                sp.dma_start(rows.rearrange("(p r) h -> p (r h)", r=2), zeros)\
                                    .then_inc(filled, 16)
            sp.wait_ge(filled, 16 * CHAINS * (LOADS_AHEAD + GROUPS * FILLS))

        @block.gpsimd
        def _(pool):
            for s in (f_pol, b_pol, w_pol):
                s.start(pool)
            for t in (xhi, xlo):
                nc.gpsimd.memset(flat(t)[:, :, 0:1], 0.0)
            nc.gpsimd.memset(flat(bsum)[:, :, 0:1], 0.0).then_inc(edges, 1)

            def split(i):
                wait(pool, f_sca, i, "hi")
                wait(pool, f_pen, i - 1, "v")
                nc.gpsimd.tensor_tensor(flat(xlo)[:, :, 1:T + 1], flat(xn)[:, :, 1:T + 1],
                                        flat(xhi)[:, :, 1:T + 1], ALU.subtract).then_inc(f_pol.sem, 1)

            def weights(i, n):
                pool.wait_ge(w_loaded[n % 2], i * (16 * PARTS // 2) + 16 * (n // 2 + 1))
                whi, wlo = (w[:, bass.ds(i * (PARTS * WCOLS) + n * WCOLS, WCOLS)] for w in (k.moe_hi, k.moe_lo))
                nc.gpsimd.tensor_copy(whi, wraw[:, n % 2, :]).then_inc(w_pol.sem, 1)
                wait(pool, w_pol, i, f"hi{n}")
                nc.gpsimd.tensor_tensor(wlo, wraw[:, n % 2, :], whi, ALU.subtract).then_inc(w_pol.sem, 1)

            def body(i, front=True, end=True):
                for n in range(3):
                    weights(i, n)
                if front:
                    split(i + 1)
                wait(pool, b_vec, i, "a")
                nc.gpsimd.tensor_tensor(flat(kS), flat(e1), a_old, ALU.mult).then_inc(b_pol.sem, 1)
                wait(pool, b_vec, i, "e2v")
                wait(pool, b_pol, i, "e1a")
                nc.gpsimd.tensor_tensor(flat(e1), flat(kS), flat(e2), ALU.add).then_inc(b_pol.sem, 1)
                for n in range(3, 5):
                    weights(i, n)
                wait(pool, b_sca, i, "hi_y")
                wait(pool, b_pen, i - 1, "wo")
                nc.gpsimd.tensor_tensor(ylo[:, :, :].rearrange("p m t -> p (m t)"), line(c2),
                                        yhi[:, :, :].rearrange("p m t -> p (m t)"), ALU.subtract)\
                    .then_inc(b_pol.sem, 1)
                for n in range(5, PARTS):
                    weights(i, n)

            split(0)
            groups(pool, body)

        @block.tensor
        def _(pe):
            for s in (f_pen, b_pen):
                s.start(pe)
            parts = [w[:, 0:C_MIX].rearrange("p (j a m h) -> p j a m h", j=3, a=2, m=KT)
                     for w in (k.l0_hi, k.l0_lo)]
            out_w = [w[:, C_MIX:C_TM].rearrange("p (m h) -> p m h", m=KT) for w in (k.l0_hi, k.l0_lo)]

            def turn(i):
                wait(pe, f_sca, i, "xhat")
                if not (isinstance(i, int) and i == 0):
                    wait(pe, e_vec, i - 2, "res")
                for m in range(KT):
                    for t in range(GROUP):
                        last = nc.tensor.transpose(ps[:, m, t * P:(t + 1) * P], xh[:, t, m * P:(m + 1) * P],
                                                   k.ident[:, :])
                last.then_inc(f_pen.sem, 1)

            def project(i, name):
                if name == "k":
                    wait(pe, f_pol, i, "lo")
                if name == "v":
                    wait(pe, b_vec, i - 1, "e2v")
                else:
                    wait(pe, s_sca, i - 1, {"k": "k", "r": "gate"}[name])
                for o in range(KT):
                    for a in range(2):
                        for m in range(KT):
                            last = split_matmul(
                                nc, ps[:, bank[name] + o, :].rearrange("p (s t) -> p s t", t=T),
                                [w[:, "kvr".index(name), a, m, o * P:(o + 1) * P] for w in parts],
                                [x[:, m, :, 1 - a:T + 1 - a] for x in (xhi, xlo)],
                                a == 0 and m == 0, a == 1 and m == KT - 1)
                last.then_inc(f_pen.sem, 1)

            def body(i, front=True, end=True):
                if front:
                    turn(i + 1)
                    project(i + 1, "k")
                    project(i + 1, "r")
                    wait(pe, f_sca, i + 1, "xn")
                wait(pe, b_pol, i, "lo_y")
                for t in range(GROUP):
                    for m in range(KT):
                        last = split_matmul(nc, ps[:, t // 2, (t % 2) * H:(t % 2 + 1) * H],
                                            [y[:, m, t * P:(t + 1) * P] for y in (yhi, ylo)],
                                            [w[:, m, :] for w in out_w], m == 0, m == KT - 1)
                last.then_inc(b_pen.sem, 1)
                if front:
                    project(i + 1, "v")

            turn(0)
            for name in "krv":
                project(0, name)
            groups(pe, body)

        @block.scalar
        def _(act):
            for s in (f_sca, s_sca, b_sca, e_sca):
                s.start(act)

            def root(i, which, steps, done):
                wait(act, steps, i, "mv")
                nc.scalar.activation(std[which][:, :], mv[which][:, :, 1], ACT.Sqrt, bias=k.eps[:, 0:1])\
                    .then_inc(done.sem, 1)

            def normalise(i, which, steps, done, out, source):
                wait(act, steps, i, "shift")
                for t in range(GROUP):
                    last = nc.scalar.activation(out(t), source(t), ACT.Identity, scale=rstd[which][:, t:t + 1],
                                                bias=shift[which][:, t:t + 1])
                last.then_inc(done.sem, 1)

            def front_normalise(i):
                wait(act, f_pen, i - 1, "xT")
                normalise(i, 0, f_vec, f_sca, lambda t: xh[:, t, :], lambda t: xs(i, t))

            def end_normalise(i):
                normalise(i, 1, e_vec, e_sca, lambda t: xs(i, t), lambda t: res[:, t, :])

            def turned(i):
                wait(act, f_pen, i, "xT")
                wait(act, f_pol, i - 1, "lo")
                for m in range(KT):
                    last = nc.scalar.activation(xn[:, m, :, 1:T + 1],
                                                ps[:, m, :].rearrange("p (s t) -> p s t", t=T), ACT.Identity,
                                                scale=k.vecs[:, m:m + 1], bias=k.vecs[:, 2 + m:3 + m])
                last.then_inc(f_sca.sem, 1)

            def split(i):
                wait(act, f_sca, i, "xn")
                wait(act, f_pen, i - 1, "v")
                nc.scalar.activation(flat(xhi)[:, :, 1:T + 1], flat(xn)[:, :, 1:T + 1], ACT.Copy)\
                    .then_inc(f_sca.sem, 1)

            def keys(i):
                wait(act, f_pen, i, "k")
                wait(act, b_pol, i - 1, "num")
                nc.scalar.activation(flat(kS), k_ps, ACT.Copy).then_inc(s_sca.sem, 1)

            def gates(i):
                wait(act, f_pen, i, "r")
                wait(act, b_vec, i - 1, "gated")
                nc.scalar.activation(flat(gate), r_ps, ACT.Tanh, scale=0.5).then_inc(s_sca.sem, 1)

            def body(i, front=True, end=True):
                for name, buf in (("t1", e1), ("t2", e2), ("t3", c1), ("t4", c2)):
                    wait(act, b_vec, i, name)
                    nc.scalar.activation(flat(buf), flat(buf), ACT.Exp).then_inc(b_sca.sem, 1)
                if front:
                    root(i + 1, 0, f_vec, f_sca)
                if end:
                    root(i - 1, 1, e_vec, e_sca)
                if front:
                    front_normalise(i + 1)
                    turned(i + 1)
                    split(i + 1)
                if end:
                    end_normalise(i - 1)
                if front:
                    keys(i + 1)
                wait(act, b_vec, i, "y")
                wait(act, b_pen, i - 1, "wo")
                nc.scalar.activation(yhi[:, :, :].rearrange("p m t -> p (m t)"), line(c2), ACT.Copy)\
                    .then_inc(b_sca.sem, 1)
                if front:
                    gates(i + 1)

            root(0, 0, f_vec, f_sca)
            front_normalise(0)
            turned(0)
            split(0)
            keys(0)
            gates(0)
            groups(act, body)
            root(GROUPS - 1, 1, e_vec, e_sca)
            end_normalise(GROUPS - 1)

        @block.vector
        def _(dve):
            for s in (f_vec, b_vec, e_vec):
                s.start(dve)
            dve.wait_ge(edges, 1)

            def statistics(i, which, steps, source):
                for t in range(GROUP):
                    last = nc.vector.bn_stats(st[which][:, t, :], source(t))
                last.then_inc(steps.sem, 1)
                hold(dve, steps.sem, steps.after(i, "stats"), passed)
                for t in range(GROUP):
                    last = nc.vector.bn_aggr(mv[which][:, t, :], st[which][:, t, :])
                last.then_inc(steps.sem, 1)

            def inverse(i, which, steps, root):
                wait(dve, root, i, "std")
                nc.vector.reciprocal(rstd[which][:, :], std[which][:, :]).then_inc(steps.sem, 1)
                wait(dve, steps, i, "rstd")
                nc.vector.scalar_tensor_tensor(out=shift[which][:, :], in0=mv[which][:, :, 0], scalar=-1.0,
                                               in1=rstd[which][:, :], op0=ALU.mult, op1=ALU.mult)\
                    .then_inc(steps.sem, 1)

            def front_statistics(i):
                wait(dve, f_vec, i - 1, "shift")
                statistics(i, 0, f_vec, lambda t: xs(i, t))

            def end_sum(i):
                wait(dve, b_pen, i, "wo")
                wait(dve, e_sca, i - 1, "out")
                for h2 in range(GROUP // 2):
                    last = nc.vector.scalar_tensor_tensor(
                        out=res[:, 2 * h2:2 * h2 + 2, :].rearrange("p t h -> p (t h)"),
                        in0=k.x[:, bass.ds(i * (GROUP * H) + h2 * 2 * H, 2 * H)], scalar=2.0,
                        in1=ps[:, h2, :], op0=ALU.mult, op1=ALU.add)
                last.then_inc(e_vec.sem, 1)
                wait(dve, e_vec, i, "res")
                statistics(i, 1, e_vec, lambda t: res[:, t, :])

            def sums(out, values):
                for m in range(KT):
                    for s in range(GSEQ):
                        last = nc.vector.tensor_tensor_scan(out[:, m, s, 1:T + 1], c1[:, m, s, :],
                                                            values[:, m, s, :], 0.0, ALU.mult, ALU.add)
                return last

            def exponents(i):
                wait(dve, s_sca, i, "k")
                wait(dve, b_vec, i - 1, "y")
                nc.vector.memset(flat(pmax)[:, :, 0:1], NEG)
                for m in range(KT):
                    for s in range(GSEQ):
                        last = nc.vector.tensor_tensor_scan(pmax[:, m, s, 1:T + 1],
                                                            k.decay[:, m:m + 1].broadcast_to([P, T]),
                                                            kS[:, m, s, :], NEG, ALU.add, ALU.max)
                last.then_inc(b_vec.sem, 1)
                wait(dve, b_vec, i, "p")
                for m in range(KT):
                    last = nc.vector.scalar_tensor_tensor(
                        out=e2[:, m, :, :], in0=kS[:, m, :, :], scalar=first[:, m:m + 1],
                        in1=pmax[:, m, :, 0:T], op0=ALU.add, op1=ALU.max)
                last.then_inc(b_vec.sem, 1)
                wait(dve, b_vec, i, "q")
                nc.vector.tensor_tensor(flat(e1), p_old, flat(e2), ALU.subtract).then_inc(b_vec.sem, 1)
                wait(dve, b_vec, i, "t1")
                for m in range(KT):
                    last = nc.vector.scalar_tensor_tensor(
                        out=e2[:, m, :, :], in0=kS[:, m, :, :], scalar=first[:, m:m + 1],
                        in1=e2[:, m, :, :], op0=ALU.add, op1=ALU.subtract)
                last.then_inc(b_vec.sem, 1)
                for m in range(KT):
                    last = nc.vector.scalar_tensor_tensor(
                        out=c1[:, m, :, :], in0=pmax[:, m, :, 0:T], scalar=k.decay[:, m:m + 1],
                        in1=pmax[:, m, :, 1:T + 1], op0=ALU.add, op1=ALU.subtract)
                last.then_inc(b_vec.sem, 1)
                wait(dve, b_pol, i - 1, "lo_y")
                nc.vector.tensor_tensor(flat(c2), flat(kS), p_new, ALU.subtract).then_inc(b_vec.sem, 1)

            def state(i):
                wait(dve, b_sca, i, "c2")
                wait(dve, f_pen, i, "v")
                nc.vector.tensor_tensor(flat(kS), flat(c2), v_ps, ALU.mult).then_inc(b_vec.sem, 1)
                sums(bsum, c2).then_inc(b_vec.sem, 1)
                nc.vector.memset(flat(asum)[:, :, 0:1], 0.0)
                wait(dve, b_vec, i, "c2v")
                sums(asum, kS).then_inc(b_vec.sem, 1)
                wait(dve, b_vec, i, "a")
                nc.vector.tensor_tensor(flat(c1), flat(e1), b_old, ALU.mult).then_inc(b_vec.sem, 1)
                wait(dve, b_vec, i, "e1b")
                nc.vector.tensor_tensor(flat(c2), flat(c1), flat(e2), ALU.add).then_inc(b_vec.sem, 1)
                wait(dve, b_vec, i, "den")
                nc.vector.tensor_tensor(flat(e2), flat(e2), v_ps, ALU.mult).then_inc(b_vec.sem, 1)

            def result(i):
                wait(dve, b_pol, i, "num")
                wait(dve, s_sca, i, "gate")
                nc.vector.scalar_tensor_tensor(out=line(e2), in0=line(gate), scalar=1.0, in1=line(e1),
                                               op0=ALU.add, op1=ALU.mult).then_inc(b_vec.sem, 1)
                wait(dve, b_vec, i, "gated")
                nc.vector.scalar_tensor_tensor(out=line(c2), in0=line(e2), scalar=0.5, in1=line(c1),
                                               op0=ALU.mult, op1=ALU.mult).then_inc(b_vec.sem, 1)

            def body(i, front=True, end=True):
                if front:
                    front_statistics(i + 1)
                exponents(i)
                if end:
                    end_sum(i - 1)
                if front:
                    inverse(i + 1, 0, f_vec, f_sca)
                if end:
                    inverse(i - 1, 1, e_vec, e_sca)
                state(i)
                nc.vector.reciprocal(flat(c1), flat(c2)).then_inc(b_vec.sem, 1)
                result(i)

            front_statistics(0)
            inverse(0, 0, f_vec, f_sca)
            groups(dve, body)
            end_sum(GROUPS - 1)
            inverse(GROUPS - 1, 1, e_vec, e_sca)


def router_stage(nc, k):
    with ExitStack() as ctx:
        def sb(name, shape, dt=F32):
            return ctx.enter_context(nc.sbuf_tensor("rt_" + name, shape, dt))

        def sem(name):
            return ctx.enter_context(nc.semaphore("rt_" + name))

        xc = sb("xc", [P, 2, GROUP, H])
        xhi, xlo = (sb(n, [P, 2, KT, GTOK], F16) for n in ("xhi", "xlo"))
        logit = sb("logit", [P, TILES, E + 1])
        prob = sb("prob", [P, TILES, E])
        top = sb("top", [P, TILES])
        tot = sb("tot", [P, TILES])
        rec = sb("rec", [P, TILES])
        gate = sb("gate", [P, TILES])
        eight = sb("eight", [P, TILES, 8])
        above, level, chosen = (k.spare_lo(TILES, E) for _ in range(3))
        order, share = k.order, k.share
        picked = k.spare_hi(TILES, E)
        first_of = sb("first_of", [P, CHAINS, E])
        begun = sb("begun", [P, CHAINS, E])
        expert_f = sb("expert_f", [P, CHAINS])
        need = sb("need", [P, TILES])
        slot_f = sb("slot_f", [P, TILES, TOPK])
        consts = sb("consts", [P, C_ROUTE])
        upper_f, steps, own = consts[:, 0:P], consts[:, P:P + CTILES], consts[:, P + CTILES:]
        upper = sb("upper", [P, P], BF16)
        ones = sb("ones", [P, P], BF16)
        restart = sb("restart", [P, TILES, E])
        mask = sb("mask", [P, CHAINS, E, CTILES], BF16)
        total, upto, place = (k.spare_lo(CHAINS, E, CTILES) for _ in range(3))
        tiles_of, tiles_to = (sb(n, [P, CHAINS, E]) for n in ("tiles_of", "tiles_to"))
        loaded, prepared, counted = sem("loaded"), sem("prepared"), sem("counted")
        first_copied, last_copied, transposed, hi_done, lo_done, scored, kept = (
            Count(sem(n)) for n in ("first_copied", "last_copied", "transposed", "hi_done", "lo_done", "scored",
                                    "kept"))
        chain, exps, masked = sem("vector_chain"), sem("exps"), sem("masked")
        experts_found, experts_turned = sem("experts_found"), sem("experts_turned")
        ps = k.ps
        W = E + 1
        wt = [w[:, C_TM:C_L0].rearrange("p (m e) -> p m e", m=KT) for w in (k.l0_hi, k.l0_lo)]
        block = ctx.enter_context(nc.Block())

        def wait(eng, count, n):
            eng.wait_ge(count.sem, count.after(n))

        def groups(eng, start, body):
            start(0, 0)
            with eng.Fori(0, GROUPS // 2) as i:
                for par in range(2):
                    body(i * 2 + par, par, start)

        def copy_x(eng, copy, count, g, par, half):
            wait(eng, transposed, g - 2)
            copy(xc[:, par, 2 * half:2 * half + 2, :].rearrange("p t h -> p (t h)"),
                 k.x[:, bass.ds(g * (GROUP * H) + half * 2 * H, 2 * H)]).then_inc(count.sem, 1)

        @block.sync
        def _(sp):
            sp.dma_start(consts[:, :], k.d_route).then_inc(loaded, 16)

        @block.gpsimd
        def _(pool):
            nc.gpsimd.memset(ones[:, :], 1.0)
            nc.gpsimd.memset(restart[:, :, 1:], 1.0)
            nc.gpsimd.memset(restart[:, :, 0:1], 0.0)
            pool.wait_ge(loaded, 16)
            nc.gpsimd.tensor_copy(upper[:, :], upper_f).then_inc(prepared, 1)
            first_copied.start(pool)

            def start(g, par):
                copy_x(pool, nc.gpsimd.tensor_copy, first_copied, g, par, 0)

            groups(pool, start, lambda g, par, start: start(g + 1, 1 - par))

        @block.tensor
        def _(pe):
            transposed.start(pe)
            scored.start(pe)

            def start(g, par):
                wait(pe, first_copied, g)
                wait(pe, last_copied, g)
                wait(pe, lo_done, g - 2)
                for m in range(KT):
                    for t in range(GROUP):
                        last = nc.tensor.transpose(ps[:, 2 * par + m, t * P:(t + 1) * P],
                                                   xc[:, par, t, m * P:(m + 1) * P], k.ident[:, :])
                last.then_inc(transposed.sem, 1)

            def body(g, par, start):
                start(g + 1, 1 - par)
                wait(pe, lo_done, g)
                wait(pe, kept, g - 2)
                for t in range(GROUP):
                    for m in range(KT):
                        last = split_matmul(nc, ps[:, 4 + par, t * W:(t + 1) * W],
                                            [a[:, par, m, t * P:(t + 1) * P] for a in (xhi, xlo)],
                                            [w[:, m, :] for w in wt], m == 0, m == KT - 1)
                last.then_inc(scored.sem, 1)

            groups(pe, start, body)
            pe.wait_ge(prepared, 1)
            pe.wait_ge(masked, 1)
            taken = mask[:, :, :, :].rearrange("p c e t -> p (c e t)")
            nc.tensor.matmul(ps[:, 6, :], upper[:, :], taken, start=True, stop=True)
            nc.tensor.matmul(ps[:, 7, :], ones[:, :], taken, start=True, stop=True).then_inc(counted, 1)
            pe.wait_ge(experts_found, 1)
            for c in range(CHAINS):
                last = nc.tensor.matmul(ps[0:1, c, 0:P], expert_f[:, c:c + 1], k.ident[:, :], start=True, stop=True)
            last.then_inc(experts_turned, 1)

        @block.scalar
        def _(act):
            last_copied.start(act)
            hi_done.start(act)

            def start(g, par):
                copy_x(act, lambda out, x: nc.scalar.activation(out, x, ACT.Copy), last_copied, g, par, 1)
                wait(act, transposed, g)
                wait(act, scored, g - 2)
                nc.scalar.activation(xhi[:, par, :, :], ps[:, 2 * par:2 * par + 2, :], ACT.Copy)\
                    .then_inc(hi_done.sem, 1)

            groups(act, start, lambda g, par, start: start(g + 1, 1 - par))
            act.wait_ge(chain, 2)
            nc.scalar.activation(prob[:, :, :], prob[:, :, :], ACT.Exp).then_inc(exps, 1)
            act.wait_ge(chain, 3)
            nc.scalar.activation(gate[:, :], gate[:, :], ACT.Exp).then_inc(exps, 1)

        @block.vector
        def _(dve):
            lo_done.start(dve)
            kept.start(dve)

            def start(g, par):
                wait(dve, hi_done, g)
                wait(dve, scored, g - 2)
                nc.vector.tensor_tensor(xlo[:, par, :, :], ps[:, 2 * par:2 * par + 2, :], xhi[:, par, :, :],
                                        ALU.subtract).then_inc(lo_done.sem, 1)

            def body(g, par, start):
                start(g + 1, 1 - par)
                wait(dve, scored, g)
                nc.vector.tensor_copy(logit[:, :, :].rearrange("p t e -> p (t e)")[:, bass.ds(g * (GROUP * W), GROUP * W)],
                                      ps[:, 4 + par, 0:GROUP * W]).then_inc(kept.sem, 1)

            groups(dve, start, body)
            wait(dve, kept, GROUPS - 1)
            links = [0]

            def link(ins):
                ins.then_inc(chain, 1)
                links[0] += 1
                dve.wait_ge(chain, links[0])

            def per_expert(t):
                return t.unsqueeze(2).broadcast_to([P, TILES, E])

            link(nc.vector.tensor_reduce(top[:, :], logit[:, :, 0:E], AX_X, ALU.max))
            link(nc.vector.tensor_tensor(prob[:, :, :], logit[:, :, 0:E], per_expert(top[:, :]), ALU.subtract))
            link(nc.vector.tensor_scalar(gate[:, :], logit[:, :, E], -1.0, 87.0, ALU.mult, ALU.min))
            dve.wait_ge(exps, 1)
            link(nc.vector.tensor_reduce(tot[:, :], prob[:, :, :], AX_X, ALU.add))
            link(nc.vector.reciprocal(rec[:, :], tot[:, :]))
            link(nc.vector.tensor_tensor(prob[:, :, :], prob[:, :, :], per_expert(rec[:, :]), ALU.mult))
            dve.wait_ge(prepared, 1)
            for t in range(TILES):
                last = nc.vector.max(eight[:, t, :], prob[:, t, :])
            link(last)
            fourth = per_expert(eight[:, :, TOPK - 1])
            link(nc.vector.tensor_tensor(above[:, :, :], prob[:, :, :], fourth, ALU.is_gt))
            link(nc.vector.tensor_tensor(level[:, :, :], prob[:, :, :], fourth, ALU.is_equal))
            link(nc.vector.tensor_reduce(need[:, :], above[:, :, :], AX_X, ALU.add))
            link(nc.vector.tensor_scalar(need[:, :], need[:, :], -1.0, float(TOPK), ALU.mult, ALU.add))

            def flat(t):
                return t[:, :, :].rearrange("p t e -> p (t e)")

            def scan(out, begin, values):
                return nc.vector.tensor_tensor_scan(out, begin, values, 0.0, ALU.mult, ALU.add)

            link(scan(flat(order), flat(restart), flat(level)))
            link(nc.vector.tensor_tensor(order[:, :, :], order[:, :, :], per_expert(need[:, :]), ALU.is_le))
            link(nc.vector.tensor_tensor(flat(level), flat(level), flat(order), ALU.mult))
            link(nc.vector.tensor_tensor(flat(chosen), flat(above), flat(level), ALU.add))
            nc.vector.tensor_copy(mask[:, :, :, :].rearrange("p c e t -> p t c e"),
                                  chosen[:, :, :].rearrange("p (t c) e -> p t c e", c=CHAINS)).then_inc(masked, 1)
            link(scan(flat(order), flat(restart), flat(chosen)))
            link(nc.vector.tensor_tensor(flat(order), flat(order), flat(chosen), ALU.mult))
            link(nc.vector.tensor_tensor(flat(share), flat(prob), flat(chosen), ALU.mult))
            dve.wait_ge(counted, 1)

            def wide(t):
                return t[:, :, :, :].rearrange("p c e t -> p (c e t)")

            link(nc.vector.tensor_copy(wide(total), ps[:, 7, :]))
            link(scan(wide(upto), flat(restart), wide(total)))
            link(nc.vector.tensor_tensor(wide(place), wide(upto), wide(total), ALU.subtract))
            link(nc.vector.tensor_tensor(wide(place), wide(place), ps[:, 6, :], ALU.add))
            count = upto[:, :, :, CTILES - 1].rearrange("p c e -> p (c e)")
            pairs = [P, CHAINS * E, CTILES]
            link(nc.vector.tensor_tensor(total[:, :, :, :].rearrange("p c e t -> p (c e) t"),
                                         count.unsqueeze(2).broadcast_to(pairs),
                                         steps.unsqueeze(1).broadcast_to(pairs), ALU.is_gt))
            link(nc.vector.tensor_reduce(tiles_of[:, :, :].rearrange("p c e -> p (c e)"),
                                         total[:, :, :, :].rearrange("p c e t -> p (c e) t"), AX_X, ALU.add))
            link(scan(flat(tiles_to), restart[:, 0:CHAINS, :].rearrange("p c e -> p (c e)"), flat(tiles_of)))
            link(nc.vector.tensor_tensor(flat(first_of), flat(tiles_to), flat(tiles_of), ALU.subtract))
            link(nc.vector.tensor_scalar(begun[:, :, :], first_of[:, :, :], own, 0.0, ALU.is_le, ALU.add))
            link(nc.vector.tensor_reduce(expert_f[:, :], begun[:, :, :], AX_X, ALU.add))
            nc.vector.tensor_scalar_add(expert_f[:, :], expert_f[:, :], -1.0).then_inc(experts_found, 1)
            link(nc.vector.scalar_tensor_tensor(out=place[:, :, :, :].rearrange("p c e t -> p (c e) t"),
                                                in0=flat(first_of).unsqueeze(2).broadcast_to(pairs),
                                                scalar=float(P),
                                                in1=place[:, :, :, :].rearrange("p c e t -> p (c e) t"),
                                                op0=ALU.mult, op1=ALU.add))
            link(nc.vector.tensor_copy(chosen[:, :, :].rearrange("p (t c) e -> p t c e", c=CHAINS),
                                       place[:, :, :, :].rearrange("p c e t -> p t c e")))
            for j in range(TOPK):
                link(nc.vector.scalar_tensor_tensor(out=flat(picked), in0=flat(order), scalar=float(j + 1),
                                                    in1=flat(chosen), op0=ALU.is_equal, op1=ALU.mult))
                link(nc.vector.tensor_reduce(slot_f[:, :, j], picked[:, :, :], AX_X, ALU.add))
            link(nc.vector.tensor_copy(k.slot[:, 0:TILES, :], slot_f[:, :, :]))
            dve.wait_ge(experts_turned, 1)
            link(nc.vector.tensor_copy(k.expert[:, :].rearrange("p (c t) -> p c t", c=CHAINS), ps[0:1, 0:CHAINS, 0:P]))
            dve.wait_ge(exps, 2)
            link(nc.vector.tensor_scalar_add(gate[:, :], gate[:, :], 1.0))
            link(nc.vector.reciprocal(k.gate[:, :], gate[:, :]))


def feed_forward_stage(nc, k, tag, chunks, width, blocks, up, down, unroll, shared=False):
    U, C, NP = unroll, chunks, blocks // 2
    NB = 3
    ITERS = TILES // U
    bank_of = [j % NB for j in range(U * C)]

    def since(j):
        return next(d for d in range(1, U * C + 1) if bank_of[(j - d) % (U * C)] == bank_of[j])

    def covers(p):
        return min(-(-256 * (p + 1) // width), C) - 1

    def last_pair(c):
        return min(((c + 1) * width - 1) // 256, NP - 1)

    transpose_at, down_at = {}, {}
    for u in range(U):
        for p in range(NP):
            j = u * C + covers(p) + 2
            while len(transpose_at.get(j, [])) >= 1 and NP > 4:
                j += 1
            transpose_at.setdefault(j, []).append((u, p))
            down_at.setdefault(j + 2, []).append((u, p))
    ends = {max(j for j, l in down_at.items() if (u, NP - 1) in l) + 1: u for u in range(U)}
    STEPS = max(max(down_at), max(ends)) + 1

    with ExitStack() as ctx:
        def sb(name, shape, dt=F32):
            return ctx.enter_context(nc.sbuf_tensor(tag + name, shape, dt))

        def sem(name):
            return ctx.enter_context(nc.semaphore(tag + name))

        xc = sb("xc", [P, 2, H])
        xhi = sb("xhi", [P, 2, KT * P], F16)
        xlo = sb("xlo", [P, 2, KT * P], F16)
        sil = sb("sil", [P, NB, width])
        hid = sb("hid", [P, blocks * P])
        hhi = sb("hhi", [P, 2, 256], F16)
        hlo = sb("hlo", [P, 2, 256], F16)
        res = sb("res", [P, 2, H])
        st = sb("st", [P, 2, 6])
        mv = sb("mv", [P, 2, 2])
        std = sb("std", [P, 2])
        rstd = sb("rstd", [P, 2])
        copied = sem("copied")
        x_turned = sem("x_turned")
        x_hi = sem("x_hi")
        x_lo = sem("x_lo")
        up_done = sem("up_done")
        sil_done = sem("sil_done")
        hid_done = sem("hid_done")
        turned = sem("turned")
        h_hi = sem("h_hi")
        h_lo = sem("h_lo")
        down_done = sem("down_done")
        summed = sem("summed")
        std_done = sem("std_done")
        chain = sem("norm_chain")
        passed = k.vector_waits
        zeroed = sem("zeroed")
        stored = sem("stored")
        ps = k.ps
        slots = k.slot[:, :, :].rearrange("p t j -> p (t j)")
        assert U % 2 == 0
        block = ctx.enter_context(nc.Block())

        if shared:
            split = sb("split", [P, U, 2 * H], F16)
            slot = sb("slot", [P, U, TOPK], I32)
            split_hi, scatter_waits = sem("split_hi"), k.pool_waits
            split_lo = sem("split_lo")
            scattered = [sem(f"scattered{c}") for c in range(CHAINS)]
            spread = sem("spread")
            ROUNDS = U // CHAINS
        else:
            @block.sync
            def _(sp):
                with sp.Fori(0, ITERS) as i:
                    for u in range(U):
                        sp.wait_ge(chain, (i * U + u + 1) * 4)
                        sp.dma_start(k.d_out[bass.ds(i * U + u, 1)].rearrange("t p h -> p (t h)"),
                                     k.x[:, bass.ds(i * (U * H) + u * H, H)]).then_inc(stored, 16)
                sp.wait_ge(stored, 16 * TILES)

        @block.gpsimd
        def _(pool):
            if blocks * P > C * width:
                nc.gpsimd.memset(hid[:, C * width:], 0.0).then_inc(zeroed, 1)
            if shared:
                pool.sem_inc(spread, ROUNDS)
            pool.wait_ge(x_turned, 1)
            nc.gpsimd.tensor_copy(xc[:, 0, :], k.x[:, 0:H]).then_inc(copied, 1)

            def scatter(i, q, j):
                for c in range(CHAINS):
                    u = q * CHAINS + c
                    before = i * (16 * TOPK * ROUNDS) + 16 * (q * TOPK + j)
                    if not (isinstance(before, int) and before == 0):
                        pool.wait_ge(scattered[c], before)
                        pool.sem_inc(spread if (c, j) == (CHAINS - 1, 0) else scatter_waits, 1)
                    if j == 0:
                        hold(pool, split_lo, i * U + u + 3, scatter_waits)
                    nc.gpsimd.indirect_dma_start(k.d_slots[c],
                                                 bass.IndirectOffsetOnAxis(slot[:, u, j:j + 1], 0),
                                                 split[:, u, :], None).then_inc(scattered[c], 16)

            def body(i):
                for q in range(ROUNDS):
                    for j in range(TOPK):
                        scatter(i, q, j)

            if shared:
                body(0)
                with pool.Fori(1, ITERS) as i:
                    body(i)
                for c in range(CHAINS):
                    pool.wait_ge(scattered[c], 16 * TOPK * ROUNDS * ITERS)
                    pool.sem_inc(scatter_waits, 1)
            else:
                with pool.Fori(0, ITERS) as i:
                    for u in range(U):
                        pool.wait_ge(x_turned, i * U + u + 1)
                        nc.gpsimd.tensor_copy(xc[:, (u + 1) % 2, :],
                                              k.x[:, bass.ds(i * (U * H) + (u + 1) * H, H)]).then_inc(copied, 1)

        def x_turn(pe, u):
            for m in range(KT):
                last = nc.tensor.transpose(ps[:, 7, m * P:(m + 1) * P], xc[:, u % 2, m * P:(m + 1) * P],
                                           k.ident[:, :])
            last.then_inc(x_turned, 1)

        @block.tensor
        def _(pe):
            pe.sem_inc(x_turned, 1)
            pe.sem_inc(turned, NP)
            pe.sem_inc(down_done, 2)
            if blocks * P > C * width:
                pe.wait_ge(zeroed, 1)
            pe.wait_ge(copied, 1)
            x_turn(pe, 0)
            with pe.Fori(0, ITERS) as i:
                for j in range(STEPS):
                    u, c = j // C, j % C
                    if j < U * C:
                        if c == 0:
                            pe.wait_ge(x_lo, i * U + u + 1)
                        pe.wait_ge(hid_done, i * (U * C) + j + 1 - since(j) + NB)
                        for m in range(KT):
                            last = split_matmul(nc, ps[:, bank_of[j], 0:2 * width],
                                                [a[:, u % 2, m * P:(m + 1) * P] for a in (xhi, xlo)],
                                                [w[:, m, c, :] for w in up], m == 0, m == KT - 1)
                        last.then_inc(up_done, 1)
                        if c == C // 2:
                            pe.wait_ge(copied, i * U + u + 2)
                            x_turn(pe, u + 1)
                    for uu, p in down_at.get(j, []):
                        pe.wait_ge(h_lo, i * (U * NP) + uu * NP + p + 3)
                        if p == 0:
                            pe.wait_ge(summed, i * U + uu + 1)
                        for b in range(2):
                            last = split_matmul(nc, ps[:, 5 + uu % 2, 0:H],
                                                [a[:, p % 2, b * P:(b + 1) * P] for a in (hhi, hlo)],
                                                [w[:, 2 * p + b, :] for w in down],
                                                p == 0 and b == 0, p == NP - 1 and b == 1)
                        last.then_inc(down_done, 1)
                    for uu, p in transpose_at.get(j, []):
                        pe.wait_ge(hid_done, i * (U * C) + uu * C + covers(p) + 1 + NB)
                        pe.wait_ge(h_lo, i * (U * NP) + uu * NP + p + 1)
                        for b in range(2):
                            last = nc.tensor.transpose(ps[:, 3 + p % 2, b * P:(b + 1) * P],
                                                       hid[:, (2 * p + b) * P:(2 * p + b + 1) * P],
                                                       k.ident[:, :])
                        last.then_inc(turned, 1)

        @block.scalar
        def _(act):
            act.wait_ge(x_turned, 2)
            nc.scalar.activation(xhi[:, 0, :], ps[:, 7, 0:H], ACT.Copy).then_inc(x_hi, 1)
            with act.Fori(0, ITERS) as i:
                for j in range(STEPS):
                    u, c = j // C, j % C
                    if shared and j < U * C and c == 1:
                        act.wait_ge(copied, i * U + u + 1)
                        act.wait_ge(spread, i * ROUNDS + u // CHAINS + 1)
                        nc.scalar.activation(split[:, u, 0:H], xc[:, u % 2, :], ACT.Copy).then_inc(split_hi, 1)
                    if j < U * C:
                        act.wait_ge(up_done, i * (U * C) + j + 1)
                        nc.scalar.activation(sil[:, bank_of[j], :], ps[:, bank_of[j], 0:width], ACT.Silu)\
                            .then_inc(sil_done, 1)
                        if c == C // 2:
                            act.wait_ge(x_turned, i * U + u + 3)
                            nc.scalar.activation(xhi[:, (u + 1) % 2, :], ps[:, 7, 0:H], ACT.Copy)\
                                .then_inc(x_hi, 1)
                    for uu, p in transpose_at.get(j, []):
                        act.wait_ge(turned, i * (U * NP) + uu * NP + p + 1 + NP)
                        act.wait_ge(down_done, i * (U * NP) + uu * NP + p + 1)
                        nc.scalar.activation(hhi[:, p % 2, :], ps[:, 3 + p % 2, 0:256], ACT.Copy)\
                            .then_inc(h_hi, 1)
                    if j in ends and not shared:
                        uu = ends[j]
                        act.wait_ge(chain, i * (4 * U) + 4 * uu + 2)
                        nc.scalar.activation(std[:, uu % 2:uu % 2 + 1], mv[:, uu % 2, 1:2], ACT.Sqrt,
                                             bias=k.eps[:, 0:1]).then_inc(std_done, 1)

        @block.vector
        def _(dve):
            dve.sem_inc(hid_done, NB)
            dve.sem_inc(h_lo, 2)
            dve.sem_inc(summed, 2)
            if shared:
                dve.sem_inc(split_lo, 2)
            dve.wait_ge(x_hi, 1)
            nc.vector.tensor_tensor(xlo[:, 0, :], ps[:, 7, 0:H], xhi[:, 0, :], ALU.subtract).then_inc(x_lo, 1)
            with dve.Fori(0, ITERS) as i:
                for j in range(STEPS):
                    u, c = j // C, j % C
                    if shared and j < U * C and c == 1:
                        dve.wait_ge(split_hi, i * U + u + 1)
                        nc.vector.tensor_tensor(split[:, u, H:2 * H], xc[:, u % 2, :], split[:, u, 0:H], ALU.subtract)
                        nc.vector.tensor_copy(slot[:, u, :],
                                              slots[:, bass.ds(i * (U * TOPK) + u * TOPK, TOPK)])\
                            .then_inc(split_lo, 1)
                        dve.wait_ge(x_turned, i * U + u + 1)
                        dve.wait_ge(split_lo, i * U + u + 2)
                        nc.vector.tensor_copy(xc[:, (u + 1) % 2, :],
                                              k.x[:, bass.ds(i * (U * H) + (u + 1) * H, H)]).then_inc(copied, 1)
                    if j < U * C:
                        dve.wait_ge(sil_done, i * (U * C) + j + 1)
                        dve.wait_ge(turned, i * (U * NP) + u * NP + last_pair(c) + 1)
                        out = hid[:, c * width:(c + 1) * width]
                        upper = ps[:, bank_of[j], width:2 * width]
                        if not shared:
                            nc.vector.tensor_tensor(out, sil[:, bank_of[j], :], upper, ALU.mult)\
                                .then_inc(hid_done, 1)
                        else:
                            nc.vector.scalar_tensor_tensor(
                                out=out, in0=sil[:, bank_of[j], :],
                                scalar=k.gate[:, bass.ds(i * U + u, 1)], in1=upper,
                                op0=ALU.mult, op1=ALU.mult).then_inc(hid_done, 1)
                        if c == C // 2:
                            dve.wait_ge(x_hi, i * U + u + 2)
                            nc.vector.tensor_tensor(xlo[:, (u + 1) % 2, :], ps[:, 7, 0:H],
                                                    xhi[:, (u + 1) % 2, :], ALU.subtract).then_inc(x_lo, 1)
                    for uu, p in transpose_at.get(j, []):
                        dve.wait_ge(h_hi, i * (U * NP) + uu * NP + p + 1)
                        nc.vector.tensor_tensor(hlo[:, p % 2, :], ps[:, 3 + p % 2, 0:256], hhi[:, p % 2, :],
                                                ALU.subtract).then_inc(h_lo, 1)
                    if j in ends:
                        uu = ends[j]
                        s = uu % 2
                        mine = k.x[:, bass.ds(i * (U * H) + uu * H, H)]
                        dve.wait_ge(down_done, i * (U * NP) + (uu + 1) * NP + 2)
                        if shared:
                            nc.vector.tensor_tensor(mine, ps[:, 5 + s, 0:H], mine, ALU.add).then_inc(summed, 1)
                            continue
                        nc.vector.tensor_tensor(res[:, s, :], ps[:, 5 + s, 0:H], mine, ALU.add)\
                            .then_inc(summed, 1)
                        dve.wait_ge(summed, i * U + uu + 3)
                        nc.vector.bn_stats(st[:, s, :], res[:, s, :]).then_inc(chain, 1)
                        hold(dve, chain, i * (4 * U) + 4 * uu + 1, passed)
                        nc.vector.bn_aggr(mv[:, s, :], st[:, s, :]).then_inc(chain, 1)
                        dve.wait_ge(std_done, i * U + uu + 1)
                        nc.vector.reciprocal(rstd[:, s:s + 1], std[:, s:s + 1]).then_inc(chain, 1)
                        dve.wait_ge(chain, i * (4 * U) + 4 * uu + 3)
                        nc.vector.tensor_scalar(mine, res[:, s, :], mv[:, s, 0:1], rstd[:, s:s + 1],
                                                ALU.subtract, ALU.mult).then_inc(chain, 1)

def expert_stage(nc, k, tag, chain=None, combine=None):
    ITERS = SLOT_TILES // BODY
    RING = LOADS_AHEAD
    PART = BODY // 2
    PARTS = SLOT_TILES // PART
    PER = CTILES // PARTS
    MIX = [f"mix{s}{j}" for s in range(PER) for j in range(TOPK)]
    MIX_AT, STATS_AT, SQRT_AT, OUT_AT = {0: (0, 0), 1: (0, 2), 2: (1, 0), 3: (1, 2)}, 4, 6, 8
    assert BODY % RING == 0 and BODY % 2 == 0 and CTILES % PARTS == 0

    with ExitStack() as ctx:
        def sb(name, shape, dt=F32):
            return ctx.enter_context(nc.sbuf_tensor(tag + name, shape, dt))

        def sem(name):
            return ctx.enter_context(nc.semaphore(tag + name))

        ps = k.ps
        if chain is not None:
            xs = sb("xs", [P, RING, 2 * H], F16)
            xt = sb("xt", [P, 2, 2, KT, P], F16)
            ident = sb("ident", [P, P], F16)
            sil = sb("sil", [P, 2, I_MOE])
            hid = sb("hid", [P, 2, EXPERT_BLOCKS * P])
            hhi = sb("hhi", [P, 2, EXPERT_BLOCKS * P], F16)
            hlo = sb("hlo", [P, 2, EXPERT_BLOCKS * P], F16)
            y = sb("y", [P, RING, H])
            loaded = [sem(f"loaded{r}") for r in range(RING)]
            stored = [sem(f"stored{r}") for r in range(RING)]
            prepared = sem("prepared")
            x_turned, x_copied, up_done, sil_done, hid_done, turned, h_hi, h_lo, down_done, y_done = (
                Count(sem(n)) for n in ("x_turned", "x_copied", "up_done", "sil_done", "hid_done", "turned",
                                        "h_hi", "h_lo", "down_done", "y_done"))
            prep = Layer1Split(nc, ctx, k, PARTS) if chain == 0 else None
            FT = TILES // ITERS
            picked, total = sb("picked", [P, FT, E]), sb("total", [P, FT])
            factors = Steps(sem("factor_steps"), ["sum", "cap", "inverse", "share"]
                            + [w + str(j) for j in range(TOPK) for w in ("pick", "take")])
        if combine is not None:
            got = sb("got", [P, PER, TOPK * H])
            slot = sb("slot", [P, PER, TOPK], I32)
            res = sb("res", [P, PER, H])
            st = sb("st", [P, PER, 6])
            mv = sb("mv", [P, PER, 2])
            std = sb("std", [P, PER])
            rstd = sb("rstd", [P, PER])
            gathered = [sem(f"gathered{s}") for s in range(PER)]
            slots_here, gather_waits = sem("slots_here"), k.pool_waits
            mix = Steps(sem("mix_steps"), MIX + ["stats", "mv", "rstd", "out"])
            root = Steps(sem("root_steps"), ["std"])
            passed = k.vector_waits
        fold = Layer1Fold(nc, ctx, k) if chain is None else None
        block = ctx.enter_context(nc.Block())

        if fold:
            @block.sync
            def _(sp):
                fold.load(sp)

            @block.tensor
            def _(pe):
                fold.multiply(pe)

        def wait(eng, count, n):
            eng.wait_ge(count.sem, count.after(n))

        if chain is not None:
            @block.sync
            def _(sp):
                def load(n, r):
                    sp.dma_start(xs[:, r, :], k.d_slots[chain][bass.ds(n * P, P)]).then_inc(loaded[r], 16)

                for r in range(RING):
                    load(r, r)
                with sp.Fori(0, ITERS) as i:
                    for s in range(BODY):
                        n, r = i * BODY + s, s % RING
                        if prep and s % PART == 0:
                            prep.load(sp, i * 2 + s // PART)
                        wait(sp, x_turned, n)
                        load(n + RING, r)
                        wait(sp, y_done, n)
                        sp.dma_start(k.d_y[chain][bass.ds(n * P, P)], y[:, r, :]).then_inc(stored[r], 16)
                for r in range(RING):
                    sp.wait_ge(stored[r], 16 * (SLOT_TILES // RING + 1))
                    sp.wait_ge(loaded[r], 16 * (SLOT_TILES // RING + 1))

            @block.tensor
            def _(pe):
                def load_experts(first, count):
                    row = k.expert[0:1, bass.ds(first + chain * P, count)]
                    return nc.values_load_multi_w_load_instructions(row, engines=[mybir.EngineType.PE],
                                                                    min_val=0, max_val=E - 1)[1]

                def turn_x(n, r, turn, par):
                    pe.wait_ge(loaded[r], turn)
                    wait(pe, x_copied, n - 2)
                    for h in range(2):
                        for m in range(KT):
                            last = nc.tensor.matmul(ps[:, par, (h * KT + m) * P:(h * KT + m + 1) * P],
                                                    xs[:, r, h * H + m * P:h * H + (m + 1) * P], ident[:, :],
                                                    start=True, stop=True, skip_group_check=True)
                    last.then_inc(x_turned.sem, 1)

                def gate_up(n, par, expert):
                    wait(pe, x_copied, n)
                    wait(pe, hid_done, n - 2)
                    for m in range(KT):
                        cols = bass.ds(expert * (2 * I_MOE) + m * (SLICES * 2 * I_MOE), 2 * I_MOE)
                        last = split_matmul(nc, ps[:, 2 + par, 0:2 * I_MOE], [xt[:, par, h, m, :] for h in range(2)],
                                            [w[:, cols] for w in (k.moe_hi, k.moe_lo)], m == 0, m == KT - 1)
                    last.then_inc(up_done.sem, 1)

                def turn_hidden(n, par):
                    wait(pe, hid_done, n)
                    wait(pe, h_lo, n - 2)
                    for b in range(EXPERT_BLOCKS):
                        last = nc.tensor.transpose(ps[:, 4 + par, b * P:(b + 1) * P],
                                                   hid[:, par, b * P:(b + 1) * P], k.ident[:, :])
                    last.then_inc(turned.sem, 1)

                def multiply_down(n, par, expert):
                    wait(pe, h_lo, n)
                    wait(pe, y_done, n - 2)
                    for b in range(EXPERT_BLOCKS):
                        cols = bass.ds(expert * (EXPERT_BLOCKS * H) + C_GU + b * H, H)
                        last = split_matmul(nc, ps[:, 6 + par, 0:H],
                                            [a[:, par, b * P:(b + 1) * P] for a in (hhi, hlo)],
                                            [w[:, cols] for w in (k.moe_hi, k.moe_lo)], b == 0,
                                            b == EXPERT_BLOCKS - 1)
                    last.then_inc(down_done.sem, 1)

                for c in (x_turned, up_done, turned, down_done):
                    c.start(pe)
                pe.wait_ge(prepared, 1)
                begin = load_experts(0, 2)
                turn_x(0, 0, 16, 0)
                turn_x(1, 1, 16, 1)
                gate_up(0, 0, begin[0])
                turn_x(2, 2, 16, 0)
                gate_up(1, 1, begin[1])
                turn_hidden(0, 0)
                with pe.Fori(0, ITERS) as i:
                    experts = list(load_experts(i * BODY, 2))
                    for s in range(BODY):
                        n = i * BODY + s
                        experts += load_experts(n + 2, 1)
                        turn_x(n + 3, (s + 3) % RING, i * (16 * BODY // RING) + 16 * ((s + 3) // RING + 1),
                               (s + 3) % 2)
                        gate_up(n + 2, s % 2, experts[s + 2])
                        turn_hidden(n + 1, (s + 1) % 2)
                        multiply_down(n, s % 2, experts[s])

        @block.gpsimd
        def _(pool):
            if chain is not None:
                nc.gpsimd.memset(hid[:, :, I_MOE:], 0.0)
                nc.gpsimd.tensor_copy(ident[:, :], k.ident[:, :]).then_inc(prepared, 1)
                if prep:
                    prep.start(pool)
            with pool.Fori(0, PARTS) as i:
                if combine is not None:
                    for s in range(PER):
                        at = i * (PER * CHAINS * TOPK) + (s * CHAINS + combine) * TOPK
                        pool.wait_ge(mix.sem, mix.after(i - 1, f"mix{s}{TOPK - 1}"))
                        nc.gpsimd.tensor_copy(slot[:, s, :],
                                              k.slot[:, :, :].rearrange("p t j -> p (t j)")[:, bass.ds(at, TOPK)])\
                            .then_inc(slots_here, 1)
                        hold(pool, slots_here, i * PER + s + 1, gather_waits)
                        for j in range(TOPK):
                            nc.gpsimd.indirect_dma_start(got[:, s, j * H:(j + 1) * H], None, k.d_y[combine],
                                                         bass.IndirectOffsetOnAxis(slot[:, s, j:j + 1], 0))\
                                .then_inc(gathered[s], 16)
                if chain is not None and prep:
                    prep.split(pool, i)

        @block.scalar
        def _(act):
            def copy_x(n, par):
                wait(act, x_turned, n)
                wait(act, up_done, n - 2)
                nc.scalar.activation(xt[:, par, :, :, :].rearrange("p a m t -> p (a m t)"), ps[:, par, :],
                                     ACT.Copy).then_inc(x_copied.sem, 1)

            def silu(n, par):
                wait(act, up_done, n)
                wait(act, hid_done, n - 2)
                nc.scalar.activation(sil[:, par, :], ps[:, 2 + par, 0:I_MOE], ACT.Silu).then_inc(sil_done.sem, 1)

            def split_hi(n, par):
                wait(act, turned, n)
                wait(act, down_done, n - 2)
                nc.scalar.activation(hhi[:, par, :], ps[:, 4 + par, 0:EXPERT_BLOCKS * P], ACT.Copy)\
                    .then_inc(h_hi.sem, 1)

            if chain is not None:
                for c in (x_copied, sil_done, h_hi):
                    c.start(act)
                copy_x(0, 0)
                copy_x(1, 1)
                silu(0, 0)
                copy_x(2, 0)
                silu(1, 1)
                split_hi(0, 0)
            if combine is not None:
                root.start(act)
            with act.Fori(0, ITERS) as i:
                for s in range(BODY):
                    n = i * BODY + s
                    if chain is not None:
                        silu(n + 2, s % 2)
                        copy_x(n + 3, (s + 3) % 2)
                        split_hi(n + 1, (s + 1) % 2)
                    if combine is not None and s % PART == SQRT_AT:
                        act.wait_ge(mix.sem, mix.after(i * 2 + s // PART, "mv"))
                        nc.scalar.activation(std[:, :], mv[:, :, 1], ACT.Sqrt, bias=k.eps[:, 0:1])\
                            .then_inc(root.sem, 1)
            if fold:
                fold.split_hi(act)

        @block.vector
        def _(dve):
            def hidden(n, par):
                wait(dve, sil_done, n)
                wait(dve, turned, n - 2)
                nc.vector.tensor_tensor(hid[:, par, 0:I_MOE], sil[:, par, :], ps[:, 2 + par, I_MOE:2 * I_MOE],
                                        ALU.mult).then_inc(hid_done.sem, 1)

            def split_lo(n, par):
                wait(dve, h_hi, n)
                nc.vector.tensor_tensor(hlo[:, par, :], ps[:, 4 + par, 0:EXPERT_BLOCKS * P], hhi[:, par, :],
                                        ALU.subtract).then_inc(h_lo.sem, 1)

            def keep(n, par, r, turn):
                wait(dve, down_done, n)
                dve.wait_ge(stored[r], turn)
                nc.vector.tensor_copy(y[:, r, :], ps[:, 6 + par, 0:H]).then_inc(y_done.sem, 1)

            if chain is not None:
                for c in (hid_done, h_lo, y_done):
                    c.start(dve)
                for r in range(RING):
                    dve.sem_inc(stored[r], 16)
                hidden(0, 0)
                hidden(1, 1)
                split_lo(0, 0)
            if combine is not None:
                mix.start(dve)

            def tile_of(i, s):
                return k.x[:, bass.ds(i * (PER * CHAINS * H) + (s * CHAINS + combine) * H, H)]

            def combine_step(i, s):
                if s in MIX_AT:
                    t, first = MIX_AT[s]
                    for j in range(first, first + 2):
                        if j == 0:
                            dve.wait_ge(gathered[t], i * (16 * TOPK) + 16 * TOPK)
                            dve.wait_ge(mix.sem, mix.after(i - 1, "out"))
                        else:
                            dve.wait_ge(mix.sem, mix.after(i, f"mix{t}{j - 1}"))
                        at = i * (PER * CHAINS * TOPK) + (t * CHAINS + combine) * TOPK + j
                        nc.vector.scalar_tensor_tensor(
                            out=res[:, t, :], in0=got[:, t, j * H:(j + 1) * H],
                            scalar=k.weight[:, :, :].rearrange("p t j -> p (t j)")[:, bass.ds(at, 1)],
                            in1=tile_of(i, t) if j == 0 else res[:, t, :], op0=ALU.mult, op1=ALU.add)\
                            .then_inc(mix.sem, 1)
                if s == STATS_AT:
                    dve.wait_ge(mix.sem, mix.after(i, MIX[-1]))
                    for t in range(PER):
                        last = nc.vector.bn_stats(st[:, t, :], res[:, t, :])
                    last.then_inc(mix.sem, 1)
                    hold(dve, mix.sem, mix.after(i, "stats"), passed)
                    for t in range(PER):
                        last = nc.vector.bn_aggr(mv[:, t, :], st[:, t, :])
                    last.then_inc(mix.sem, 1)
                if s == OUT_AT:
                    dve.wait_ge(root.sem, root.after(i, "std"))
                    nc.vector.reciprocal(rstd[:, :], std[:, :]).then_inc(mix.sem, 1)
                    dve.wait_ge(mix.sem, mix.after(i, "rstd"))
                    for t in range(PER):
                        last = nc.vector.tensor_scalar(tile_of(i, t), res[:, t, :], mv[:, t, 0:1],
                                                       rstd[:, t:t + 1], ALU.subtract, ALU.mult)
                    last.then_inc(mix.sem, 1)

            if chain == 0:
                factors.start(dve)

            def factor_step(i, s):
                if s >= len(factors.names):
                    return

                def mine(t):
                    return t[:, :, :].rearrange("p t e -> p (t e)")[:, bass.ds(i * (FT * E), FT * E)]

                def by_tile(t):
                    return mine(t).rearrange("p (t e) -> p t e", e=E)

                if s:
                    dve.wait_ge(factors.sem, factors.after(i, factors.names[s - 1]))
                else:
                    dve.wait_ge(factors.sem, factors.after(i - 1, factors.names[-1]))
                if s == 0:
                    ins = nc.vector.tensor_reduce(total[:, :], by_tile(k.share), AX_X, ALU.add)
                elif s == 1:
                    ins = nc.vector.tensor_scalar_max(total[:, :], total[:, :], 1e-9)
                elif s == 2:
                    ins = nc.vector.reciprocal(total[:, :], total[:, :])
                elif s == 3:
                    ins = nc.vector.tensor_tensor(by_tile(k.share), by_tile(k.share),
                                                  total[:, :].unsqueeze(2).broadcast_to([P, FT, E]), ALU.mult)
                elif s % 2 == 0:
                    ins = nc.vector.scalar_tensor_tensor(
                        out=picked[:, :, :].rearrange("p t e -> p (t e)"), in0=mine(k.order),
                        scalar=float(s // 2 - 1), in1=mine(k.share), op0=ALU.is_equal, op1=ALU.mult)
                else:
                    out = k.weight[:, :, :].rearrange("p t j -> p (t j)")[:, bass.ds(i * (FT * TOPK), FT * TOPK)]
                    ins = nc.vector.tensor_reduce(out.rearrange("p (t j) -> p t j", j=TOPK)[:, :, s // 2 - 2],
                                                  picked[:, :, :], AX_X, ALU.add)
                ins.then_inc(factors.sem, 1)

            with dve.Fori(0, ITERS) as i:
                for s in range(BODY):
                    n, r = i * BODY + s, s % RING
                    if chain == 0:
                        factor_step(i, s)
                    if chain is not None:
                        hidden(n + 2, s % 2)
                        split_lo(n + 1, (s + 1) % 2)
                        keep(n, s % 2, r, i * (16 * BODY // RING) + 16 * (s // RING + 1))
                    if combine is not None:
                        combine_step(i * 2 + s // PART, s % PART)
            if fold:
                fold.split_lo(dve)


class Layer1Split:

    def __init__(self, nc, ctx, k, parts):
        self.nc, self.k, self.n = nc, k, C_L1 // parts
        assert C_L1 % parts == 0
        self.raw = ctx.enter_context(nc.sbuf_tensor("l1_raw", [P, self.n], F32))
        self.loaded = ctx.enter_context(nc.semaphore("l1_loaded"))
        self.hi_done = ctx.enter_context(nc.semaphore("l1_hi_done"))
        self.lo_done = ctx.enter_context(nc.semaphore("l1_lo_done"))

    def start(self, pool):
        pool.sem_inc(self.lo_done, 1)

    def load(self, sp, i):
        sp.wait_ge(self.lo_done, i + 1)
        sp.dma_start(self.raw[:, :], self.k.d_l1[:, bass.ds(i * self.n, self.n)]).then_inc(self.loaded, 16)

    def split(self, pool, i):
        nc, k = self.nc, self.k
        hi = k.l1_hi[:, bass.ds(i * self.n, self.n)]
        pool.wait_ge(self.loaded, (i + 1) * 16)
        nc.gpsimd.tensor_copy(hi, self.raw[:, :]).then_inc(self.hi_done, 1)
        pool.wait_ge(self.hi_done, i + 1)
        nc.gpsimd.tensor_tensor(k.l1_lo[:, bass.ds(i * self.n, self.n)], self.raw[:, :], hi, ALU.subtract)\
            .then_inc(self.lo_done, 1)


class Layer1Fold:

    def __init__(self, nc, ctx, k):
        self.nc, self.k = nc, k

        def sb(name, shape, dt=F32):
            return ctx.enter_context(nc.sbuf_tensor("fold_" + name, shape, dt))

        def sem(name):
            return ctx.enter_context(nc.semaphore("fold_" + name))

        self.raw = sb("raw", [P, FF_BLOCKS, H])
        self.had = sb("had", [P, 2, P])
        self.loaded, self.others, self.multiplied = sem("loaded"), sem("others_loaded"), sem("multiplied")
        self.hi_done, self.lo_done = sem("hi_done"), sem("lo_done")
        self.banks = FF_BLOCKS * H // 512

    def load(self, sp):
        k = self.k
        sp.dma_start(self.had[:, :, :], k.d_had).then_inc(self.loaded, 16)
        sp.dma_start(self.raw[:, :, :], k.d_w2).then_inc(self.loaded, 16)
        sp.dma_start(k.att_const[:, :], k.d_att).then_inc(self.others, 16)
        sp.dma_start(k.bias_flat, k.d_bias).then_inc(self.others, 16)
        sp.wait_ge(self.others, 32)

    def multiply(self, pe):
        nc, k = self.nc, self.k
        pe.wait_ge(self.loaded, 32)
        for c in range(FF_BLOCKS):
            for j in range(FF_BLOCKS):
                sign = bin(c & j).count("1") % 2
                last = nc.tensor.matmul(k.ps[:, c // 2, (c % 2) * H:(c % 2 + 1) * H], self.had[:, sign, :],
                                        self.raw[:, j, :], start=j == 0, stop=j == FF_BLOCKS - 1,
                                        skip_group_check=True)
            if c % 2:
                last.then_inc(self.multiplied, 1)

    def whole(self, w, b):
        return w[:, 2 * b:2 * b + 2, :].rearrange("p c h -> p (c h)")

    def split_hi(self, act):
        nc, k = self.nc, self.k
        for b in range(self.banks):
            act.wait_ge(self.multiplied, b + 1)
            nc.scalar.activation(self.whole(k.w2_hi, b), k.ps[:, b, :], ACT.Copy).then_inc(self.hi_done, 1)

    def split_lo(self, dve):
        nc, k = self.nc, self.k
        for b in range(self.banks):
            dve.wait_ge(self.hi_done, b + 1)
            nc.vector.tensor_tensor(self.whole(k.w2_lo, b), k.ps[:, b, :], self.whole(k.w2_hi, b),
                                    ALU.subtract).then_inc(self.lo_done, 1)


def attention_stage(nc, k):
    AU = 4
    PV = [(t, kt) for t in range(2) for kt in range(t + 1)]
    UNITS = [(t, g, kt) for t, kt in PV for g in range(KV)]
    NU, RING_E, RING_P = len(UNITS), 3, 2 * KV
    NAT = [(0, g, 0, REP) for g in range(KV)] + [(1, g, r, 2) for g in range(KV) for r in (0, 2)]
    NN = len(NAT)
    LAG = 2
    SLOTS = NU + LAG
    pv_at = {v: [p for p in range(len(PV)) if KV * p + KV - 1 == v - LAG] for v in range(SLOTS)}
    A_AT = {0: ["qkv"], 10: ["top"], 11: ["x"]}
    for u in range(NN):
        A_AT.setdefault(3 + u // 2, []).append(u)
    REC = 2
    DIV1_AT = {0: ["sum", "rec0"], 1: ["rec1", "out"]}
    DIV0_AT = {9: ["sum", "rec0", "rec1"], 11: ["out"]}
    WO_AT, RES_AT = 5, 7
    HI1_AT, LO1_AT, HI0_AT, LO0_AT = 3, 4, 12, 11
    COPY_AT = 4
    NORM_AT, SQRT_AT, OUT_AT = 8, 11, 12
    V1 = 2 * D

    with ExitStack() as ctx:
        def sb(name, shape, dt=F32):
            return ctx.enter_context(nc.sbuf_tensor("at_" + name, shape, dt))

        def sem(name):
            return ctx.enter_context(nc.semaphore("at_" + name))

        free = FF_BLOCKS * H
        bias = k.bias_flat.rearrange("p (g y r n) -> p g y r n", g=KV, y=2, r=REP)
        cst = sb("cst", [P, 2 * P], BF16)
        eye, mask = cst[:, 0:P], cst[:, P:2 * P]
        negate = k.att_const[:, 0:1]
        xc = sb("xc", [P, 2 * H])
        xhi = sb("xhi", [P, KT, T], F16)
        xlo = sb("xlo", [P, KT, T], F16)
        qh = sb("qh", [P, REP, T], F16)
        q_ = sb("q", [P, 2, REP, T], F16)
        v1_ = sb("v1", [P, 2, 2, KV, V1])
        top = sb("top", [P, 2, KV, SLOT])
        shift_ = sb("shift", [P, 2, 2 * P], BF16)
        taken = [free + 4 * HEADS * P, free]

        def there(which, dt, *dims):
            size = int(np.prod(dims)) * (2 if dt == F32 else 1)
            whole = (k.moe_hi, k.moe_lo)[which][:, taken[which]:taken[which] + size]
            taken[which] += size
            names = " ".join("abcd"[:len(dims)])
            return whole.bitcast(dt).rearrange(f"p ({names}) -> p {names}", **dict(zip("abcd", dims)))

        ex = there(1, F32, RING_E, REP * P)
        pr = there(1, F32, RING_P, REP * P)
        kh_, kl_ = (there(0, F16, 2, KV, T) for _ in range(2))
        pick = there(0, BF16, KV, REP, P)
        rec = sb("rec", [P, 2, REP * P])
        o = sb("o", [P, 2, REP * P])
        ohi = sb("ohi", [P, 2, REP, P], F16)
        olo = sb("olo", [P, 2, REP, P], F16)
        res = there(0, F32, AU, 2 * H)
        st = sb("st", [P, 2 * AU, 6])
        mv = sb("mv", [P, 2 * AU, 2])
        std = sb("std", [P, 2 * AU])
        rstd = sb("rstd", [P, 2 * AU])
        nat_names, unit_names = [f"max{u}" for u in range(NN)], [f"unit{v}" for v in range(NU)]
        a_vec = Steps(sem("a_vector_steps"), ["xlo", "klo", "q0", "q1"] + nat_names)
        a_sca = Steps(sem("a_scalar_steps"), ["xhi", "khi", "v", "qhi0", "qhi1", "shift"])
        a_pen = Steps(sem("a_tensor_steps"), ["xT", "kv", "q0", "q1"] + nat_names + ["maxT"])
        a_pol = Steps(sem("a_pool_steps"), ["copy"])
        scores = Steps(sem("b_scores"), unit_names)
        exps = Steps(sem("b_exps"), unit_names)
        probs = Steps(sem("b_probs"), unit_names)
        pvs = Steps(sem("b_pv"), [f"pv{n}" for n in range(len(PV))])
        div = [Steps(sem(f"c_divide{t}"), ["sum"] + [f"rec{j}" for j in range(REC)] + ["out"]) for t in range(2)]
        c_vec = Steps(sem("c_vector_steps"), ["res", "stats"])
        c_sca = Steps(sem("c_scalar_steps"), ["ohi0", "ohi1"])
        c_pol = Steps(sem("c_pool_steps"), ["olo0", "olo1"])
        c_pen = Steps(sem("c_tensor_steps"), ["wo"])
        norm_vec = Steps(sem("norm_vector_steps"), ["mv", "rstd", "out"])
        norm_sca = Steps(sem("norm_scalar_steps"), ["std"])
        ready, passed = sem("constants_ready"), k.vector_waits
        cleared = sem("constants_cleared")
        ps = k.ps
        at = [0]
        w = []
        for n, dims in ((C_Q, (REP, P)), (C_K, (1, P)), (C_V, (1, KV * D)), (C_O, (REP, H))):
            w.append([s[:, at[0]:at[0] + n].rearrange("p (m r n) -> p m r n", r=dims[0], n=dims[1])
                      for s in (k.l1_hi, k.l1_lo)])
            at[0] += n
        wq, wk, wv, wo = w
        block = ctx.enter_context(nc.Block())

        def slot(g):
            return slice(SLOT * g, SLOT * (g + 1))

        def wait(eng, steps, n, name):
            eng.wait_ge(steps.sem, steps.after(n, name))

        @block.gpsimd
        def _(pool):
            for s in (a_pol, probs, c_pol):
                s.start(pool)
            nc.gpsimd.memset(top[:, :, :, :], 0.0)
            nc.gpsimd.memset(v1_[:, :, :, :, D:V1], 1.0)
            nc.gpsimd.memset(pick, 0.0).then_inc(cleared, 1)
            for g in range(KV):
                pool.wait_ge(cleared, g + 1)
                nc.gpsimd.tensor_copy(pick[slot(g), g, :, :],
                                      k.att_const[slot(g), 1 + 2 * P:].rearrange("p (r n) -> p r n", r=REP))\
                    .then_inc(cleared, 1)
            pool.wait_ge(cleared, KV + 1)
            nc.gpsimd.tensor_copy(cst[:, :], k.att_const[:, 1:1 + 2 * P]).then_inc(ready, 1)

            def phase_a(n):
                wait(pool, a_pen, n - 1, "xT")
                nc.gpsimd.tensor_copy(xc[:, :], k.x[:, bass.ds(n * (2 * H), 2 * H)]).then_inc(a_pol.sem, 1)

            def split_lo(n, t):
                wait(pool, c_sca, n, f"ohi{t}")
                wait(pool, c_pen, n - 1, "wo")
                nc.gpsimd.tensor_tensor(olo[:, t, :, :].rearrange("p r n -> p (r n)"), o[:, t, :],
                                        ohi[:, t, :, :].rearrange("p r n -> p (r n)"), ALU.subtract)\
                    .then_inc(c_pol.sem, 1)

            phase_a(0)
            split_lo(0, 0)
            phase_a(1)
            with pool.Fori(0, SEQS // AU) as i:
                for s in range(AU):
                    n = i * AU + s
                    for v, (t, g, kt) in enumerate(UNITS):
                        wait(pool, exps, n, f"unit{v}")
                        wait(pool, pvs, n if v >= RING_P else n - 1, f"pv{len(PV) - 1 - v // KV}")
                        nc.gpsimd.tensor_tensor(pr[:, v % RING_P, :], ex[:, v % RING_E, :],
                                                bias[:, g, t - kt, :, :].rearrange("p r n -> p (r n)"), ALU.mult)\
                            .then_inc(probs.sem, 1)
                        if v == LO1_AT:
                            split_lo(n, 1)
                        if v == COPY_AT:
                            phase_a(n + 2)
                        if v == LO0_AT:
                            split_lo(n + 1, 0)
            split_lo(SEQS, 1)

        @block.tensor
        def _(pe):
            for s in (a_pen, scores, pvs, c_pen):
                s.start(pe)
            pe.wait_ge(ready, 2)

            def phase_a(step, n, par):
                q, kh = q_[:, par], kh_[:, par]
                if step == "x":
                    wait(pe, a_pol, n, "copy")
                    wait(pe, a_sca, n - 1, "shift")
                    for m in range(KT):
                        for t in range(2):
                            last = nc.tensor.transpose(ps[:, 0, m * T + t * P:m * T + (t + 1) * P],
                                                       xc[:, t * H + m * P:t * H + (m + 1) * P], k.ident[:, :])
                    last.then_inc(a_pen.sem, 1)
                elif step == "qkv":
                    wait(pe, a_vec, n, "xlo")
                    for m in range(KT):
                        split_matmul(nc, ps[:, 0, 0:T], [s[:, m, 0, :] for s in wk],
                                     [s[:, m, :] for s in (xhi, xlo)], m == 0, m == KT - 1)
                    for t in range(2):
                        for m in range(KT):
                            last = split_matmul(nc, ps[:, 0, T + t * KV * D:T + (t + 1) * KV * D],
                                                [s[:, m, t * P:(t + 1) * P] for s in (xhi, xlo)],
                                                [s[:, m, 0, :] for s in wv], m == 0, m == KT - 1)
                    last.then_inc(a_pen.sem, 1)
                    wait(pe, a_vec, n - 1, f"max{NN - 1}")
                    for r in range(REP):
                        for m in range(KT):
                            last = split_matmul(nc, ps[:, 1 + r // 2, (r % 2) * T:(r % 2 + 1) * T],
                                                [s[:, m, r, :] for s in wq], [s[:, m, :] for s in (xhi, xlo)],
                                                m == 0, m == KT - 1)
                        if r % 2:
                            last.then_inc(a_pen.sem, 1)
                elif step == "top":
                    wait(pe, a_vec, n, f"max{NN - 1}")
                    for t in range(2):
                        last = nc.tensor.transpose(ps[:, 0, t * P:(t + 1) * P],
                                                   top[:, t, :, :].rearrange("p g s -> p (g s)"), k.ident[:, :])
                    last.then_inc(a_pen.sem, 1)
                else:
                    u = step
                    t, g, r0, heads = NAT[u]
                    if u == 0:
                        wait(pe, a_vec, n, "q1")
                        wait(pe, a_sca, n, "khi")
                    if u >= 2:
                        wait(pe, a_vec, n, f"max{u - 2}")
                    nk = P * (t + 1)
                    out = ps[:, 1 + u % 2, :].rearrange("p (r n) -> p r n", n=nk)
                    nc.tensor.matmul(out[:, :, nk - P:nk], eye, mask.unsqueeze(1).broadcast_to([P, heads, P]),
                                     start=True, stop=False, skip_group_check=True)
                    for r in range(heads):
                        last = nc.tensor.matmul(out[:, r, :], q[:, r0 + r, t * P:(t + 1) * P],
                                                kh[:, g, 0:nk], start=False, stop=r == heads - 1,
                                                skip_group_check=True)
                    last.then_inc(a_pen.sem, 1)

            def multiply_values(n, par, p):
                t, kt = PV[p]
                wait(pe, probs, n, f"unit{KV * p + KV - 1}")
                if p < 2:
                    wait(pe, div[p], n, "out")
                for g in range(KV):
                    last = nc.tensor.matmul(ps[slot(g), 6 + t, :], v1_[:, par, kt, g, :],
                                            pr[:, (KV * p + g) % RING_P, :], start=kt == 0, stop=kt == t,
                                            skip_group_check=True, tile_position=(0, SLOT * g))
                last.then_inc(pvs.sem, 1)

            def project(n):
                wait(pe, c_pol, n, "olo1")
                wait(pe, c_vec, n - 1, "res")
                for t in range(2):
                    for r in range(REP):
                        last = split_matmul(nc, ps[:, 5, t * H:(t + 1) * H], [s[:, t, r, :] for s in (ohi, olo)],
                                            [s[:, 0, r, :] for s in wo], r == 0, r == REP - 1)
                last.then_inc(c_pen.sem, 1)

            phase_a("x", 0, 0)
            for v in range(SLOTS):
                for step in A_AT.get(v, []):
                    phase_a(step, 1 if step == "x" else 0, 0)
            with pe.Fori(0, SEQS // AU) as i:
                for s in range(AU):
                    n, par = i * AU + s, s % 2
                    q, keys = q_[:, par], (kh_[:, par], kl_[:, par])
                    for v in range(SLOTS):
                        if v < NU:
                            t, g, kt = UNITS[v]
                            if v == 0:
                                wait(pe, a_sca, n, "shift")
                            wait(pe, exps, n if v >= 2 else n - 1, f"unit{(v - 2) % NU}")
                            out = ps[:, 3 + v % 2, :]
                            for e in range(2):
                                nc.tensor.matmul(out.rearrange("p (r n) -> p r n", r=REP),
                                                 keys[e][:, g, kt * P:(kt + 1) * P],
                                                 q[:, :, t * P:(t + 1) * P],
                                                 start=e == 0, stop=False, skip_group_check=True)
                            for r in range(REP):
                                last = nc.tensor.matmul(out[:, r * P:(r + 1) * P], pick[:, g, r, :],
                                                        shift_[:, par, t * P:(t + 1) * P], start=False,
                                                        stop=r == REP - 1, skip_group_check=True)
                            last.then_inc(scores.sem, 1)
                        if v == 0 and s > 0:
                            multiply_values(n - 1, 1 - par, len(PV) - 1)
                        for p in pv_at[v]:
                            if p < len(PV) - 1 or s == AU - 1:
                                multiply_values(n, par, p)
                        for step in A_AT.get(v, []):
                            phase_a(step, n + 2 if step == "x" else n + 1, 1 - par)
                        if v == WO_AT:
                            project(n)
            project(SEQS)

        @block.scalar
        def _(act):
            for s in (a_sca, exps, c_sca, norm_sca):
                s.start(act)
            act.wait_ge(ready, 2)

            def phase_a(step, n, par):
                if step == "x":
                    wait(act, a_pen, n, "xT")
                    nc.scalar.activation(xhi[:, :, :].rearrange("p m t -> p (m t)"), ps[:, 0, :], ACT.Copy)\
                        .then_inc(a_sca.sem, 1)
                elif step == "qkv":
                    wait(act, a_pen, n, "kv")
                    for g in range(KV):
                        last = nc.scalar.activation(kh_[slot(g), par, g, :], ps[slot(g), 0, 0:T], ACT.Copy)
                    last.then_inc(a_sca.sem, 1)
                    nc.scalar.activation(v1_[:, par, :, :, 0:D],
                                         ps[:, 0, T:T + 2 * KV * D].rearrange("p (t g d) -> p t g d", t=2, g=KV),
                                         ACT.Copy).then_inc(a_sca.sem, 1)
                    for b in range(2):
                        wait(act, a_pen, n, f"q{b}")
                        nc.scalar.activation(qh[:, 2 * b:2 * b + 2, :].rearrange("p r t -> p (r t)"),
                                             ps[:, 1 + b, :], ACT.Copy).then_inc(a_sca.sem, 1)
                elif step == "top":
                    wait(act, a_pen, n, "maxT")
                    nc.scalar.activation(shift_[:, par, :], ps[:, 0, 0:2 * P], ACT.Copy, scale=-1.0)\
                        .then_inc(a_sca.sem, 1)

            def split_hi(n, t):
                wait(act, div[t], n, "out")
                wait(act, c_pen, n - 1, "wo")
                nc.scalar.activation(ohi[:, t, :, :].rearrange("p r n -> p (r n)"), o[:, t, :], ACT.Copy)\
                    .then_inc(c_sca.sem, 1)

            def root(i):
                wait(act, norm_vec, i, "mv")
                nc.scalar.activation(std[:, :], mv[:, :, 1], ACT.Sqrt, bias=k.eps[:, 0:1])\
                    .then_inc(norm_sca.sem, 1)

            split_hi(0, 0)
            phase_a("x", 0, 0)
            for v in range(SLOTS):
                for step in A_AT.get(v, []):
                    phase_a(step, 1 if step == "x" else 0, 0)
            with act.Fori(0, SEQS // AU) as i:
                for s in range(AU):
                    n, par = i * AU + s, s % 2
                    for v in range(SLOTS):
                        if v < NU:
                            wait(act, scores, n, f"unit{v}")
                            wait(act, probs, n if v >= RING_E else n - 1, f"unit{(v - RING_E) % NU}")
                            nc.scalar.activation(ex[:, v % RING_E, :], ps[:, 3 + v % 2, :], ACT.Exp, scale=SCALE)\
                                .then_inc(exps.sem, 1)
                        for step in A_AT.get(v, []):
                            phase_a(step, n + 2 if step == "x" else n + 1, 1 - par)
                        if v == HI1_AT:
                            split_hi(n, 1)
                        if v == HI0_AT:
                            split_hi(n + 1, 0)
                        if s == AU - 1 and v == SQRT_AT:
                            root(i)
            split_hi(SEQS, 1)
            root(SEQS // AU)

        @block.vector
        def _(dve):
            for s in (a_vec, *div, c_vec, norm_vec):
                s.start(dve)
            for t in (kh_, kl_):
                last = nc.vector.memset(t, 0.0)
            last.then_inc(ready, 1)
            dve.wait_ge(ready, 2)
            nc.vector.memset(ps[:, 6:8, :], 1.0).then_inc(ready, 1)
            hold(dve, ready, 3, passed)

            def phase_a(step, n, par):
                if step == "x":
                    wait(dve, a_sca, n, "xhi")
                    nc.vector.tensor_tensor(xlo[:, :, :].rearrange("p m t -> p (m t)"), ps[:, 0, :],
                                            xhi[:, :, :].rearrange("p m t -> p (m t)"), ALU.subtract)\
                        .then_inc(a_vec.sem, 1)
                elif step == "qkv":
                    wait(dve, a_sca, n, "v")
                    for g in range(KV):
                        last = nc.vector.tensor_tensor(kl_[slot(g), par, g, :], ps[slot(g), 0, 0:T],
                                                       kh_[slot(g), par, g, :], ALU.subtract)
                    last.then_inc(a_vec.sem, 1)
                    for b in range(2):
                        wait(dve, a_sca, n, f"qhi{b}")
                        nc.vector.scalar_tensor_tensor(
                            out=q_[:, par, 2 * b:2 * b + 2, :].rearrange("p r t -> p (r t)"),
                            in0=qh[:, 2 * b:2 * b + 2, :].rearrange("p r t -> p (r t)"), scalar=negate,
                            in1=ps[:, 1 + b, :], op0=ALU.mult, op1=ALU.add).then_inc(a_vec.sem, 1)
                elif step != "top":
                    u = step
                    t, g, r0, heads = NAT[u]
                    wait(dve, a_pen, n, f"max{u}")
                    nc.vector.tensor_reduce(top[:, t, g, r0:r0 + heads],
                                            ps[:, 1 + u % 2, :].rearrange("p (r n) -> p r n", r=heads),
                                            AX_X, ALU.max).then_inc(a_vec.sem, 1)

            def divide(n, t, steps=None):
                for step in steps or div[t].names:
                    if step == "sum":
                        wait(dve, c_pol, n - 1, f"olo{t}")
                        hold(dve, pvs.sem, pvs.after(n - 1, f"pv{2 * t}"), passed)
                        ins = nc.vector.stream_shuffle(rec[:, t, :], ps[:, 6 + t, :], [D] * SLOT)
                    elif step == "out":
                        wait(dve, div[t], n, f"rec{REC - 1}")
                        ins = nc.vector.tensor_tensor(o[:, t, :], ps[:, 6 + t, :], rec[:, t, :], ALU.mult)
                    else:
                        part = REP * P // REC
                        cols = slice(int(step[3:]) * part, (int(step[3:]) + 1) * part)
                        if step == "rec0":
                            wait(dve, div[t], n, "sum")
                        ins = nc.vector.reciprocal(rec[:, t, cols], rec[:, t, cols])
                    ins.then_inc(div[t].sem, 1)

            def add_residual(n, s):
                wait(dve, c_pen, n, "wo")
                nc.vector.tensor_tensor(res[:, s, :], ps[:, 5, :], k.x_all[:, bass.ds(n * (2 * H), 2 * H)],
                                        ALU.add).then_inc(c_vec.sem, 1)
                wait(dve, c_vec, n, "res")
                for t in range(2):
                    last = nc.vector.bn_stats(st[:, 2 * s + t, :], res[:, s, t * H:(t + 1) * H])
                last.then_inc(c_vec.sem, 1)

            divide(0, 0)
            phase_a("x", 0, 0)
            for v in range(SLOTS):
                for step in A_AT.get(v, []):
                    phase_a(step, 1 if step == "x" else 0, 0)

            def variance(i, last_s, tiles):
                hold(dve, c_vec.sem, c_vec.after(i * AU + last_s, "stats"), passed)
                for t in range(tiles):
                    last = nc.vector.bn_aggr(mv[:, t, :], st[:, t, :])
                last.then_inc(norm_vec.sem, 1)

            def normalise(i, tiles):
                wait(dve, norm_sca, i, "std")
                nc.vector.reciprocal(rstd[:, :], std[:, :]).then_inc(norm_vec.sem, 1)
                wait(dve, norm_vec, i, "rstd")
                for t in range(tiles):
                    last = nc.vector.tensor_scalar(k.x_all[:, bass.ds(i * (2 * AU * H) + t * H, H)],
                                                   res[:, t // 2, (t % 2) * H:(t % 2 + 1) * H],
                                                   mv[:, t, 0:1], rstd[:, t:t + 1], ALU.subtract, ALU.mult)
                last.then_inc(norm_vec.sem, 1)

            with dve.Fori(0, SEQS // AU) as i:
                for s in range(AU):
                    n, par = i * AU + s, s % 2
                    for v in range(SLOTS):
                        if v in DIV1_AT:
                            divide(n, 1, DIV1_AT[v])
                        for step in A_AT.get(v, []):
                            phase_a(step, n + 2 if step == "x" else n + 1, 1 - par)
                        if v == RES_AT:
                            add_residual(n, s)
                        if v in DIV0_AT:
                            divide(n + 1, 0, DIV0_AT[v])
                        if s == AU - 1 and v == NORM_AT:
                            variance(i, AU - 1, 2 * AU)
                        if s == AU - 1 and v == OUT_AT:
                            normalise(i, 2 * AU)
            divide(SEQS, 1)
            add_residual(SEQS, 0)
            variance(SEQS // AU, 0, 2)
            normalise(SEQS // AU, 2)


def layer1_network_stage(nc, k, up, down):
    B, LAG, RING = FF_BLOCKS, 2, 4
    X_AT, HI_AT, END_AT, ROOT_AT, OUT_AT = 4, 5, 1, 2, 3
    with ExitStack() as ctx:
        def sb(name, shape, dt=F32):
            return ctx.enter_context(nc.sbuf_tensor("ff_" + name, shape, dt))

        def sem(name):
            return ctx.enter_context(nc.semaphore("ff_" + name))

        xc = sb("xc", [P, GROUP, H])
        xhi, xlo = (sb(n, [P, 2, KT, GTOK], F16) for n in ("xhi", "xlo"))
        sil, hid = (w[:, FF_BLOCKS * H:FF_BLOCKS * H + 4 * GTOK].bitcast(F32).rearrange("p (b n) -> p b n", b=2)
                    for w in (k.moe_hi, k.moe_lo))
        hhi, hlo = (sb(n, [P, RING, GTOK], F16) for n in ("hhi", "hlo"))
        res = sb("res", [P, GROUP, H])
        st = sb("st", [P, GROUP, 6])
        mv = sb("mv", [P, GROUP, 2])
        std = sb("std", [P, GROUP])
        rstd = sb("rstd", [P, GROUP])

        def blocks(name):
            return Steps(sem(name), [str(b) for b in range(B)])

        copied, turned = Steps(sem("x_copied"), ["x"]), Steps(sem("x_turned"), ["x"])
        x_hi, x_lo = Steps(sem("x_hi"), ["x"]), Steps(sem("x_lo"), ["x"])
        up_done, sil_done, hid_done = blocks("up_done"), blocks("sil_done"), blocks("hid_done")
        h_hi, h_lo, down_done = blocks("h_hi"), blocks("h_lo"), blocks("down_done")
        norm = Steps(sem("norm_steps"), ["res", "stats", "mv", "rstd", "out"])
        root = Steps(sem("root_steps"), ["std"])
        passed, stored = k.vector_waits, sem("stored")
        ps = k.ps
        block = ctx.enter_context(nc.Block())

        def wait(eng, steps, g, name):
            eng.wait_ge(steps.sem, steps.after(g, str(name)))

        def back(g, b, by):
            return (g, b - by) if b >= by else (g - 1, b - by + B)

        def groups(eng, body):
            body(0, 0, first=True)
            with eng.Fori(0, GROUPS // 2 - 1) as i:
                body(i * 2 + 1, 1)
                body(i * 2 + 2, 0)
            body(GROUPS - 1, 1)

        @block.sync
        def _(sp):
            with sp.Fori(0, GROUPS) as g:
                wait(sp, norm, g, "out")
                sp.dma_start(k.d_out[bass.ds(g * GROUP, GROUP)].rearrange("t p h -> p t h"),
                             k.x[:, bass.ds(g * (GROUP * H), GROUP * H)].rearrange("p (t h) -> p t h", h=H))\
                    .then_inc(stored, 16)
            sp.wait_ge(stored, 16 * GROUPS)

        @block.gpsimd
        def _(pool):
            copied.start(pool)
            with pool.Fori(0, GROUPS + 1) as g:
                wait(pool, turned, g - 1, "x")
                nc.gpsimd.tensor_copy(xc[:, :, :].rearrange("p t h -> p (t h)"),
                                      k.x[:, bass.ds(g * (GROUP * H), GROUP * H)]).then_inc(copied.sem, 1)

        @block.tensor
        def _(pe):
            for s in (turned, up_done, down_done):
                s.start(pe)

            def turn_x(g):
                wait(pe, copied, g, "x")
                wait(pe, x_lo, g - 1, "x")
                for m in range(KT):
                    for t in range(GROUP):
                        last = nc.tensor.transpose(ps[:, 4 + m, t * P:(t + 1) * P],
                                                   xc[:, t, m * P:(m + 1) * P], k.ident[:, :])
                last.then_inc(turned.sem, 1)

            def gate_up(g, b, par):
                if b == 0:
                    wait(pe, x_lo, g, "x")
                wait(pe, hid_done, *back(g, b, 2))
                for half in range(2):
                    at = half * 256 + (b % 2) * P
                    for m in range(KT):
                        last = split_matmul(nc, ps[:, 2 * (b % 2) + half, :],
                                            [w[:, m, b // 2, at:at + P] for w in up],
                                            [x[:, par, m, :] for x in (xhi, xlo)], m == 0, m == KT - 1)
                last.then_inc(up_done.sem, 1)

            def multiply_down(g, b):
                wait(pe, h_lo, g, b)
                if b == 0:
                    wait(pe, norm, g - 1, "res")
                for t in range(GROUP):
                    last = split_matmul(nc, ps[:, 6 + t // 2, (t % 2) * H:(t % 2 + 1) * H],
                                        [a[:, b % RING, t * P:(t + 1) * P] for a in (hhi, hlo)],
                                        [w[:, b, :] for w in down], b == 0 and t % 2 == 0, b == B - 1)
                last.then_inc(down_done.sem, 1)

            def body(g, par, first=False):
                for b in range(B):
                    gate_up(g, b, par)
                    if b == X_AT:
                        turn_x(g + 1)
                    if b >= LAG or not first:
                        multiply_down(*back(g, b, LAG))

            turn_x(0)
            groups(pe, body)
            for b in range(B - LAG, B):
                multiply_down(GROUPS - 1, b)

        @block.scalar
        def _(act):
            for s in (x_hi, sil_done, h_hi, root):
                s.start(act)

            def x_split(g, par):
                wait(act, turned, g, "x")
                if not (isinstance(g, int) and g == 0):
                    wait(act, up_done, g - 2, B - 1)
                nc.scalar.activation(xhi[:, par, :, :].rearrange("p m t -> p (m t)"),
                                     ps[:, 4:6, :].rearrange("p m t -> p (m t)"), ACT.Copy).then_inc(x_hi.sem, 1)

            def take_root(g):
                wait(act, norm, g, "mv")
                nc.scalar.activation(std[:, :], mv[:, :, 1], ACT.Sqrt, bias=k.eps[:, 0:1]).then_inc(root.sem, 1)

            def body(g, par, first=False):
                for b in range(B):
                    wait(act, up_done, g, b)
                    wait(act, hid_done, *back(g, b, 2))
                    nc.scalar.activation(sil[:, b % 2, :], ps[:, 2 * (b % 2), :], ACT.Silu)\
                        .then_inc(sil_done.sem, 1)
                    wait(act, hid_done, g, b)
                    wait(act, down_done, *back(g, b, RING))
                    nc.scalar.activation(hhi[:, b % RING, :], hid[:, b % 2, :], ACT.Copy).then_inc(h_hi.sem, 1)
                    if b == HI_AT:
                        x_split(g + 1, 1 - par)
                    if b == ROOT_AT and not first:
                        take_root(g - 1)

            x_split(0, 0)
            groups(act, body)
            take_root(GROUPS - 1)

        @block.vector
        def _(dve):
            for s in (x_lo, hid_done, h_lo, norm):
                s.start(dve)

            def x_split(g, par):
                wait(dve, x_hi, g, "x")
                nc.vector.tensor_tensor(xlo[:, par, :, :].rearrange("p m t -> p (m t)"),
                                        ps[:, 4:6, :].rearrange("p m t -> p (m t)"),
                                        xhi[:, par, :, :].rearrange("p m t -> p (m t)"), ALU.subtract)\
                    .then_inc(x_lo.sem, 1)

            def end_sum(g):
                wait(dve, down_done, g, B - 1)
                wait(dve, norm, g - 1, "out")
                for b in range(2):
                    last = nc.vector.tensor_tensor(
                        res[:, 2 * b:2 * b + 2, :].rearrange("p t h -> p (t h)"), ps[:, 6 + b, :],
                        k.x[:, bass.ds(g * (GROUP * H) + b * 2 * H, 2 * H)], ALU.add)
                last.then_inc(norm.sem, 1)
                wait(dve, norm, g, "res")
                for t in range(GROUP):
                    last = nc.vector.bn_stats(st[:, t, :], res[:, t, :])
                last.then_inc(norm.sem, 1)
                hold(dve, norm.sem, norm.after(g, "stats"), passed)
                for t in range(GROUP):
                    last = nc.vector.bn_aggr(mv[:, t, :], st[:, t, :])
                last.then_inc(norm.sem, 1)

            def end_normalise(g):
                wait(dve, root, g, "std")
                nc.vector.reciprocal(rstd[:, :], std[:, :]).then_inc(norm.sem, 1)
                wait(dve, norm, g, "rstd")
                for t in range(GROUP):
                    last = nc.vector.tensor_scalar(k.x[:, bass.ds(g * (GROUP * H) + t * H, H)], res[:, t, :],
                                                   mv[:, t, 0:1], rstd[:, t:t + 1], ALU.subtract, ALU.mult)
                last.then_inc(norm.sem, 1)

            def body(g, par, first=False):
                for b in range(B):
                    wait(dve, sil_done, g, b)
                    wait(dve, h_lo, *back(g, b, 2))
                    nc.vector.tensor_tensor(hid[:, b % 2, :], sil[:, b % 2, :], ps[:, 2 * (b % 2) + 1, :],
                                            ALU.mult).then_inc(hid_done.sem, 1)
                    wait(dve, h_hi, g, b)
                    nc.vector.tensor_tensor(hlo[:, b % RING, :], hid[:, b % 2, :], hhi[:, b % RING, :],
                                            ALU.subtract).then_inc(h_lo.sem, 1)
                    if b == HI_AT:
                        x_split(g + 1, 1 - par)
                    if b == END_AT and not first:
                        end_sum(g - 1)
                    if b == OUT_AT and not first:
                        end_normalise(g - 1)

            x_split(0, 0)
            groups(dve, body)
            end_sum(GROUPS - 1)
            end_normalise(GROUPS - 1)


class Shared:
    pass


def spare(whole):
    taken = [0]

    def there(*dims):
        size = 2 * int(np.prod(dims))
        part = whole[:, taken[0]:taken[0] + size].bitcast(F32)
        taken[0] += size
        names = " ".join("abcd"[:len(dims)])
        return part.rearrange(f"p ({names}) -> p {names}", **dict(zip("abcd", dims)))

    return there


def build(nc, x, l0, vecs, route, moe, l1, w2, ident, had, att, bias, slots, results, out):
    k = Shared()
    k.d_l0, k.d_vecs, k.d_moe, k.d_l1, k.d_w2, k.d_ident, k.d_had, k.d_att, k.d_bias = \
        l0, vecs, moe, l1, w2, ident, had, att, bias
    k.d_x, k.d_out, k.d_route = x, out, route
    k.d_slots, k.d_y = slots, results
    with ExitStack() as ctx:
        def sb(name, shape, dt=F32):
            return ctx.enter_context(nc.sbuf_tensor(name, shape, dt))

        k.ps = ctx.enter_context(nc.psum_tensor("ps", [P, 8, 512], F32))
        k.x_all = sb("x", [P, (TILES + 6) * H])
        k.x = k.x_all[:, 2 * H:]
        k.vecs = sb("vecs", [P, 14])
        k.decay = sb("decay", [P, KT])
        k.eps = sb("eps", [P, 1])
        k.ident = sb("ident", [P, P])
        k.l0_hi, k.l0_lo = sb("l0_hi", [P, C_L0], F16), sb("l0_lo", [P, C_L0], F16)
        k.moe_hi, k.moe_lo = sb("moe_hi", [P, C_MOE], F16), sb("moe_lo", [P, C_MOE], F16)
        k.vector_waits, k.pool_waits = (ctx.enter_context(nc.semaphore(n)) for n in ("vector_waits", "pool_waits"))
        load_stage(nc, k)
        time_mix_stage(nc, k)
        k.gate = sb("gate", [P, TILES])
        k.weight = sb("weight", [P, TILES, TOPK])
        k.slot = sb("slot", [P, TILES, TOPK], I32)
        k.expert = sb("expert", [1, CHAINS * P], I32)
        k.l1_hi, k.l1_lo = sb("l1_hi", [P, C_L1], F16), sb("l1_lo", [P, C_L1], F16)
        k.att_const = sb("att_const", [P, 1 + 6 * P])
        k.spare_hi, k.spare_lo = spare(k.l1_hi), spare(k.l1_lo)
        with ExitStack() as routing:
            k.order, k.share = (routing.enter_context(nc.sbuf_tensor(n, [P, TILES, E], F32))
                                for n in ("order", "share"))
            router_stage(nc, k)
            gate_up = [w[:, 0:C_GU].rearrange("p (m c n) -> p m c n", m=KT, c=SLICES) for w in (k.moe_hi, k.moe_lo)]
            down = [w[:, C_GU:].rearrange("p (b h) -> p b h", h=H) for w in (k.moe_hi, k.moe_lo)]
            feed_forward_stage(nc, k, "sh_", SH, I_MOE, SHARED_BLOCKS, [w[:, :, E:, :] for w in gate_up],
                               [w[:, E * EXPERT_BLOCKS:, :] for w in down], 2 * CHAINS, shared=True)
            expert_stage(nc, k, "even_", chain=0)
        expert_stage(nc, k, "odd_", chain=1, combine=0)
        k.w2_hi = k.moe_hi[:, 0:FF_BLOCKS * H].rearrange("p (c h) -> p c h", h=H)
        k.w2_lo = k.moe_lo[:, 0:FF_BLOCKS * H].rearrange("p (c h) -> p c h", h=H)
        free = FF_BLOCKS * H
        k.bias_flat = k.moe_hi[:, free:free + 4 * HEADS * P].bitcast(F32)
        expert_stage(nc, k, "last_", combine=1)
        attention_stage(nc, k)
        at = C_Q + C_K + C_V + C_O
        up = [w[:, at:at + C_FF].rearrange("p (m c n) -> p m c n", m=KT, c=I_FF // 256)
              for w in (k.l1_hi, k.l1_lo)]
        layer1_network_stage(nc, k, up, [k.w2_hi, k.w2_lo])


def rows(a):
    return a.reshape(-1, P, a.shape[-1]).transpose(1, 0, 2)


def cols(*parts):
    return np.ascontiguousarray(np.concatenate([p.reshape(P, -1) for p in parts], axis=1))


def kernel(**inputs):
    import concourse.bacc as bacc
    from concourse.bass_utils import run_bass_kernel_spmd

    a = {n: np.asarray(v) for n, v in inputs.items()}
    A, F, B, G = "L0_attn_", "L0_ffn_", "L1_attn_", "L1_ffn_"
    f32 = np.float32

    gates = np.concatenate([a[F + "w_gate"].transpose(1, 0, 2), a[F + "sh_gate"].reshape(H, SH, I_MOE)], 1)
    ups = np.concatenate([a[F + "w_up"].transpose(1, 0, 2), a[F + "sh_up"].reshape(H, SH, I_MOE)], 1)
    gate_up = np.concatenate([gates, ups], 2).reshape(H, -1)
    down = np.zeros((E, EXPERT_BLOCKS * P, H), f32)
    down[:, :I_MOE] = a[F + "w_down"]
    sh_down = np.zeros((SHARED_BLOCKS * P, H), f32)
    sh_down[:I_SH] = a[F + "sh_down"]
    down = np.concatenate([down.reshape(-1, H), sh_down], 0)

    wq = a[B + "Wq"].T.reshape(H, KV, REP, D).transpose(0, 2, 1, 3)
    wq = np.concatenate([wq, wq], 3).reshape(H, REP * P)
    wk = a[B + "Wk"].T.reshape(H, KV, D)
    wk = np.concatenate([wk, wk], 2).reshape(H, P)
    wo = np.zeros((REP, KV, SLOT, H), f32)
    wo[:, :, :D] = a[B + "Wo"].T.reshape(KV, REP, D, H).transpose(1, 0, 2, 3)
    chunks = I_FF // 256
    ff = np.concatenate([a[G + "W1"].T.reshape(H, chunks, 256), a[G + "W3"].T.reshape(H, chunks, 256)], 2)

    vec_names = ["ln_scale", "ln_bias", "mix_k", "mix_v", "mix_r", "time_first", "time_decay"]
    upper = np.triu(np.ones((P, P), f32), 1)
    steps = np.broadcast_to(P * np.arange(CTILES), (P, CTILES)).astype(f32)

    had = np.ones((1, 1), f32)
    while had.shape[0] < P:
        had = np.block([[had, had], [had, -had]])
    row, col = np.arange(P)[:, None], np.arange(P)[None, :]
    negate = np.where(np.arange(P)[:, None] % SLOT < D, 0.0, -1.0).astype(f32)
    mask = np.where(col > row, NEG, 0.0).astype(f32)
    pick = np.stack([np.broadcast_to((np.arange(P) % SLOT == r)[:, None], (P, P)) for r in range(REP)], 1)
    slopes = 2.0 ** (-8.0 / HEADS * np.arange(1, HEADS + 1))
    dist = np.stack([col - row, col - row + P], 0).astype(np.float64)
    bias = np.exp(-slopes[:, None, None, None] * np.sqrt(np.maximum(dist, 0))) * (dist >= 0)
    bias = bias.reshape(KV, REP, 2, P, P).transpose(3, 0, 2, 1, 4).astype(f32)

    arrays = {
        "x": a[A + "x"].reshape(TILES, P, H),
        "l0": cols(*[rows(a[A + n]) for n in ("Wk", "Wv", "Wr", "Wo")],
                   rows(np.concatenate([a[F + "router_w"].T, a[F + "sh_gate_w"]], 1))),
        "vecs": cols(*[a[A + n].reshape(KT, P).T for n in vec_names]),
        "route": cols(upper, steps, np.arange(P, dtype=f32)),
        "moe": cols(rows(gate_up), rows(down)),
        "l1": cols(rows(wq), rows(wk), rows(a[B + "Wv"].T), rows(wo.reshape(-1, H)), rows(ff.reshape(H, -1))),
        "w2": cols(rows(a[G + "W2"].T)),
        "ident": np.eye(P, dtype=f32),
        "had": cols(had * I_FF ** -0.5, had * -I_FF ** -0.5),
        "att": cols(negate, np.eye(P, dtype=f32), mask, pick.astype(f32)),
        "bias": cols(bias),
    }
    nc = bacc.Bacc("TRN2", target_bir_lowering=False, num_devices=1)
    args = {}
    feed = {}
    for name, v in arrays.items():
        v = np.ascontiguousarray(v)
        feed[f"in_{name}"] = v
        args[name] = nc.dram_tensor(f"in_{name}", v.shape, F32, kind="ExternalInput").ap()
    for name, tiles, width, dt in (("slots", SLOT_TILES + LOADS_AHEAD, 2 * H, F16), ("results", SLOT_TILES, H, F32)):
        args[name] = [nc.dram_tensor(f"{name}_{c}", (tiles * P, width), dt, kind="Internal").ap()
                      for c in range(CHAINS)]
    args["out"] = nc.dram_tensor("out_0", (TILES, P, H), F32, kind="ExternalOutput").ap()
    build(nc, **args)
    r = run_bass_kernel_spmd(nc, [feed], core_ids=[0])
    return r.results[0]["out_0"].reshape(SEQS, T, H)
```
